# Optimizing a Trainium2 kernel written in Bass

```python
import numpy as np
import jax
import jax.numpy as jnp

def _softmax(x, axis=-1):
    return jax.nn.softmax(x, axis=axis)

def _gelu(x):
    return jax.nn.gelu(x, approximate=True)

def _silu(x):
    return jax.nn.silu(x)

def _sigmoid(x):
    return jax.nn.sigmoid(x)

def _layernorm(x, axis=-1, eps=1e-05):
    m = jnp.mean(x, axis=axis, keepdims=True)
    v = jnp.var(x, axis=axis, keepdims=True)
    return (x - m) / jnp.sqrt(v + eps)

def _scatter_add(tgt, idx, src, axis=0):
    return tgt.at[idx].add(src)

def _segment_sum(src, seg, n):
    return jax.ops.segment_sum(src, seg, n)
kernel_name = 'mk_lm_tower_d2_tok_ids256_r4_d82789'

def setup_inputs(seed: int=0):
    np.random.seed(seed)
    _w = jnp.asarray

    def _rec_inputs():
        import jax
        import jax.numpy as jnp
        _rk = jax.random.key(seed)
        x = jax.random.randint(jax.random.fold_in(_rk, 1), (4, 2048), 0, 100001, jnp.int32)
        return x
    x = _rec_inputs()

    def _L0_tok_setup():
        import jax, jax.numpy as jnp
        import numpy as np
        NUM_ITEMS = 25000
        D = 64
        FOURIER_DIM = 64
        VISIT_DIM = 24
        RESIDUAL_SCALE = 0.1
        LN_EPS = 1e-05

        def _layer_norm(x, gamma, beta):
            mu = jnp.mean(x, axis=-1, keepdims=True)
            var = jnp.mean(jnp.square(x - mu), axis=-1, keepdims=True)
            return (x - mu) * jax.lax.rsqrt(var + LN_EPS) * gamma + beta
        key = jax.random.key(seed)
        ks = jax.random.split(key, 12)
        item_ids = jax.random.randint(ks[0], (128, 512), 0, NUM_ITEMS + 1)
        emb_table = 0.02 * jax.random.normal(ks[1], (NUM_ITEMS + 1, D), dtype=jnp.float32)
        emb_table = emb_table.at[0].set(0.0)
        geo_table = jax.random.normal(ks[2], (NUM_ITEMS + 1, FOURIER_DIM), dtype=jnp.float32)
        visit_table = jax.random.uniform(ks[3], (NUM_ITEMS + 1, VISIT_DIM), dtype=jnp.float32)

        def xavier(k, fan_in, fan_out):
            lim = np.sqrt(6.0 / (fan_in + fan_out))
            return jax.random.uniform(k, (fan_in, fan_out), jnp.float32, -lim, lim)
        w_item = xavier(ks[4], D, D)
        b_item = jnp.zeros((D,), jnp.float32)
        w_geo = xavier(ks[5], FOURIER_DIM, D)
        b_geo = jnp.zeros((D,), jnp.float32)
        w_visit = xavier(ks[6], VISIT_DIM, D)
        b_visit = jnp.zeros((D,), jnp.float32)
        w_fuse = xavier(ks[7], 3 * D, D)
        b_fuse = jnp.zeros((D,), jnp.float32)
        ln_gamma = jnp.ones((D,), jnp.float32)
        ln_beta = jnp.zeros((D,), jnp.float32)
        return dict(item_ids=item_ids, emb_table=emb_table, geo_table=geo_table, visit_table=visit_table, w_item=w_item, b_item=b_item, w_geo=w_geo, b_geo=b_geo, w_visit=w_visit, b_visit=b_visit, w_fuse=w_fuse, b_fuse=b_fuse, ln_gamma=ln_gamma, ln_beta=ln_beta)
    _L0_tok_all = _L0_tok_setup()
    _L0_tok_in = {k: v for k, v in _L0_tok_all.items() if k in ('emb_table', 'geo_table', 'visit_table', 'w_item', 'b_item', 'w_geo', 'b_geo', 'w_visit', 'b_visit', 'w_fuse', 'b_fuse', 'ln_gamma', 'ln_beta')}
    del _L0_tok_all

    def _L0_attn_setup():
        import jax, jax.numpy as jnp
        import numpy as np
        B, L, H, N, NLAYERS = (16, 512, 64, 64, 4)
        PRENORM = True

        def layer_norm(z, scale, bias, eps=1e-05):
            mu = jnp.mean(z, axis=-1, keepdims=True)
            var = jnp.var(z, axis=-1, keepdims=True)
            return (z - mu) * jax.lax.rsqrt(var + eps) * scale + bias

        def s4_block(u, log_dt, Alog, Aim, Cre, Cim, D, Wout, bout):
            Lq = u.shape[-1]
            dt = jnp.exp(log_dt)[:, None]
            A = -jnp.exp(Alog) + 1j * Aim
            C = Cre + 1j * Cim
            dtA = A * dt
            Cd = C * (jnp.exp(dtA) - 1.0) / A
            vand = jnp.exp(dtA[:, :, None] * jnp.arange(Lq))
            K = 2.0 * jnp.real(jnp.einsum('hn,hnl->hl', Cd, vand))
            n = 2 * Lq
            y = jnp.fft.irfft(jnp.fft.rfft(u, n=n) * jnp.fft.rfft(K, n=n), n=n)[..., :Lq]
            y = y + D[:, None] * u
            y = jax.nn.gelu(y)
            z = jnp.einsum('oh,bhl->bol', Wout, y) + bout[None, :, None]
            z1, z2 = jnp.split(z, 2, axis=1)
            return z1 * jax.nn.sigmoid(z2)
        key = jax.random.key(seed)
        ks = jax.random.split(key, 8)
        x = jax.random.normal(ks[0], (B, L, H), jnp.float32)
        log_dt = jnp.log(10.0 ** jax.random.uniform(ks[1], (NLAYERS, H), minval=-3.0, maxval=-1.0)).astype(jnp.float32)
        Alog = jnp.log(0.5 * jnp.ones((NLAYERS, H, N), jnp.float32))
        Aim = jnp.broadcast_to(np.pi * jnp.arange(N, dtype=jnp.float32), (NLAYERS, H, N)).copy()
        Cre = jax.random.normal(ks[2], (NLAYERS, H, N), jnp.float32) * 0.5 ** 0.5
        Cim = jax.random.normal(ks[3], (NLAYERS, H, N), jnp.float32) * 0.5 ** 0.5
        D = jax.random.normal(ks[4], (NLAYERS, H), jnp.float32)
        Wout = jax.random.normal(ks[5], (NLAYERS, 2 * H, H), jnp.float32) / jnp.sqrt(jnp.float32(H))
        bout = jnp.zeros((NLAYERS, 2 * H), jnp.float32)
        ln_scale = jnp.ones((NLAYERS, H), jnp.float32)
        ln_bias = jnp.zeros((NLAYERS, H), jnp.float32)
        return dict(x=x, log_dt=log_dt, Alog=Alog, Aim=Aim, Cre=Cre, Cim=Cim, D=D, Wout=Wout, bout=bout, ln_scale=ln_scale, ln_bias=ln_bias)
    _L0_attn_all = _L0_attn_setup()
    _L0_attn_in = {k: v for k, v in _L0_attn_all.items() if k in ('log_dt', 'Alog', 'Aim', 'Cre', 'Cim', 'D', 'Wout', 'bout', 'ln_scale', 'ln_bias')}
    del _L0_attn_all

    def _L0_ffn_setup():
        import jax, jax.numpy as jnp
        import numpy as np
        BN_EPS = 0.001

        def _bn(h, g, b, m, v):
            return g * (h - m) * jax.lax.rsqrt(v + BN_EPS) + b
        key = jax.random.key(seed)
        ks = jax.random.split(key, 8)
        B, F, Df = (64, 64, 64)
        E, H, D = (8, 64, 64)
        s1 = 1.0 / np.sqrt(Df)
        s2 = 1.0 / np.sqrt(H)
        return {'x': jax.random.normal(ks[0], (B, F, Df), jnp.float32), 'Wr': jax.random.normal(ks[1], (Df, E), jnp.float32) * s1, 'br': jnp.zeros((E,), jnp.float32), 'W1': jax.random.normal(ks[2], (E, Df, H), jnp.float32) * s1, 'b1': jnp.zeros((E, H), jnp.float32), 'g1': jnp.ones((E, H), jnp.float32), 'be1': jnp.zeros((E, H), jnp.float32), 'm1': jnp.zeros((E, H), jnp.float32), 'v1': jnp.ones((E, H), jnp.float32), 'W2': jax.random.normal(ks[3], (E, H, H), jnp.float32) * s2, 'b2': jnp.zeros((E, H), jnp.float32), 'g2': jnp.ones((E, H), jnp.float32), 'be2': jnp.zeros((E, H), jnp.float32), 'm2': jnp.zeros((E, H), jnp.float32), 'v2': jnp.ones((E, H), jnp.float32), 'Wo': jax.random.normal(ks[4], (E, H, D), jnp.float32) * s2, 'bo': jnp.zeros((E, D), jnp.float32)}
    _L0_ffn_all = _L0_ffn_setup()
    _L0_ffn_in = {k: v for k, v in _L0_ffn_all.items() if k in ('Wr', 'br', 'W1', 'b1', 'g1', 'be1', 'm1', 'v1', 'W2', 'b2', 'g2', 'be2', 'm2', 'v2', 'Wo', 'bo')}
    del _L0_ffn_all

    def _L1_attn_setup():
        import jax, jax.numpy as jnp
        import numpy as np
        B, S, F, H = (4, 256, 64, 8)
        SCALE = float(F) ** 0.5
        key = jax.random.key(seed)
        ks = jax.random.split(key, 5)
        return {'q_input': jax.random.normal(ks[0], (B, S, F), dtype=jnp.float32), 'Wq': jax.random.normal(ks[1], (F, F * H), dtype=jnp.float32) * 0.02, 'Wk': jax.random.normal(ks[2], (F, F * H), dtype=jnp.float32) * 0.02, 'Wv': jax.random.normal(ks[3], (F, F * H), dtype=jnp.float32) * 0.02, 'Wo': jax.random.normal(ks[4], (F * H, F), dtype=jnp.float32) * 0.02}
    _L1_attn_all = _L1_attn_setup()
    _L1_attn_in = {k: v for k, v in _L1_attn_all.items() if k in ('Wq', 'Wk', 'Wv', 'Wo')}
    del _L1_attn_all

    def _L1_ffn_setup():
        import jax, jax.numpy as jnp
        import numpy as np
        B, S, D = (8, 1024, 64)
        H = 4 * D
        CAPACITY = 0.5
        key = jax.random.key(seed)
        ks = jax.random.split(key, 6)
        x = jax.random.normal(ks[0], (B, S, D), dtype=jnp.float32)
        attention_mask = jnp.zeros((B, 1, 1, S), dtype=jnp.float32)
        wr = jax.random.normal(ks[1], (D, 1), dtype=jnp.float32) * 0.02
        br = jnp.zeros((1,), dtype=jnp.float32)
        w1 = jax.random.normal(ks[2], (D, H), dtype=jnp.float32) * 0.02
        b1 = jnp.zeros((H,), dtype=jnp.float32)
        w2 = jax.random.normal(ks[3], (H, D), dtype=jnp.float32) * 0.02
        b2 = jnp.zeros((D,), dtype=jnp.float32)
        return {'x': x, 'attention_mask': attention_mask, 'wr': wr, 'br': br, 'w1': w1, 'b1': b1, 'w2': w2, 'b2': b2}
    _L1_ffn_all = _L1_ffn_setup()
    _L1_ffn_in = {k: v for k, v in _L1_ffn_all.items() if k in ('attention_mask', 'wr', 'br', 'w1', 'b1', 'w2', 'b2')}
    del _L1_ffn_all
    return {'x': x, 'L0_tok_emb_table': _L0_tok_in['emb_table'], 'L0_tok_geo_table': _L0_tok_in['geo_table'], 'L0_tok_visit_table': _L0_tok_in['visit_table'], 'L0_tok_w_item': _L0_tok_in['w_item'], 'L0_tok_b_item': _L0_tok_in['b_item'], 'L0_tok_w_geo': _L0_tok_in['w_geo'], 'L0_tok_b_geo': _L0_tok_in['b_geo'], 'L0_tok_w_visit': _L0_tok_in['w_visit'], 'L0_tok_b_visit': _L0_tok_in['b_visit'], 'L0_tok_w_fuse': _L0_tok_in['w_fuse'], 'L0_tok_b_fuse': _L0_tok_in['b_fuse'], 'L0_tok_ln_gamma': _L0_tok_in['ln_gamma'], 'L0_tok_ln_beta': _L0_tok_in['ln_beta'], 'L0_attn_log_dt': _L0_attn_in['log_dt'], 'L0_attn_Alog': _L0_attn_in['Alog'], 'L0_attn_Aim': _L0_attn_in['Aim'], 'L0_attn_Cre': _L0_attn_in['Cre'], 'L0_attn_Cim': _L0_attn_in['Cim'], 'L0_attn_D': _L0_attn_in['D'], 'L0_attn_Wout': _L0_attn_in['Wout'], 'L0_attn_bout': _L0_attn_in['bout'], 'L0_attn_ln_scale': _L0_attn_in['ln_scale'], 'L0_attn_ln_bias': _L0_attn_in['ln_bias'], 'L0_ffn_Wr': _L0_ffn_in['Wr'], 'L0_ffn_br': _L0_ffn_in['br'], 'L0_ffn_W1': _L0_ffn_in['W1'], 'L0_ffn_b1': _L0_ffn_in['b1'], 'L0_ffn_g1': _L0_ffn_in['g1'], 'L0_ffn_be1': _L0_ffn_in['be1'], 'L0_ffn_m1': _L0_ffn_in['m1'], 'L0_ffn_v1': _L0_ffn_in['v1'], 'L0_ffn_W2': _L0_ffn_in['W2'], 'L0_ffn_b2': _L0_ffn_in['b2'], 'L0_ffn_g2': _L0_ffn_in['g2'], 'L0_ffn_be2': _L0_ffn_in['be2'], 'L0_ffn_m2': _L0_ffn_in['m2'], 'L0_ffn_v2': _L0_ffn_in['v2'], 'L0_ffn_Wo': _L0_ffn_in['Wo'], 'L0_ffn_bo': _L0_ffn_in['bo'], 'L1_attn_Wq': _L1_attn_in['Wq'], 'L1_attn_Wk': _L1_attn_in['Wk'], 'L1_attn_Wv': _L1_attn_in['Wv'], 'L1_attn_Wo': _L1_attn_in['Wo'], 'L1_ffn_attention_mask': _L1_ffn_in['attention_mask'], 'L1_ffn_wr': _L1_ffn_in['wr'], 'L1_ffn_br': _L1_ffn_in['br'], 'L1_ffn_w1': _L1_ffn_in['w1'], 'L1_ffn_b1': _L1_ffn_in['b1'], 'L1_ffn_w2': _L1_ffn_in['w2'], 'L1_ffn_b2': _L1_ffn_in['b2']}

def reference(x, L0_tok_emb_table, L0_tok_geo_table, L0_tok_visit_table, L0_tok_w_item, L0_tok_b_item, L0_tok_w_geo, L0_tok_b_geo, L0_tok_w_visit, L0_tok_b_visit, L0_tok_w_fuse, L0_tok_b_fuse, L0_tok_ln_gamma, L0_tok_ln_beta, L0_attn_log_dt, L0_attn_Alog, L0_attn_Aim, L0_attn_Cre, L0_attn_Cim, L0_attn_D, L0_attn_Wout, L0_attn_bout, L0_attn_ln_scale, L0_attn_ln_bias, L0_ffn_Wr, L0_ffn_br, L0_ffn_W1, L0_ffn_b1, L0_ffn_g1, L0_ffn_be1, L0_ffn_m1, L0_ffn_v1, L0_ffn_W2, L0_ffn_b2, L0_ffn_g2, L0_ffn_be2, L0_ffn_m2, L0_ffn_v2, L0_ffn_Wo, L0_ffn_bo, L1_attn_Wq, L1_attn_Wk, L1_attn_Wv, L1_attn_Wo, L1_ffn_attention_mask, L1_ffn_wr, L1_ffn_br, L1_ffn_w1, L1_ffn_b1, L1_ffn_w2, L1_ffn_b2):
    import jax
    import jax.numpy as jnp

    def _L0_tok_ref(item_ids, emb_table, geo_table, visit_table, w_item, b_item, w_geo, b_geo, w_visit, b_visit, w_fuse, b_fuse, ln_gamma, ln_beta):
        import jax, jax.numpy as jnp
        import numpy as np
        NUM_ITEMS = 25000
        D = 64
        FOURIER_DIM = 64
        VISIT_DIM = 24
        RESIDUAL_SCALE = 0.1
        LN_EPS = 1e-05

        def _layer_norm(x, gamma, beta):
            mu = jnp.mean(x, axis=-1, keepdims=True)
            var = jnp.mean(jnp.square(x - mu), axis=-1, keepdims=True)
            return (x - mu) * jax.lax.rsqrt(var + LN_EPS) * gamma + beta
        gelu = lambda x: jax.nn.gelu(x, approximate=False)
        safe_ids = jnp.clip(item_ids, 0, emb_table.shape[0] - 1)
        item_emb = emb_table[safe_ids]
        fourier_feat = geo_table[safe_ids]
        visit_feat = visit_table[safe_ids]
        item_h = gelu(item_emb @ w_item + b_item)
        geo_h = gelu(fourier_feat @ w_geo + b_geo)
        visit_h = gelu(visit_feat @ w_visit + b_visit)
        cat = jnp.concatenate([item_h, geo_h, visit_h], axis=-1)
        fused = _layer_norm(gelu(cat @ w_fuse + b_fuse), ln_gamma, ln_beta)
        valid_mask = (item_ids != 0)[..., None].astype(fused.dtype)
        fused = fused * valid_mask
        return item_emb + RESIDUAL_SCALE * fused

    def _L0_attn_ref(x, log_dt, Alog, Aim, Cre, Cim, D, Wout, bout, ln_scale, ln_bias):
        import jax, jax.numpy as jnp
        import numpy as np
        B, L, H, N, NLAYERS = (16, 512, 64, 64, 4)
        PRENORM = True

        def layer_norm(z, scale, bias, eps=1e-05):
            mu = jnp.mean(z, axis=-1, keepdims=True)
            var = jnp.var(z, axis=-1, keepdims=True)
            return (z - mu) * jax.lax.rsqrt(var + eps) * scale + bias

        def s4_block(u, log_dt, Alog, Aim, Cre, Cim, D, Wout, bout):
            Lq = u.shape[-1]
            dt = jnp.exp(log_dt)[:, None]
            A = -jnp.exp(Alog) + 1j * Aim
            C = Cre + 1j * Cim
            dtA = A * dt
            Cd = C * (jnp.exp(dtA) - 1.0) / A
            vand = jnp.exp(dtA[:, :, None] * jnp.arange(Lq))
            K = 2.0 * jnp.real(jnp.einsum('hn,hnl->hl', Cd, vand))
            n = 2 * Lq
            y = jnp.fft.irfft(jnp.fft.rfft(u, n=n) * jnp.fft.rfft(K, n=n), n=n)[..., :Lq]
            y = y + D[:, None] * u
            y = jax.nn.gelu(y)
            z = jnp.einsum('oh,bhl->bol', Wout, y) + bout[None, :, None]
            z1, z2 = jnp.split(z, 2, axis=1)
            return z1 * jax.nn.sigmoid(z2)
        h = jnp.swapaxes(x, -1, -2)
        for i in range(NLAYERS):
            z = h
            if PRENORM:
                z = jnp.swapaxes(layer_norm(jnp.swapaxes(z, -1, -2), ln_scale[i], ln_bias[i]), -1, -2)
            z = s4_block(z, log_dt[i], Alog[i], Aim[i], Cre[i], Cim[i], D[i], Wout[i], bout[i])
            h = z + h
            if not PRENORM:
                h = jnp.swapaxes(layer_norm(jnp.swapaxes(h, -1, -2), ln_scale[i], ln_bias[i]), -1, -2)
        return jnp.swapaxes(h, -1, -2)

    def _L0_ffn_ref(x, Wr, br, W1, b1, g1, be1, m1, v1, W2, b2, g2, be2, m2, v2, Wo, bo):
        import jax, jax.numpy as jnp
        import numpy as np
        BN_EPS = 0.001

        def _bn(h, g, b, m, v):
            return g * (h - m) * jax.lax.rsqrt(v + BN_EPS) + b
        feat = jnp.mean(x, axis=0)
        w = jax.nn.softmax(feat @ Wr + br, axis=-1)
        h = jnp.einsum('bfd,edh->bfeh', x, W1) + b1
        h = jax.nn.relu(_bn(h, g1, be1, m1, v1))
        h = jnp.einsum('bfeh,ehk->bfek', h, W2) + b2
        h = jax.nn.relu(_bn(h, g2, be2, m2, v2))
        y = jnp.einsum('bfeh,ehd->bfed', h, Wo) + bo
        return jnp.einsum('bfed,fe->bfd', y, w)

    def _L1_attn_ref(q_input, Wq, Wk, Wv, Wo):
        import jax, jax.numpy as jnp
        import numpy as np
        B, S, F, H = (4, 256, 64, 8)
        SCALE = float(F) ** 0.5
        b, s, f = q_input.shape
        h = Wq.shape[1] // f
        q = (q_input.reshape(b * s, f) @ Wq).reshape(b, s, f, h)
        k = (q_input.reshape(b * s, f) @ Wk).reshape(b, s, f, h)
        v = (q_input.reshape(b * s, f) @ Wv).reshape(b, s, f, h)
        qkt = jnp.einsum('bifh,bjfh->bijh', q, k)
        attn = jax.nn.sigmoid(qkt * SCALE)
        wv = jnp.einsum('bijh,bjfh->bifh', attn, v)
        wv = wv.reshape(b * s, f * h)
        out = jax.nn.relu(wv @ Wo)
        return out.reshape(b, s, f)

    def _L1_ffn_ref(x, attention_mask, wr, br, w1, b1, w2, b2):
        import jax, jax.numpy as jnp
        import numpy as np
        B, S, D = (8, 1024, 64)
        H = 4 * D
        CAPACITY = 0.5
        b, s, d = x.shape
        weights = (jnp.einsum('bsd,do->bso', x, wr) + br)[..., 0]
        k = max(1, int(CAPACITY * s))
        kk = k - 1 if k > 1 else 1
        _, idx = jax.lax.top_k(weights, k)
        sel_idx = idx[:, :kk]
        sel = jnp.take_along_axis(x, sel_idx[:, :, None], axis=1)
        h = jax.nn.gelu(jnp.einsum('bkd,dh->bkh', sel, w1) + b1)
        y = jnp.einsum('bkh,hd->bkd', h, w2) + b2
        w_sel = jnp.take_along_axis(weights, sel_idx, axis=1)
        y = y * w_sel[..., None]
        batch_idx = jnp.arange(b)[:, None]
        processed = jnp.zeros_like(x).at[batch_idx, sel_idx].set(y)
        return processed + x
    h = _L0_tok_ref(x, L0_tok_emb_table, L0_tok_geo_table, L0_tok_visit_table, L0_tok_w_item, L0_tok_b_item, L0_tok_w_geo, L0_tok_b_geo, L0_tok_w_visit, L0_tok_b_visit, L0_tok_w_fuse, L0_tok_b_fuse, L0_tok_ln_gamma, L0_tok_ln_beta)
    h = h + _L0_attn_ref(_layernorm(h, axis=-1), L0_attn_log_dt, L0_attn_Alog, L0_attn_Aim, L0_attn_Cre, L0_attn_Cim, L0_attn_D, L0_attn_Wout, L0_attn_bout, L0_attn_ln_scale, L0_attn_ln_bias)
    h = h + _L0_ffn_ref(_layernorm(h, axis=-1), L0_ffn_Wr, L0_ffn_br, L0_ffn_W1, L0_ffn_b1, L0_ffn_g1, L0_ffn_be1, L0_ffn_m1, L0_ffn_v1, L0_ffn_W2, L0_ffn_b2, L0_ffn_g2, L0_ffn_be2, L0_ffn_m2, L0_ffn_v2, L0_ffn_Wo, L0_ffn_bo)
    h = h + _L1_attn_ref(_layernorm(h, axis=-1), L1_attn_Wq, L1_attn_Wk, L1_attn_Wv, L1_attn_Wo)
    h = h + _L1_ffn_ref(_layernorm(h, axis=-1), L1_ffn_attention_mask, L1_ffn_wr, L1_ffn_br, L1_ffn_w1, L1_ffn_b1, L1_ffn_w2, L1_ffn_b2)
    return h

_drawn_inputs = setup_inputs


def setup_inputs(seed=0):
    import zlib

    import numpy as np

    out = dict(_drawn_inputs(seed))
    spreads = {'L0_tok_b_item': (0.0, 0.1),
     'L0_tok_b_geo': (0.0, 0.1),
     'L0_tok_b_visit': (0.0, 0.1),
     'L0_tok_b_fuse': (0.0, 0.1),
     'L0_tok_ln_gamma': (1.0, 0.2),
     'L0_tok_ln_beta': (0.0, 0.1),
     'L0_attn_Alog': (-0.6931471824645996, 0.2),
     'L0_attn_bout': (0.0, 0.1),
     'L0_attn_ln_scale': (1.0, 0.2),
     'L0_attn_ln_bias': (0.0, 0.1),
     'L0_ffn_br': (0.0, 0.564),
     'L0_ffn_b1': (0.0, 0.693),
     'L0_ffn_g1': (1.0, 0.6),
     'L0_ffn_be1': (0.0, 0.47),
     'L0_ffn_m1': (0.0, 0.665),
     'L0_ffn_v1': (1.0, 0.6),
     'L0_ffn_b2': (0.0, 0.577),
     'L0_ffn_g2': (1.0, 0.6),
     'L0_ffn_be2': (0.0, 0.489),
     'L0_ffn_m2': (0.0, 0.472),
     'L0_ffn_v2': (1.0, 0.6),
     'L0_ffn_bo': (0.0, 0.281),
     'L1_ffn_b1': (0.0, 0.8),
     'L1_ffn_b2': (0.0, 0.8)}
    factors = {'L1_ffn_wr': 8.0, 'L1_ffn_w1': 8.0, 'L1_ffn_w2': 8.0}
    for name, (base, spread) in spreads.items():
        noise = np.random.default_rng([zlib.crc32(name.encode()), seed]).standard_normal(out[name].shape)
        drawn = base * np.exp(spread * noise) if base else spread * noise
        out[name] = jnp.asarray(drawn.astype(out[name].dtype))
    for name, factor in factors.items():
        out[name] = (out[name] * factor).astype(out[name].dtype)
    return out
```

```python
from contextlib import ExitStack

import concourse.bass as bass
from concourse import mybir

F32 = mybir.dt.float32
F16 = mybir.dt.float16
I32 = mybir.dt.int32
ACT = mybir.ActivationFunctionType
ALU = mybir.AluOpType
AX = mybir.AxisListType

P = 128
BATCH, SEQ, D = 4, 2048, 64
CHUNKS = SEQ // P
TILES = BATCH * CHUNKS
VISIT = 24
ROW = D + D + VISIT
LAST_ID = 25000
LN_EPS = 1e-5


class Memory:

    def __init__(self, nc, stack, name):
        self.nc, self.stack, self.name = nc, stack, name

    def sb(self, name, shape, dt=F32):
        return self.stack.enter_context(self.nc.sbuf_tensor(f"{self.name}_{name}", shape, dt))

    def ps(self, name, shape, dt=F32):
        return self.stack.enter_context(self.nc.psum_tensor(f"{self.name}_{name}", shape, dt))

    def sem(self, name):
        return self.stack.enter_context(self.nc.semaphore(f"{self.name}_{name}"))


def over_last(ap, n):
    return ap.unsqueeze(len(ap.shape)).broadcast_to(list(ap.shape) + [n])


def layer_norm(nc, e, out, x, centred, square, stat, eps, scaled=None):
    n = x.shape[-1]
    nc.vector.tensor_reduce(out=stat[:, 0], in_=x, axis=AX.X, op=ALU.add)
    e.drain()
    nc.vector.tensor_scalar(stat[:, 0], stat[:, 0], 1.0 / n, None, ALU.mult)
    e.drain()
    nc.vector.tensor_tensor(centred, x, over_last(stat[:, 0], n), ALU.subtract)
    e.drain()
    nc.vector.tensor_tensor(square, centred, centred, ALU.mult)
    e.drain()
    nc.vector.tensor_reduce(out=stat[:, 1], in_=square, axis=AX.X, op=ALU.add)
    e.drain()
    nc.vector.tensor_scalar(stat[:, 1], stat[:, 1], 1.0 / n, eps, ALU.mult, ALU.add)
    scaled()
    nc.vector.reciprocal(stat[:, 0], stat[:, 2])
    e.drain()
    nc.vector.tensor_tensor(out, centred, over_last(stat[:, 0], n), ALU.mult)


def constants(nc, m):
    ident = m.sb("ident", [P, P])
    flip = m.sb("flip", [P, P])
    made = m.sem("ident_made")
    with nc.Block() as block:

        @block.gpsimd
        def _(pool):
            nc.gpsimd.memset(ident[:, :], 0.0).then_inc(made, 1)
            pool.wait_ge(made, 1)
            nc.gpsimd.affine_select(out=ident[:, :], in_=ident[:, :], compare_op=ALU.not_equal, fill=1.0,
                                    base=0, pattern=[[-1, P]], channel_multiplier=1).then_inc(made, 1)
            pool.wait_ge(made, 2)
            nc.gpsimd.memset(flip[:, :], 0.0).then_inc(made, 1)
            pool.wait_ge(made, 3)
            nc.gpsimd.affine_select(out=flip[:, :], in_=flip[:, :], compare_op=ALU.not_equal, fill=1.0,
                                    base=1 - P, pattern=[[1, P]], channel_multiplier=1).then_inc(made, 1)
            pool.wait_ge(made, 4)
    return ident, flip


def embed_tokens(nc, m, A, resid, ident, flip):
    GROUP = 4
    RING = 4
    NG = TILES // GROUP
    GT = GROUP * P

    ids = m.sb("ids", [TILES, P], I32)
    idf = m.sb("idf", [TILES, 2, P])
    index = m.sb("index", [P, TILES], I32)
    keep = m.sb("keep", [P, TILES])
    rows = m.sb("rows", [P, RING * GROUP, ROW])
    w_ig = m.sb("w_ig", [P, P])
    w_v = m.sb("w_v", [VISIT, D])
    w_f1 = m.sb("w_f1", [P, D])
    w_f2 = m.sb("w_f2", [D + 1, D])
    b_ig = m.sb("b_ig", [P, 1])
    b_v = m.sb("b_v", [D, 1])
    gamma = m.sb("gamma", [P, D])
    beta = m.sb("beta", [P, D])
    featT = m.sb("featT", [P, 2, GT])
    visitT = m.sb("visitT", [VISIT, 2, GT])
    hidT = m.sb("hidT", [P, 2, GT])
    hidvT = m.sb("hidvT", [D + 1, 2, GT])
    fused = m.sb("fused", [P, TILES, D])
    centred = m.sb("centred", [P, TILES, D])
    square = m.sb("square", [P, TILES, D])
    stat = m.sb("stat", [P, 3, TILES])
    ps_ids = m.ps("ps_ids", [P, 2, TILES])
    ps_feat = m.ps("ps_feat", [P, GT])
    ps_visit = m.ps("ps_visit", [VISIT, GT])
    ps_h = [m.ps(f"ps_h{i}", [P, GT]) for i in range(1)]
    ps_hv = [m.ps(f"ps_hv{i}", [D, GT]) for i in range(1)]
    ps_f = [m.ps(f"ps_f{i}", [P, GROUP, D]) for i in range(2)]

    zeroed, loaded, ids_in, clipped, ids_tr, index_ok = map(m.sem, ("zeroed", "loaded", "ids_in", "clipped", "ids_tr", "index_ok"))
    gathered = [m.sem(f"gathered{r}") for r in range(RING)]
    rows_used, feat_tr, feat_sb, proj, hid_ok, fuse_mm, fuse_ok, emb_ok, root_in, root_out = map(m.sem, (
        "rows_used", "feat_tr", "feat_sb", "proj", "hid_ok", "fuse_mm", "fuse_ok", "emb_ok", "root_in", "root_out"))
    N_LOADS = 11

    with nc.Block() as block:

        @block.sync
        def _(sp):
            sp.dma_start(ids[:, :], A["x"].rearrange("b (c p) -> (b c) p", p=P)).then_inc(ids_in, 16)
            sp.wait_ge(zeroed, 1)
            for dst, src in ((w_ig[0:D, 0:D], A["L0_tok_w_item"]), (w_ig[D:P, D:P], A["L0_tok_w_geo"]),
                             (w_v[:, :], A["L0_tok_w_visit"]),
                             (w_f1[:, :], A["L0_tok_w_fuse"][0:P, :]), (w_f2[0:D, :], A["L0_tok_w_fuse"][P:P + D, :]),
                             (w_f2[D:D + 1, :], A["L0_tok_b_fuse"].unsqueeze(0)),
                             (b_ig[0:D, :], A["L0_tok_b_item"].unsqueeze(1)), (b_ig[D:P, :], A["L0_tok_b_geo"].unsqueeze(1)),
                             (b_v[:, :], A["L0_tok_b_visit"].unsqueeze(1)),
                             (gamma[:, :], A["L0_tok_ln_gamma"].partition_broadcast(P)),
                             (beta[:, :], A["L0_tok_ln_beta"].partition_broadcast(P))):
                sp.dma_start(dst, src).then_inc(loaded, 16)

        @block.gpsimd
        def _(pool):
            nc.gpsimd.memset(w_ig[:, :], 0.0).then_inc(zeroed, 1)
            pool.wait_ge(zeroed, 1)
            nc.gpsimd.memset(hidvT[D:D + 1, :, :], 1.0).then_inc(zeroed, 1)
            pool.wait_ge(zeroed, 2)
            pool.wait_ge(index_ok, 1)
            for t in range(TILES):
                g, r = t // GROUP, t // GROUP % RING
                if t % GROUP == 0 and g >= RING:
                    pool.wait_ge(rows_used, 2 * (g - RING + 1))
                nc.gpsimd.indirect_dma_start(
                    out=rows[:, t % (RING * GROUP), :], out_offset=None, in_=A["rows"],
                    in_offset=bass.IndirectOffsetOnAxis(ap=index[:, t:t + 1], axis=0)).then_inc(gathered[r], 16)

        @block.tensor
        def _(pe):
            pe.wait_ge(clipped, 1)
            nc.tensor.transpose(ps_ids[:, 0, :], idf[:, 0, :], ident[0:TILES, 0:TILES])
            nc.tensor.transpose(ps_ids[:, 1, :], idf[:, 1, :], ident[0:TILES, 0:TILES]).then_inc(ids_tr, 1)
            pe.wait_ge(loaded, 16 * N_LOADS)
            pe.wait_ge(zeroed, 2)
            with pe.Fori(0, NG // RING) as it:
                for r in range(RING):
                    g = it * RING + r
                    pe.wait_ge(gathered[r], it * 16 * GROUP + 16 * GROUP)
                    for k in range(GROUP):
                        row = rows[:, r * GROUP + k, :]
                        nc.tensor.transpose(ps_feat[:, k * P:(k + 1) * P], row[:, 0:P], ident[:, :])
                    for k in range(GROUP):
                        row = rows[:, r * GROUP + k, :]
                        last = nc.tensor.transpose(ps_visit[:, k * P:(k + 1) * P], row[:, P:ROW], ident[:, :])
                    last.then_inc(feat_tr, 1)
                    pe.wait_ge(feat_sb, 2 * g + 2)
                    nc.tensor.matmul(ps_h[0][:, :], w_ig[:, :], featT[:, r % 2, :], start=True, stop=True)
                    nc.tensor.matmul(ps_hv[0][:, :], w_v[:, :], visitT[:, r % 2, :], start=True, stop=True).then_inc(proj, 1)
                    pe.wait_ge(hid_ok, g + 1)
                    for k in range(GROUP):
                        tok = slice(k * P, (k + 1) * P)
                        nc.tensor.matmul(ps_f[r % 2][:, k, :], hidT[:, r % 2, tok], w_f1[:, :], start=True, stop=False)
                        last = nc.tensor.matmul(ps_f[r % 2][:, k, :], hidvT[:, r % 2, tok], w_f2[:, :], start=False, stop=True)
                    last.then_inc(fuse_mm, 1)

        @block.scalar
        def _(act):
            act.wait_ge(loaded, 16 * N_LOADS)
            with act.Fori(0, NG // RING) as it:
                for r in range(RING):
                    g = it * RING + r
                    act.wait_ge(feat_tr, g + 1)
                    nc.scalar.activation(visitT[:, r % 2, :], ps_visit[:, :], ACT.Copy).then_inc(feat_sb, 1)
                    act.wait_ge(proj, g + 1)
                    nc.scalar.activation(hidT[:, r % 2, :], ps_h[0][:, :], ACT.Gelu, bias=b_ig[:, :])
                    nc.scalar.activation(hidvT[0:D, r % 2, :], ps_hv[0][:, :], ACT.Gelu, bias=b_v[:, :]).then_inc(hid_ok, 1)
                    act.wait_ge(fuse_mm, g + 1)
                    nc.scalar.activation(fused[:, bass.ts(g, GROUP), :], ps_f[r % 2][:, :, :], ACT.Gelu).then_inc(fuse_ok, 1)
            act.wait_ge(root_in, 1)
            nc.scalar.activation(stat[:, 2], stat[:, 1], ACT.Sqrt).then_inc(root_out, 1)

        @block.vector
        def _(dve):
            dve.wait_ge(ids_in, 16)
            nc.vector.tensor_scalar(idf[:, 0, :], ids[:, ::-1], 0.0, float(LAST_ID), ALU.max, ALU.min)
            nc.vector.tensor_scalar(idf[:, 1, :], ids[:, ::-1], 0.0, None, ALU.not_equal)
            dve.drain()
            dve.nop().then_inc(clipped, 1)
            dve.wait_ge(ids_tr, 1)
            nc.vector.tensor_copy(index[:, :], ps_ids[:, 0, :]).then_inc(index_ok, 1)
            nc.vector.tensor_copy(keep[:, :], ps_ids[:, 1, :])
            with dve.Fori(0, NG // RING) as it:
                for r in range(RING):
                    g = it * RING + r
                    dve.wait_ge(feat_tr, g + 1)
                    nc.vector.tensor_copy(resid[:, bass.ts(g, GROUP), :], rows[:, r * GROUP:(r + 1) * GROUP, 0:D]).then_inc(rows_used, 1)
                    nc.vector.tensor_copy(featT[:, r % 2, :], ps_feat[:, :]).then_inc(feat_sb, 1)
                    dve.nop().then_inc(rows_used, 1)
            dve.wait_ge(fuse_ok, NG)

            def root():
                dve.drain()
                dve.nop().then_inc(root_in, 1)
                dve.wait_ge(root_out, 1)

            layer_norm(nc, dve, fused[:, :, :], fused[:, :, :], centred[:, :, :], square[:, :, :], stat, LN_EPS, root)
            dve.drain()
            nc.vector.tensor_tensor(fused[:, :, :], fused[:, :, :], gamma[:, :].unsqueeze(1).broadcast_to([P, TILES, D]), ALU.mult)
            dve.drain()
            nc.vector.tensor_tensor(fused[:, :, :], fused[:, :, :], beta[:, :].unsqueeze(1).broadcast_to([P, TILES, D]), ALU.add)
            dve.drain()
            nc.vector.tensor_tensor(fused[:, :, :], fused[:, :, :], over_last(keep[:, :], D), ALU.mult)
            dve.drain()
            nc.vector.scalar_tensor_tensor(resid[:, :, :], fused[:, :, :], 0.1, resid[:, :, :], ALU.mult, ALU.add)


def state_space_layers(nc, m, A, resid, ident, flip):
    LAYERS = 4
    PAIRS = D // 2
    HALF = PAIRS // 2
    GP = 4
    GROUPS = PAIRS // GP
    HCOLS = HALF * P
    MAGIC = 1.5 * 2 ** 23
    TURN = 6.2831845
    QUARTER = TURN / 4

    hs = m.sb("hs", [P, TILES, D])
    u = m.sb("u", [P, D, TILES])
    work = m.sb("work", [P, 2, HCOLS])
    y = work[:, :, :].rearrange("p a b -> p (a b)").rearrange("p (t h) -> p t h", h=D)
    decay_b = m.sb("decay_b", [P, HCOLS])
    angle_c = m.sb("angle_c", [P, 2, HCOLS])
    decay_c = m.sb("decay_c", [P, HCOLS])
    rowp = m.sb("rowp", [P, 2, HCOLS])
    mat_b = m.sb("mat_b", [P, HALF, 2, P])
    mat_c = m.sb("mat_c", [P, PAIRS, 2, P])
    toep = m.sb("toep", [P, 2, 2 * GP, P])
    state = resid[:, :, :].rearrange("p t d -> p (t d)").rearrange("p (q r t) -> p q r t", q=PAIRS, r=2)
    padded = m.sb("padded", [P, 2, GP, 2, 2, TILES])
    cols = m.sb("cols", [P, 4, LAYERS, PAIRS])
    cdz = m.sb("cdz", [P, PAIRS, 2, 2])
    cds = m.sb("cds", [P, PAIRS, 2])
    wr = m.sb("wr", [P, PAIRS, 2, BATCH])
    ws = m.sb("ws", [P, PAIRS, 2, BATCH])
    s1 = m.sb("s1", [P, PAIRS, 2, BATCH])
    s2 = m.sb("s2", [P, PAIRS, 2, BATCH])
    rot = m.sb("rot", [P, GP, 2, TILES])
    stat = m.sb("stat", [P, 3, TILES])
    kk = m.sb("kk", [P, P])
    kb = m.sb("kb", [P, 1])
    quarter = m.sb("quarter", [P, 1])
    scale_bc = m.sb("scale_bc", [P, D])
    bias_bc = m.sb("bias_bc", [P, D])
    kt = m.sb("kt", [P, P])
    krow = m.sb("krow", [D, P])
    zrow = m.sb("zrow", [P, 2, P])
    k0 = m.sb("k0", [P, 2])
    wout = m.sb("wout", [P, 2 * P])
    w_in = m.sb("w_in", [P, 2 * D])
    brow = m.sb("brow", [1, 2 * P])
    ones = m.sb("ones", [1, P])
    yT = m.sb("yT", [P, 2, GP * P // 2])
    gate = m.sb("gate", [P, 2, GP, D])
    zz = m.sb("zz", [P, 2, GP, D])
    dram_resid = nc.dram_tensor("parked_resid", (P, TILES, D), F32).ap()
    dram_row = nc.dram_tensor("pole_rows", (2, LAYERS, D, D), F32).ap()
    dram_k = nc.dram_tensor("kernel_rows", (LAYERS, D, 2 * P), F32)
    k_ap = dram_k.ap()

    with ExitStack() as prep_stack:
        pm = Memory(nc, prep_stack, "prep")
        N2 = 2 * D

        names = ["alog", "aim", "cre", "cim", "x", "f", "r", "q1", "sn", "cs", "sh", "th", "zr", "zi", "den", "ta", "tb",
                 "qr", "qi", "cdr", "cdi", "ar"] + [f"twice{i}" for i in range(8)]
        slots = {n: angle_c[:, :, :].rearrange("p a b -> p (a b)")[:, i * N2:(i + 1) * N2] for i, n in enumerate(names)}

        def v3(n):
            return slots[n].rearrange("p (l n) -> p l n", n=D)

        ldt = pm.sb("ldt", [P, 2])
        dt = pm.sb("dt", [P, 2])
        dskip = pm.sb("dskip", [P, 2])
        ps_q = pm.ps("ps_q", [P, 4, P])
        loaded, made, zero, trig_in, trig_out, ready, tr_done, tr_read, parked = map(pm.sem, (
            "loaded", "made", "zero", "trig_in", "trig_out", "ready", "tr_done", "tr_read", "parked"))
        root_in, root_out = pm.sem("root_in"), pm.sem("root_out")
        with nc.Block() as block:

            @block.sync
            def _(sp):
                for n, src in (("alog", "Alog"), ("aim", "Aim"), ("cre", "Cre"), ("cim", "Cim")):
                    sp.dma_start(v3(n), A["L0_attn_" + src].rearrange("(l k) h n -> (k h) l n", k=2)).then_inc(loaded, 16)
                for dst, src in ((ldt, "log_dt"), (dskip, "D")):
                    for i in range(2):
                        sp.dma_start(dst[:, i:i + 1], A["L0_attn_" + src][2 * i:2 * i + 2, :].rearrange("k h -> (k h)").unsqueeze(1)).then_inc(loaded, 16)
                sp.dma_start(dram_resid, resid[:, :, :]).then_inc(parked, 16)
                sp.wait_ge(ready, 1)
                for i, n in enumerate(("f", "x")):
                    sp.dma_start(dram_row[i].rearrange("(l k) h n -> (k h) l n", k=2), v3(n)).then_inc(parked, 16)
                sp.wait_ge(zero, 1)
                sp.dma_start(k_ap.rearrange("(l k) h x -> (k h) l x", k=2)[:, :, 1:P + 1], zrow[:, :, :]).then_inc(parked, 16)
                sp.wait_ge(parked, 64)

            @block.gpsimd
            def _(pool):
                nc.gpsimd.iota(kk[:, :], pattern=[[1, P]], base=1, channel_multiplier=0,
                               allow_small_or_imprecise_dtypes=True).then_inc(made, 1)
                pool.wait_ge(made, 1)
                nc.gpsimd.iota(kb[:, :], pattern=[[0, 1]], base=0, channel_multiplier=1,
                               allow_small_or_imprecise_dtypes=True).then_inc(made, 1)
                pool.wait_ge(made, 2)
                for i, (buf, val) in enumerate(((quarter[:, :], QUARTER), (ones[:, :], 1.0), (wout[:, :], 0.0),
                                                (cdz[:, :, :, :], 0.0), (kt[:, :], 0.0), (padded[:, :, :, :, :, :], 0.0))):
                    nc.gpsimd.memset(buf, val).then_inc(made, 1)
                    pool.wait_ge(made, 3 + i)

            @block.scalar
            def _(act):
                act.wait_ge(loaded, 128)
                nc.scalar.activation(dt[:, :], ldt[:, :], ACT.Exp)
                nc.scalar.activation(slots["ar"], slots["alog"], ACT.Exp).then_inc(trig_out, 1)
                act.wait_ge(trig_in, 1)
                nc.scalar.activation(slots["th"], slots["x"], ACT.Tanh, scale=0.5)
                nc.scalar.activation(slots["q1"], slots["r"], ACT.Abs)
                act.drain()
                act.wait_ge(made, 3)
                nc.scalar.activation(slots["cs"], slots["q1"], ACT.Sin, scale=-TURN, bias=quarter[:, :])
                nc.scalar.activation(slots["sn"], slots["r"], ACT.Sin, scale=TURN)
                nc.scalar.activation(slots["sh"], slots["r"], ACT.Sin, scale=TURN / 2)
                act.drain()
                act.nop().then_inc(trig_out, 1)
                act.wait_ge(root_in, 1)
                nc.scalar.activation(stat[:, 2], stat[:, 1], ACT.Sqrt).then_inc(root_out, 1)

            @block.vector
            def _(dve):
                def tt(o, a, b, op):
                    nc.vector.tensor_tensor(slots[o], slots[a], slots[b], op)
                    dve.drain()

                def ts(o, a, c0, c1, op0, op1=None):
                    if op1 is None:
                        nc.vector.tensor_scalar(slots[o], slots[a], c0, c1, op0)
                    else:
                        nc.vector.tensor_scalar(slots[o], slots[a], c0, c1, op0, op1)
                    dve.drain()

                dve.wait_ge(loaded, 128)
                dve.wait_ge(trig_out, 1)
                ts("ar", "ar", -1.0, None, ALU.mult)
                nc.vector.tensor_tensor(v3("x"), v3("ar"), over_last(dt[:, :], D), ALU.mult)
                nc.vector.tensor_tensor(v3("f"), v3("aim"), over_last(dt[:, :], D), ALU.mult)
                dve.drain()
                ts("f", "f", 1.0 / 6.283185307179586, None, ALU.mult)
                ts("ta", "f", MAGIC, MAGIC, ALU.add, ALU.subtract)
                tt("r", "f", "ta", ALU.subtract)
                dve.nop().then_inc(trig_in, 1)
                tt("den", "ar", "ar", ALU.mult)
                tt("ta", "aim", "aim", ALU.mult)
                tt("den", "den", "ta", ALU.add)
                nc.vector.reciprocal(slots["den"], slots["den"])
                dve.drain()
                dve.wait_ge(trig_out, 2)
                ts("ta", "th", -1.0, 1.0, ALU.mult, ALU.add)
                nc.vector.reciprocal(slots["ta"], slots["ta"])
                dve.drain()
                tt("th", "th", "ta", ALU.mult)
                ts("th", "th", 2.0, None, ALU.mult)
                tt("zr", "th", "cs", ALU.mult)
                tt("sh", "sh", "sh", ALU.mult)
                nc.vector.scalar_tensor_tensor(slots["zr"], slots["sh"], -2.0, slots["zr"], ALU.mult, ALU.add)
                nc.vector.scalar_tensor_tensor(slots["zi"], slots["th"], 1.0, slots["sn"], ALU.add, ALU.mult)
                dve.drain()

                def complex_mul(orr, oi, ar_, ai, br, bi, conj):
                    tt("ta", ar_, br, ALU.mult)
                    tt("tb", ai, bi, ALU.mult)
                    tt(orr, "ta", "tb", ALU.add if conj else ALU.subtract)
                    tt("ta", ai, br, ALU.mult)
                    tt("tb", ar_, bi, ALU.mult)
                    tt(oi, "ta", "tb", ALU.subtract if conj else ALU.add)

                complex_mul("qr", "qi", "zr", "zi", "ar", "aim", True)
                tt("qr", "qr", "den", ALU.mult)
                tt("qi", "qi", "den", ALU.mult)
                complex_mul("cdr", "cdi", "cre", "cim", "qr", "qi", False)
                ts("cdr", "cdr", 2.0, None, ALU.mult)
                ts("cdi", "cdi", 2.0, None, ALU.mult)
                nc.vector.tensor_reduce(out=k0[:, :], in_=v3("cdr"), axis=AX.X, op=ALU.add)
                nc.vector.memset(zrow[:, :, :], 0.0)
                dve.drain()
                nc.vector.tensor_tensor(zrow[:, :, P - 1], k0[:, :], dskip[:, :], ALU.add)
                dve.drain()
                dve.nop().then_inc(zero, 1)
                for i, n in enumerate(("f", "x", "cdr", "cdi")):
                    for half in range(2):
                        nc.vector.tensor_copy(v3(f"twice{2 * i + half}"), v3(n)[:, half, :].unsqueeze(1).broadcast_to([P, 2, D]))
                dve.drain()
                dve.nop().then_inc(ready, 1)
                for half in range(2):
                    dve.wait_ge(tr_done, half + 1)
                    for par in range(2):
                        side = slice(par * D, (par + 1) * D)
                        for k in range(2):
                            nc.vector.tensor_copy(cols[side, :, 2 * half + k, :],
                                                  ps_q[side, :, k * D + par:(k + 1) * D:2])
                    dve.drain()
                    dve.nop().then_inc(tr_read, 1)

                def root():
                    dve.drain()
                    dve.nop().then_inc(root_in, 1)
                    dve.wait_ge(root_out, 1)

                layer_norm(nc, dve, hs[:, :, :], resid[:, :, :], hs[:, :, :], y, stat, LN_EPS, root)

            @block.tensor
            def _(pe):
                pe.wait_ge(ready, 1)
                for half in range(2):
                    if half:
                        pe.wait_ge(tr_read, half)
                    for i in range(4):
                        last = nc.tensor.transpose(ps_q[:, i, :], slots[f"twice{2 * i + half}"], ident[:, :])
                    last.then_inc(tr_done, 1)

    ps_s = [m.ps(f"ps_s{i}", [P, GP, 2, TILES]) for i in range(2)]
    ps_k = m.ps("ps_k", [P, D + P])
    ps_y = [m.ps(f"ps_y{i}", [P, 2 * GP, TILES]) for i in range(2)]
    ps_t = m.ps("ps_t", [P, GP * P // 2])
    ps_z = [m.ps(f"ps_z{i}", [P, GP, P]) for i in range(2)]
    names = ("params", "rows_in", "rows_used", "wout_t", "wout_ok", "root_in", "root_out", "u_ok", "b_red", "b_trig", "b_ok",
             "c_red", "c_trig", "c_ok", "cdz_ok", "k_mm", "k_sb", "k_turned", "k_row", "k_out", "t0_used", "s_mm", "s_read", "scanned", "pad_ok",
             "pad_used", "y_mm", "y_ok", "yt_mm", "yt_ok", "z_mm", "gate_ok", "z_read", "layer_done", "y_read")
    S = {n: m.sem(n) for n in names}
    t0_in = [m.sem(f"t0_in{i}") for i in range(2)]
    NPARAM = 6
    BLOCKS = TILES // GP

    with nc.Block() as block:

        @block.sync
        def _(sp):
            with sp.Fori(0, LAYERS) as l:
                k_base = sp.snap(l * (D * 2 * P))
                sp.wait_ge(S["layer_done"], l + 1)
                sp.dma_start(scale_bc[:, :], A["L0_attn_ln_scale"][bass.ds(l, 1), :].partition_broadcast(P).squeeze(1)).then_inc(S["params"], 16)
                sp.dma_start(bias_bc[:, :], A["L0_attn_ln_bias"][bass.ds(l, 1), :].partition_broadcast(P).squeeze(1)).then_inc(S["params"], 16)
                for k in range(2):
                    sp.dma_start(w_in[:, k * D:(k + 1) * D], A["L0_attn_Wout"][bass.ds(l, 1), :, :].squeeze(0)).then_inc(S["params"], 16)
                    sp.dma_start(brow[:, k * P:(k + 1) * P], A["L0_attn_bout"][bass.ds(l, 1), :]).then_inc(S["params"], 16)
                for half in range(2):
                    if half:
                        sp.wait_ge(S["rows_used"], 4 * l + 2 * half)
                    for i in range(2):
                        src = dram_row[i].rearrange("l h n -> l (h n)")[bass.ds(l, 1), half * HCOLS:(half + 1) * HCOLS]
                        sp.dma_start(rowp[:, i, :], src.partition_broadcast(P).squeeze(1)).then_inc(S["rows_in"], 16)
                sp.wait_ge(S["k_row"], l + 1)
                sp.dma_start(k_ap[bass.ds(l, 1), :, P + 1:2 * P].squeeze(0), krow[:, 0:P - 1]).then_inc(S["k_out"], 16)
                sp.wait_ge(S["k_out"], 16 * l + 16)
                for g in range(GROUPS):
                    if g >= 2:
                        sp.wait_ge(S["t0_used"], l * GROUPS + g - 1)
                    src = bass.AP(tensor=dram_k, offset=k_base + 1 + g * 2 * GP * 2 * P, ap=[[1, P], [2 * P, 2 * GP], [1, P]])
                    sp.dma_start(toep[:, g % 2, :, :], src).then_inc(t0_in[g % 2], 16)

        @block.gpsimd
        def _(pool):
            with pool.Fori(0, LAYERS) as l:
                pool.wait_ge(S["layer_done"], l + 1)
                for half in range(2):
                    ang = angle_c[:, 0, :].rearrange("p (q i) -> p q i", i=P)
                    rnd = angle_c[:, 1, :].rearrange("p (q i) -> p q i", i=P)
                    dec = decay_c[:, :].rearrange("p (q i) -> p q i", i=P)
                    kb3 = kk[:, :].unsqueeze(1).broadcast_to([P, HALF, P])
                    col = [cols[:, i, bass.ds(l, 1), half * HALF:(half + 1) * HALF].squeeze(1) for i in range(2)]
                    nc.gpsimd.tensor_tensor(ang, kb3, over_last(col[0], P), ALU.mult)
                    nc.gpsimd.tensor_tensor(dec, kb3, over_last(col[1], P), ALU.mult)
                    pool.drain()
                    nc.gpsimd.tensor_scalar(rnd, ang, MAGIC, MAGIC, ALU.add, ALU.subtract)
                    pool.drain()
                    nc.gpsimd.tensor_tensor(ang, ang, rnd, ALU.subtract)
                    pool.drain()
                    pool.nop().then_inc(S["c_red"], 1)
                    pool.wait_ge(S["c_trig"], 2 * l + half + 1)
                    pairs = slice(half * HALF, (half + 1) * HALF)
                    nc.gpsimd.tensor_tensor(mat_c[:, pairs, 0, :], dec, rnd, ALU.mult)
                    nc.gpsimd.tensor_tensor(mat_c[:, pairs, 1, :], dec, ang, ALU.mult)
                    pool.drain()
                    pool.nop().then_inc(S["c_ok"], 1)

        @block.scalar
        def _(act):
            def gelu(l, g):
                act.wait_ge(S["y_mm"], l * GROUPS + g + 1)
                dst = y[:, :, g * 2 * GP:(g + 1) * 2 * GP].rearrange("p t h -> p h t")
                nc.scalar.activation(dst, ps_y[g % 2][:, :, :], ACT.Gelu_apprx_tanh).then_inc(S["y_read"], 1)

            with act.Fori(0, LAYERS) as l:
                act.wait_ge(S["root_in"], l + 1)
                nc.scalar.activation(stat[:, 2], stat[:, 1], ACT.Sqrt).then_inc(S["root_out"], 1)
                act.wait_ge(S["wout_t"], l + 1)
                nc.scalar.activation(wout[0:D, 0:P], ps_k[0:D, 0:P], ACT.Copy)
                nc.scalar.activation(wout[D:P, P:2 * P], ps_k[D:P, 0:P], ACT.Copy).then_inc(S["wout_ok"], 1)
                for half in range(2):
                    act.wait_ge(S["b_red"], 2 * l + half + 1)
                    act.wait_ge(S["c_red"], 2 * l + half + 1)
                    nc.scalar.activation(work[:, 1, :], work[:, 0, :], ACT.Abs)
                    nc.scalar.activation(angle_c[:, 1, :], angle_c[:, 0, :], ACT.Abs)
                    act.drain()
                    nc.scalar.activation(work[:, 1, :], work[:, 1, :], ACT.Sin, scale=-TURN, bias=quarter[:, :])
                    nc.scalar.activation(work[:, 0, :], work[:, 0, :], ACT.Sin, scale=TURN)
                    nc.scalar.activation(angle_c[:, 1, :], angle_c[:, 1, :], ACT.Sin, scale=-TURN, bias=quarter[:, :])
                    nc.scalar.activation(angle_c[:, 0, :], angle_c[:, 0, :], ACT.Sin, scale=-TURN)
                    nc.scalar.activation(decay_b[:, :], rowp[:, 1, :], ACT.Exp, scale=kb[:, :])
                    nc.scalar.activation(decay_c[:, :], decay_c[:, :], ACT.Exp)
                    act.drain()
                    act.nop().then_inc(S["b_trig"], 1)
                    act.nop().then_inc(S["rows_used"], 1)
                    act.nop().then_inc(S["c_trig"], 1)
                act.wait_ge(S["k_mm"], l + 1)
                nc.scalar.activation(kt[:, 0:D], ps_k[:, 0:D], ACT.Copy).then_inc(S["k_sb"], 1)
                act.wait_ge(S["k_turned"], l + 1)
                nc.scalar.activation(krow[:, :], ps_k[0:D, D:D + P], ACT.Copy).then_inc(S["k_row"], 1)
                act.wait_ge(S["scanned"], l + 1)
                for g in range(GROUPS):
                    if g >= 2:
                        act.wait_ge(S["y_mm"], l * GROUPS + g - 1)
                    for par in range(2):
                        side = slice(par * D, (par + 1) * D)
                        for ri in range(2):
                            dst = padded[side, g % 2, :, ri, par, :].rearrange("p q (b c) -> p q b c", c=CHUNKS)
                            src = state[side, g * GP:(g + 1) * GP, ri, :].rearrange("p q (b c) -> p q b c", c=CHUNKS)
                            nc.scalar.activation(dst[:, :, :, 1:CHUNKS], src[:, :, :, 0:CHUNKS - 1], ACT.Copy)
                    act.drain()
                    act.nop().then_inc(S["pad_ok"], 1)
                    if g >= 1:
                        gelu(l, g - 1)
                gelu(l, GROUPS - 1)
                act.drain()
                act.nop().then_inc(S["y_ok"], 1)
                for k in range(BLOCKS):
                    act.wait_ge(S["z_mm"], l * BLOCKS + k + 1)
                    if k >= 2:
                        act.wait_ge(S["z_read"], l * BLOCKS + k - 1)
                    nc.scalar.activation(gate[:, k % 2, :, :], ps_z[k % 2][:, :, D:P], ACT.Sigmoid).then_inc(S["gate_ok"], 1)

        @block.vector
        def _(dve):
            tile_bc = [P, TILES, D]
            dve.nop().then_inc(S["layer_done"], 1)
            with dve.Fori(0, LAYERS) as l:
                def root():
                    dve.drain()
                    dve.nop().then_inc(S["root_in"], 1)
                    dve.wait_ge(S["root_out"], l + 1)

                u_t = u[:, :, :].rearrange("p h t -> p t h")
                layer_norm(nc, dve, y, hs[:, :, :], y, u_t, stat, LN_EPS, root)
                dve.drain()
                dve.wait_ge(S["params"], 16 * NPARAM * l + 16 * NPARAM)
                nc.vector.tensor_tensor(y, y, scale_bc[:, :].unsqueeze(1).broadcast_to(tile_bc), ALU.mult)
                dve.drain()
                nc.vector.tensor_tensor(u_t, y, bias_bc[:, :].unsqueeze(1).broadcast_to(tile_bc), ALU.add)
                dve.drain()
                dve.nop().then_inc(S["u_ok"], 1)
                for half in range(2):
                    dve.wait_ge(S["rows_in"], 64 * l + 32 * half + 32)
                    nc.vector.tensor_scalar(work[:, 0, :], rowp[:, 0, :], kb[:, :], None, ALU.mult)
                    dve.drain()
                    dve.nop().then_inc(S["rows_used"], 1)
                    nc.vector.tensor_scalar(work[:, 1, :], work[:, 0, :], MAGIC, MAGIC, ALU.add, ALU.subtract)
                    dve.drain()
                    nc.vector.tensor_tensor(work[:, 0, :], work[:, 0, :], work[:, 1, :], ALU.subtract)
                    dve.drain()
                    dve.nop().then_inc(S["b_red"], 1)
                    dve.wait_ge(S["b_trig"], 2 * l + half + 1)
                    for ri in range(2):
                        dst = mat_b[:, :, ri, :].rearrange("p q (a n) -> p q a n", n=D)
                        tr = work[:, 1 - ri, :].rearrange("p (q a n) -> p q a n", n=D, a=2)
                        nc.vector.tensor_tensor(dst, decay_b[:, :].rearrange("p (q a n) -> p q a n", n=D, a=2), tr, ALU.mult)
                    dve.drain()
                    dve.nop().then_inc(S["b_ok"], 1)
                    if half == 0:
                        for ri in range(2):
                            for par in range(2):
                                side = slice(par * D, (par + 1) * D)
                                nc.vector.tensor_copy(cdz[side, :, ri, par], cols[side, 2 + ri, bass.ds(l, 1), :].squeeze(1))
                        cd_i = cols[:, 3, bass.ds(l, 1), :].squeeze(1)
                        nc.vector.tensor_scalar(cds[:, :, 0], cd_i, -1.0, None, ALU.mult)
                        nc.vector.tensor_copy(cds[:, :, 1], cd_i)
                        dve.drain()
                        dve.nop().then_inc(S["cdz_ok"], 1)
                    for g in range(half * GROUPS // 2, (half + 1) * GROUPS // 2):
                        dve.wait_ge(S["s_mm"], l * GROUPS + g + 1)
                        q = slice(g * GP, (g + 1) * GP)
                        cd_r = cols[:, 2, bass.ds(l, 1), q].squeeze(1)
                        for ri in range(2):
                            nc.vector.tensor_tensor(state[:, q, ri, :], ps_s[g % 2][:, :, ri, :], over_last(cd_r, TILES), ALU.mult)
                            nc.vector.tensor_tensor(rot[:, :, ri, :], ps_s[g % 2][:, :, 1 - ri, :], over_last(cds[:, q, ri], TILES), ALU.mult)
                        dve.drain()
                        dve.nop().then_inc(S["s_read"], 1)
                        nc.vector.tensor_tensor(state[:, q, :, :], state[:, q, :, :], rot[:, :, :, :], ALU.add)
                        dve.drain()
                dve.wait_ge(S["c_ok"], 2 * l + 2)
                w_last = mat_c[:, :, 0, P - 1]
                nw_last = mat_c[:, :, 1, P - 1]
                nc.vector.tensor_copy(wr[:, :, 0, :], over_last(w_last, BATCH))
                nc.vector.tensor_copy(wr[:, :, 1, :], over_last(w_last, BATCH))
                nc.vector.tensor_copy(ws[:, :, 0, :], over_last(nw_last, BATCH))
                nc.vector.tensor_scalar(ws[:, :, 1, :], over_last(nw_last, BATCH), -1.0, None, ALU.mult)
                dve.drain()
                st = state[:, :, :, :].rearrange("p q r (b c) -> p q r b c", c=CHUNKS)
                for c in range(1, CHUNKS - 1):
                    prev, cur = st[:, :, :, :, c - 1], st[:, :, :, :, c]
                    nc.vector.tensor_tensor(s1[:, :, :, :], wr[:, :, :, :], prev, ALU.mult)
                    for ri in range(2):
                        nc.vector.tensor_tensor(s2[:, :, ri, :], ws[:, :, ri, :], prev[:, :, 1 - ri], ALU.mult)
                    dve.drain()
                    nc.vector.tensor_tensor(s1[:, :, :, :], s1[:, :, :, :], s2[:, :, :, :], ALU.add)
                    dve.drain()
                    nc.vector.tensor_tensor(cur, cur, s1[:, :, :, :], ALU.add)
                    dve.drain()
                dve.nop().then_inc(S["scanned"], 1)
                for k in range(BLOCKS + 1):
                    if k < BLOCKS:
                        dve.wait_ge(S["yt_mm"], l * BLOCKS + k + 1)
                        nc.vector.tensor_copy(yT[:, k % 2, :].rearrange("p (j i) -> p j i", i=P),
                                              ps_t[:, :].rearrange("p (j i) -> p j i", i=P)[:, :, ::-1]).then_inc(S["yt_ok"], 1)
                    if k >= 1:
                        j = k - 1
                        dve.wait_ge(S["gate_ok"], l * BLOCKS + j + 1)
                        nc.vector.tensor_tensor(zz[:, j % 2, :, :], ps_z[j % 2][:, :, 0:D], gate[:, j % 2, :, :], ALU.mult).then_inc(S["z_read"], 1)
                        dve.drain()
                        t = slice(j * GP, (j + 1) * GP)
                        nc.vector.tensor_tensor(hs[:, t, :], hs[:, t, :], zz[:, j % 2, :, :], ALU.add)
                dve.drain()
                dve.nop().then_inc(S["layer_done"], 1)

        @block.tensor
        def _(pe):
            with pe.Fori(0, LAYERS) as l:
                pe.wait_ge(S["params"], 16 * NPARAM * l + 16 * NPARAM)
                nc.tensor.transpose(ps_k[:, 0:P], w_in[:, :], ident[:, :]).then_inc(S["wout_t"], 1)
                pe.wait_ge(S["u_ok"], l + 1)
                for g in range(GROUPS):
                    half = g // (GROUPS // 2)
                    if g % (GROUPS // 2) == 0:
                        pe.wait_ge(S["b_ok"], 2 * l + half + 1)
                    if g >= 2:
                        pe.wait_ge(S["s_read"], l * GROUPS + g - 1)
                    for q in range(GP):
                        pair = g * GP + q
                        for ri in range(2):
                            for par in range(2):
                                last = nc.tensor.matmul(ps_s[g % 2][par * D:(par + 1) * D, q, ri, :],
                                                        mat_b[:, pair % HALF, ri, par * D:(par + 1) * D],
                                                        u[:, 2 * pair + par, :], start=True, stop=True)
                    last.then_inc(S["s_mm"], 1)
                pe.wait_ge(S["c_ok"], 2 * l + 2)
                pe.wait_ge(S["cdz_ok"], l + 1)
                pe.wait_ge(S["wout_ok"], l + 1)
                for pair in range(PAIRS):
                    for ri in range(2):
                        last = nc.tensor.matmul(ps_k[:, 2 * pair:2 * pair + 2], mat_c[:, pair, ri, :], cdz[:, pair, ri, :],
                                                start=ri == 0, stop=ri == 1)
                last.then_inc(S["k_mm"], 1)
                pe.wait_ge(S["k_sb"], l + 1)
                nc.tensor.transpose(ps_k[:, D:D + P], kt[:, :], ident[:, :]).then_inc(S["k_turned"], 1)
                for g in range(GROUPS):
                    pe.wait_ge(S["pad_ok"], l * GROUPS + g + 1)
                    pe.wait_ge(t0_in[g % 2], 16 * (GROUPS // 2) * l + 16 * (g // 2) + 16)
                    if g >= 2:
                        pe.wait_ge(S["y_read"], l * GROUPS + g - 1)
                    for q in range(GP):
                        pair = g * GP + q
                        out = ps_y[g % 2][:, 2 * q:2 * q + 2, :]
                        for ri in range(2):
                            nc.tensor.matmul(out, mat_c[:, pair, ri, :], padded[:, g % 2, q, ri, :, :],
                                             start=ri == 0, stop=False, skip_group_check=True)
                        for par in range(2):
                            last = nc.tensor.matmul(ps_y[g % 2][:, 2 * q + par, :], toep[:, g % 2, 2 * q + par, :],
                                                    u[:, 2 * pair + par, :], start=False, stop=par == 1, skip_group_check=True)
                    last.then_inc(S["y_mm"], 1)
                    pe.drain()
                    pe.nop().then_inc(S["t0_used"], 1)
                pe.wait_ge(S["y_ok"], l + 1)
                for k in range(BLOCKS + 1):
                    if k < BLOCKS:
                        if k >= 1:
                            pe.wait_ge(S["yt_ok"], l * BLOCKS + k)
                        for j in range(GP // 2):
                            t = k * GP + 2 * j
                            last = nc.tensor.transpose(ps_t[:, j * P:(j + 1) * P], y[:, t:t + 2, :].rearrange("p t h -> p (t h)"), ident[:, :])
                        last.then_inc(S["yt_mm"], 1)
                    if k >= 1:
                        i = k - 1
                        pe.wait_ge(S["yt_ok"], l * BLOCKS + i + 1)
                        if i >= 2:
                            pe.wait_ge(S["z_read"], l * BLOCKS + i - 1)
                        for j in range(GP // 2):
                            dst = ps_z[i % 2][:, 2 * j:2 * j + 2, :].rearrange("p a b -> p (a b)")
                            nc.tensor.matmul(dst, yT[:, i % 2, j * P:(j + 1) * P], wout[:, :], start=True, stop=False)
                            last = nc.tensor.matmul(dst, ones[:, :], brow[:, :], start=False, stop=True)
                        last.then_inc(S["z_mm"], 1)

    with ExitStack() as stack:
        em = Memory(nc, stack, "s4_end")
        back = em.sem("back")
        with nc.Block() as block:

            @block.sync
            def _(sp):
                sp.dma_start(resid[:, :, :], dram_resid).then_inc(back, 16)

            @block.vector
            def _(dve):
                dve.wait_ge(back, 16)
                nc.vector.tensor_tensor(resid[:, :, :], resid[:, :, :], hs[:, :, :], ALU.add)


def expert_mixture(nc, m, A, resid, ident, flip):
    E = A["L0_ffn_Wr"].shape[1]
    PAIRS = E // 2
    HB = BATCH // 2
    COLS = HB * SEQ
    BN_EPS = 1e-3
    BLK = 4 * P
    VEC = ("b1", "g1", "be1", "m1", "v1", "b2", "g2", "be2", "m2", "v2")

    xT = m.sb("xT", [P, COLS])
    w1 = m.sb("w1", [P, 2, PAIRS, P])
    w2 = m.sb("w2", [P, PAIRS, P])
    wo = m.sb("wo", [P, PAIRS, D])
    bo = m.sb("bo", [E, D])
    wr = m.sb("wr", [P, E])
    br = m.sb("br", [P, E])
    rowsv = m.sb("rowsv", [len(VEC) * PAIRS, P])
    vec = m.sb("vec", [P, len(VEC), PAIRS])
    fold = m.sb("fold", [P, 2, 2, PAIRS])
    sd = m.sb("sd", [P, 2, PAIRS])
    wb = m.sb("wb", [P, PAIRS, SEQ])
    ybo = m.sb("ybo", [P, CHUNKS, D])
    V = {n: i for i, n in enumerate(VEC)}

    with ExitStack() as stack:
        pm = Memory(nc, stack, "gate")
        x = pm.sb("x", [P, TILES // 2, 2, D])
        square = pm.sb("square", [P, 2, TILES // 2, D])
        stat = pm.sb("stat", [P, 3, TILES])
        stat4 = stat[:, :, :].rearrange("p s (a t) -> p s a t", a=2)
        lg = pm.sb("lg", [P, CHUNKS, E])
        ex = pm.sb("ex", [P, CHUNKS, E])
        red = pm.sb("red", [P, 2, CHUNKS])
        wT = pm.sb("wT", [E, SEQ])
        sel = pm.sb("sel", [E, PAIRS, P])
        ps_v = pm.ps("ps_v", [P, len(VEC) * PAIRS])
        ps_x = [pm.ps(f"ps_x{i}", [P, BLK]) for i in range(2)]
        ps_l = pm.ps("ps_l", [P, CHUNKS, E])
        ps_t = pm.ps("ps_t", [E, BLK])
        ps_b = [pm.ps(f"ps_b{i}", [P, BLK]) for i in range(2)]
        ps_y = pm.ps("ps_y", [P, 8, D])
        names = ("zeroed", "loaded", "vec_tr", "root_in", "root_out", "x_ok", "xt_mm", "xt_sb", "l_mm", "exp_in", "exp_out",
                 "soft_ok", "wt_mm", "wt_sb", "wb_mm", "wb_sb", "sel_ok", "yb_mm", "yb_sb")
        S = {n: pm.sem(n) for n in names}
        ffn = {k: A["L0_ffn_" + k] for k in ("Wr", "br", "W1", "W2", "Wo", "bo") + VEC}
        NB = COLS // BLK

        with nc.Block() as block:

            @block.sync
            def _(sp):
                n = 0
                for i, v in enumerate(VEC):
                    sp.dma_start(rowsv[i * PAIRS:(i + 1) * PAIRS, :], ffn[v].rearrange("(q e) h -> q (e h)", e=2)).then_inc(S["loaded"], 16)
                    n += 1
                for k in range(2):
                    sp.dma_start(wr[k * D:(k + 1) * D, :], ffn["Wr"]).then_inc(S["loaded"], 16)
                    n += 1
                sp.dma_start(br[:, :], ffn["br"].partition_broadcast(P)).then_inc(S["loaded"], 16)
                sp.dma_start(bo[:, :], ffn["bo"]).then_inc(S["loaded"], 16)
                sp.dma_start(wo[:, :, :], ffn["Wo"].rearrange("(q e) h d -> (e h) q d", e=2)).then_inc(S["loaded"], 16)
                sp.wait_ge(S["zeroed"], 1)
                for k in range(2):
                    side = slice(k * D, (k + 1) * D)
                    for e in range(2):
                        sp.dma_start(w1[side, k, :, e * D:(e + 1) * D], ffn["W1"].rearrange("(q e) d h -> e d q h", e=2)[e]).then_inc(S["loaded"], 16)
                    sp.dma_start(w2[side, :, side], ffn["W2"].rearrange("(q e) h k -> e h q k", e=2)[k]).then_inc(S["loaded"], 16)
                assert n + 3 + 6 == 21
                sp.wait_ge(S["loaded"], 16 * 21)

            @block.gpsimd
            def _(pool):
                nc.gpsimd.memset(w1[:, :, :, :], 0.0).then_inc(S["sel_ok"], 1)
                pool.wait_ge(S["sel_ok"], 1)
                nc.gpsimd.memset(w2[:, :, :], 0.0).then_inc(S["zeroed"], 1)
                pool.wait_ge(S["zeroed"], 1)
                nc.gpsimd.memset(sel[:, :, :], 0.0).then_inc(S["sel_ok"], 1)
                pool.wait_ge(S["sel_ok"], 2)
                nc.gpsimd.affine_select(out=sel[:, :, :], in_=sel[:, :, :], compare_op=ALU.not_equal, fill=1.0, base=0,
                                        pattern=[[-2, PAIRS], [-1, 2], [0, D]], channel_multiplier=1).then_inc(S["sel_ok"], 1)
                pool.wait_ge(S["sel_ok"], 3)

            @block.scalar
            def _(act):
                act.wait_ge(S["root_in"], 1)
                nc.scalar.activation(stat[:, 2], stat[:, 1], ACT.Sqrt)
                nc.scalar.activation(sd[:, :, :], sd[:, :, :], ACT.Sqrt)
                act.drain()
                act.nop().then_inc(S["root_out"], 1)
                for k in range(NB):
                    act.wait_ge(S["xt_mm"], k + 1)
                    nc.scalar.activation(xT[:, k * BLK:(k + 1) * BLK], ps_x[k % 2][:, :], ACT.Copy).then_inc(S["xt_sb"], 1)
                act.wait_ge(S["exp_in"], 1)
                nc.scalar.activation(ex[:, :, :], lg[:, :, :], ACT.Exp).then_inc(S["exp_out"], 1)
                for k in range(4):
                    for q in range(PAIRS):
                        n = k * PAIRS + q
                        act.wait_ge(S["wb_mm"], n + 1)
                        nc.scalar.activation(wb[:, q, k * BLK:(k + 1) * BLK], ps_b[n % 2][:, :], ACT.Copy).then_inc(S["wb_sb"], 1)

            @block.vector
            def _(dve):
                dve.wait_ge(S["vec_tr"], 1)
                nc.vector.tensor_copy(vec[:, :, :], ps_v[:, :].rearrange("p (v q) -> p v q", q=PAIRS))
                dve.drain()
                for i, k in enumerate("12"):
                    nc.vector.tensor_scalar(sd[:, i, :], vec[:, V["v" + k], :], BN_EPS, None, ALU.add)

                def root():
                    dve.drain()
                    dve.nop().then_inc(S["root_in"], 1)
                    dve.wait_ge(S["root_out"], 1)

                x_t = x[:, :, :, :].rearrange("p t a d -> p a t d")
                r_t = resid[:, :, :].rearrange("p (a t) d -> p a t d", a=2)
                layer_norm(nc, dve, x_t, r_t, x_t, square[:, :, :, :], stat4, LN_EPS, root)
                dve.drain()
                dve.nop().then_inc(S["x_ok"], 1)
                nc.vector.reciprocal(sd[:, :, :], sd[:, :, :])
                dve.drain()
                for i, k in enumerate("12"):
                    nc.vector.tensor_tensor(fold[:, i, 0, :], vec[:, V["g" + k], :], sd[:, i, :], ALU.mult)
                    nc.vector.tensor_tensor(fold[:, i, 1, :], vec[:, V["b" + k], :], vec[:, V["m" + k], :], ALU.subtract)
                    dve.drain()
                    nc.vector.tensor_tensor(fold[:, i, 1, :], fold[:, i, 1, :], fold[:, i, 0, :], ALU.mult)
                    dve.drain()
                    nc.vector.tensor_tensor(fold[:, i, 1, :], fold[:, i, 1, :], vec[:, V["be" + k], :], ALU.add)
                dve.wait_ge(S["l_mm"], 1)
                nc.vector.scalar_tensor_tensor(lg[:, :, :], ps_l[:, :, :], 1.0 / BATCH, br[:, :].unsqueeze(1).broadcast_to([P, CHUNKS, E]),
                                               ALU.mult, ALU.add)
                dve.drain()
                nc.vector.tensor_reduce(out=red[:, 0, :], in_=lg[:, :, :], axis=AX.X, op=ALU.max)
                dve.drain()
                nc.vector.tensor_tensor(lg[:, :, :], lg[:, :, :], over_last(red[:, 0, :], E), ALU.subtract)
                dve.drain()
                dve.nop().then_inc(S["exp_in"], 1)
                dve.wait_ge(S["exp_out"], 1)
                nc.vector.tensor_reduce(out=red[:, 1, :], in_=ex[:, :, :], axis=AX.X, op=ALU.add)
                dve.drain()
                nc.vector.reciprocal(red[:, 0, :], red[:, 1, :])
                dve.drain()
                nc.vector.tensor_tensor(ex[:, :, :], ex[:, :, :], over_last(red[:, 0, :], E), ALU.mult)
                dve.drain()
                dve.nop().then_inc(S["soft_ok"], 1)
                for k in range(4):
                    dve.wait_ge(S["wt_mm"], k + 1)
                    nc.vector.tensor_copy(wT[:, k * BLK:(k + 1) * BLK], ps_t[:, :]).then_inc(S["wt_sb"], 1)
                for k in range(2):
                    dve.wait_ge(S["yb_mm"], k + 1)
                    nc.vector.tensor_copy(ybo[:, k * 8:(k + 1) * 8, :], ps_y[:, :, :]).then_inc(S["yb_sb"], 1)

            @block.tensor
            def _(pe):
                pe.wait_ge(S["loaded"], 16 * 21)
                nv = len(VEC) * PAIRS
                nc.tensor.transpose(ps_v[:, :], rowsv[:, :], ident[0:nv, 0:nv]).then_inc(S["vec_tr"], 1)
                pe.wait_ge(S["x_ok"], 1)
                for k in range(NB):
                    if k >= 2:
                        pe.wait_ge(S["xt_sb"], k - 1)
                    for j in range(4):
                        t = 4 * k + j
                        last = nc.tensor.transpose(ps_x[k % 2][:, j * P:(j + 1) * P], x[:, t, :, :].rearrange("p a d -> p (a d)"), ident[:, :])
                    last.then_inc(S["xt_mm"], 1)
                pe.wait_ge(S["xt_sb"], NB)
                for c in range(CHUNKS):
                    for k in range(HB):
                        a = k * SEQ + c * P
                        last = nc.tensor.matmul(ps_l[:, c, :], xT[:, a:a + P], wr[:, :], start=k == 0, stop=k == HB - 1)
                last.then_inc(S["l_mm"], 1)
                pe.wait_ge(S["soft_ok"], 1)
                for k in range(4):
                    if k:
                        pe.wait_ge(S["wt_sb"], k)
                    for j in range(4):
                        last = nc.tensor.transpose(ps_t[:, j * P:(j + 1) * P], ex[:, 4 * k + j, :], ident[:, :])
                    last.then_inc(S["wt_mm"], 1)
                pe.wait_ge(S["wt_sb"], 4)
                pe.wait_ge(S["sel_ok"], 3)
                for k in range(4):
                    for q in range(PAIRS):
                        n = k * PAIRS + q
                        if n >= 2:
                            pe.wait_ge(S["wb_sb"], n - 1)
                        nc.tensor.matmul(ps_b[n % 2][:, :], sel[:, q, :], wT[:, k * BLK:(k + 1) * BLK], start=True, stop=True).then_inc(S["wb_mm"], 1)
                for k in range(2):
                    if k:
                        pe.wait_ge(S["yb_sb"], 1)
                    for j in range(8):
                        c = 8 * k + j
                        last = nc.tensor.matmul(ps_y[:, j, :], wT[:, c * P:(c + 1) * P], bo[:, :], start=True, stop=True)
                    last.then_inc(S["yb_mm"], 1)

    STEPS = BATCH * PAIRS
    NBLK = SEQ // BLK
    h1 = m.sb("h1", [P, 2, BLK])
    h2 = m.sb("h2", [P, 2, BLK])
    h2w = m.sb("h2w", [P, 2, PAIRS, BLK])
    add = m.sb("add", [P, 2, 4, D])
    ps1 = [m.ps(f"ps1{i}", [P, BLK]) for i in range(2)]
    ps2 = [m.ps(f"ps2{i}", [P, BLK]) for i in range(2)]
    ps_o = [m.ps(f"ps_o{i}", [P, 4, D]) for i in range(2)]
    names = ("h1_mm", "h1_ok", "h2_mm", "h2_ok", "h2w_ok", "wo_mm", "wo_read")
    S = {n: m.sem(n) for n in names}

    with nc.Block() as block:

        @block.tensor
        def _(pe):
            with pe.Fori(0, NBLK) as k:
                for s in range(STEPS + 2):
                    if s < STEPS:
                        b, q = divmod(s, PAIRS)
                        if s >= 2:
                            pe.wait_ge(S["h1_ok"], k * STEPS + s - 1)
                        base = b % HB * SEQ
                        nc.tensor.matmul(ps1[s % 2][:, :], w1[:, b // HB, q, :], xT[:, bass.ds(k * BLK + base, BLK)],
                                         start=True, stop=True).then_inc(S["h1_mm"], 1)
                    if s >= 2 and (s - 2) % PAIRS == PAIRS - 1:
                        b = (s - 2) // PAIRS
                        pe.wait_ge(S["h2w_ok"], k * STEPS + (b + 1) * PAIRS)
                        pe.wait_ge(S["wo_read"], k * BATCH + b + 1)
                        for j in range(4):
                            for q in range(PAIRS):
                                last = nc.tensor.matmul(ps_o[b % 2][:, j, :], h2w[:, b % 2, q, j * P:(j + 1) * P], wo[:, q, :],
                                                        start=q == 0, stop=q == PAIRS - 1)
                        last.then_inc(S["wo_mm"], 1)
                    if 1 <= s <= STEPS:
                        i = s - 1
                        pe.wait_ge(S["h1_ok"], k * STEPS + i + 1)
                        if i >= 2:
                            pe.wait_ge(S["h2_ok"], k * STEPS + i - 1)
                        nc.tensor.matmul(ps2[i % 2][:, :], w2[:, i % PAIRS, :], h1[:, i % 2, :], start=True, stop=True).then_inc(S["h2_mm"], 1)

        @block.scalar
        def _(act):
            with act.Fori(0, NBLK) as k:
                for s in range(STEPS + 1):
                    if s < STEPS:
                        q = s % PAIRS
                        act.wait_ge(S["h1_mm"], k * STEPS + s + 1)
                        if s >= 2:
                            act.wait_ge(S["h2_mm"], k * STEPS + s - 1)
                        nc.scalar.activation(h1[:, s % 2, :], ps1[s % 2][:, :], ACT.Relu, bias=fold[:, 0, 1, q:q + 1],
                                             scale=fold[:, 0, 0, q:q + 1]).then_inc(S["h1_ok"], 1)
                    if s >= 1:
                        i, q = s - 1, (s - 1) % PAIRS
                        act.wait_ge(S["h2_mm"], k * STEPS + i + 1)
                        if i >= 2:
                            act.wait_ge(S["h2w_ok"], k * STEPS + i - 1)
                        nc.scalar.activation(h2[:, i % 2, :], ps2[i % 2][:, :], ACT.Relu, bias=fold[:, 1, 1, q:q + 1],
                                             scale=fold[:, 1, 0, q:q + 1]).then_inc(S["h2_ok"], 1)

        @block.vector
        def _(dve):
            dve.nop().then_inc(S["wo_read"], 2)
            with dve.Fori(0, NBLK) as k:
                def finish(b):
                    dve.wait_ge(S["wo_mm"], k * BATCH + b + 1)
                    nc.vector.tensor_tensor(add[:, b % 2, :, :], ps_o[b % 2][:, :, :], ybo[:, bass.ts(k, 4), :], ALU.add).then_inc(S["wo_read"], 1)
                    dve.drain()
                    tiles = resid[:, bass.ds(k * 4 + b * CHUNKS, 4), :]
                    nc.vector.tensor_tensor(tiles, tiles, add[:, b % 2, :, :], ALU.add)

                for s in range(STEPS):
                    b, q = divmod(s, PAIRS)
                    dve.wait_ge(S["h2_ok"], k * STEPS + s + 1)
                    nc.vector.tensor_tensor(h2w[:, b % 2, q, :], h2[:, s % 2, :], wb[:, q, bass.ts(k, BLK)], ALU.mult).then_inc(S["h2w_ok"], 1)
                    if q == PAIRS - 1 and b >= 1:
                        finish(b - 1)
                finish(BATCH - 1)


def sigmoid_attention(nc, m, A, resid, ident, flip):
    HEADS = 8
    PAIRS = HEADS // 2
    SCALE = float(D) ** 0.5
    X_UP, W_UP, Q_UP = 2.0 ** 4, 2.0 ** 8, 2.0 ** 6
    BLK = 512
    QB = SEQ // BLK
    IH = 2
    N = TILES * P

    wq = m.sb("wq", [P, HEADS, 2, D], F16)
    wk = m.sb("wk", [P, HEADS, 2, D], F16)
    wv = m.sb("wv", [P, HEADS, D], F16)
    wo = m.sb("wo", [P, PAIRS, D])
    x_hi = m.sb("x_hi", [P, N], F16)
    x_lo = m.sb("x_lo", [P, N], F16)

    with ExitStack() as stack:
        pm = Memory(nc, stack, "split")
        x = pm.sb("x", [P, TILES, D])
        twice = pm.sb("twice", [P, TILES, 2, D])
        stat = pm.sb("stat", [P, 3, TILES])
        raw = [pm.sb(f"raw{i}", [P, HEADS * D]) for i in range(3)]
        ps = [pm.ps(f"ps{i}", [P, BLK]) for i in range(4)]
        loaded, root_in, root_out, x_ok, x_tr, hi_ok, lo_ok = map(pm.sem, (
            "loaded", "root_in", "root_out", "x_ok", "x_tr", "hi_ok", "lo_ok"))
        NB = N // BLK
        with nc.Block() as block:

            @block.sync
            def _(sp):
                for i, n in enumerate(("Wq", "Wk", "Wv")):
                    for k in range(2):
                        sp.dma_start(raw[i][k * D:(k + 1) * D, :], A["L1_attn_" + n]).then_inc(loaded, 16)
                wo_src = A["L1_attn_Wo"].rearrange("(f q a) o -> a f q o", a=2, q=PAIRS)
                for k in range(2):
                    sp.dma_start(wo[k * D:(k + 1) * D, :, :], wo_src[k]).then_inc(loaded, 16)
                sp.wait_ge(loaded, 128)

            @block.vector
            def _(dve):
                dve.wait_ge(loaded, 128)
                lo_rows = slice(D, P)
                for i, dst in enumerate((wq, wk, wv)):
                    nc.vector.tensor_scalar(raw[i][:, :], raw[i][:, :], W_UP, None, ALU.mult)
                dve.drain()
                parts = []
                for i, dst in enumerate((wq, wk, wv)):
                    src = raw[i][:, :].rearrange("p (f h) -> p h f", h=HEADS)
                    if i < 2:
                        src = src.unsqueeze(2).broadcast_to([P, HEADS, 2, D])
                        parts.append((dst[:, :, :, :], dst[lo_rows, :, :, :], src, src[lo_rows]))
                    else:
                        parts.append((dst[:, :, :], dst[lo_rows, :, :], src, src[lo_rows]))
                for dst, _, src, _ in parts:
                    nc.vector.tensor_copy(dst, src)
                dve.drain()
                for _, dst, _, src in parts:
                    nc.vector.tensor_tensor(dst, src, dst, ALU.subtract)

                def root():
                    dve.drain()
                    dve.nop().then_inc(root_in, 1)
                    dve.wait_ge(root_out, 1)

                layer_norm(nc, dve, x[:, :, :], resid[:, :, :], x[:, :, :], twice[:, :, 0, :], stat, LN_EPS, root)
                dve.drain()
                for k in range(2):
                    nc.vector.tensor_copy(twice[:, :, k, :], x[:, :, :])
                dve.drain()
                dve.nop().then_inc(x_ok, 1)
                for k in range(NB):
                    dve.wait_ge(hi_ok, k + 1)
                    c = slice(k * BLK, (k + 1) * BLK)
                    nc.vector.scalar_tensor_tensor(x_lo[:, c], ps[k % 4][:, :], X_UP, x_hi[:, c], ALU.mult, ALU.subtract).then_inc(lo_ok, 1)

            @block.scalar
            def _(act):
                act.wait_ge(root_in, 1)
                nc.scalar.activation(stat[:, 2], stat[:, 1], ACT.Sqrt).then_inc(root_out, 1)
                for k in range(NB):
                    act.wait_ge(x_tr, k + 1)
                    nc.scalar.activation(x_hi[:, k * BLK:(k + 1) * BLK], ps[k % 4][:, :], ACT.Copy, scale=X_UP).then_inc(hi_ok, 1)

            @block.tensor
            def _(pe):
                pe.wait_ge(x_ok, 1)
                for k in range(NB):
                    if k >= 4:
                        pe.wait_ge(lo_ok, k - 3)
                    for j in range(4):
                        last = nc.tensor.transpose(ps[k % 4][:, j * P:(j + 1) * P],
                                                   twice[:, 4 * k + j, :, :].rearrange("p a d -> p (a d)"), ident[:, :])
                    last.then_inc(x_tr, 1)

    k_st = m.sb("k_st", [P, 2, SEQ], F16)
    q_hi = m.sb("q_hi", [P, 2, SEQ], F16)
    q_lo = m.sb("q_lo", [P, 2, SEQ], F16)
    v_st = m.sb("v_st", [P, CHUNKS, 2, D])
    sig = m.sb("sig", [P, 2, 2, 2 * BLK])
    ctxT = m.sb("ctxT", [P, PAIRS, SEQ])
    ps_s = [m.ps(f"ps_s{h}", [P, 2 * BLK]) for h in range(2)]
    ps_o = m.ps("ps_o", [P, 2, BLK])
    ps_p = [m.ps(f"ps_p{i}", [P, BLK]) for i in range(2)]
    names = ("p_mm", "p_hi", "p_read", "qk_mm", "sig_ok", "pv_mm", "o_read", "wo_mm", "wo_read")
    S = {n: m.sem(n) for n in names}
    KQ = 4 * QB
    PB = KQ + CHUNKS // 4
    JJ = IH * CHUNKS

    with nc.Block() as block:

        @block.tensor
        def _(pe):
            with pe.Fori(0, BATCH) as b:
                with pe.Fori(0, PAIRS) as hp:
                    n = b * PAIRS + hp
                    for i in range(PB):
                        if i >= 2:
                            pe.wait_ge(S["p_read"], n * PB + i - 1)
                        if i < KQ:
                            w = wk if i < KQ // 2 else wq
                            h, c = divmod(i % (KQ // 2), QB)
                            lhsT = w[:, bass.ds(hp * 2 + h, 1), :, :].rearrange("p a t f -> p (a t f)")
                            for part, xs in enumerate((x_hi, x_lo)):
                                last = nc.tensor.matmul(ps_p[i % 2][:, :], lhsT, xs[:, bass.ds(b * SEQ + c * BLK, BLK)],
                                                        start=part == 0, stop=part == 1)
                        else:
                            for j in range(4):
                                c = (i - KQ) * 4 + j
                                for part, xs in enumerate((x_hi, x_lo)):
                                    last = nc.tensor.matmul(ps_p[i % 2][:, j * P:(j + 1) * P], xs[:, bass.ds(b * SEQ + c * P, P)],
                                                            wv[:, bass.ds(hp * 2, 2), :].rearrange("p a f -> p (a f)"),
                                                            start=part == 0, stop=part == 1)
                        last.then_inc(S["p_mm"], 1)
                    pe.wait_ge(S["p_read"], n * PB + PB)
                    for jj in range(JJ + 1):
                        if jj < JJ:
                            ih, j = divmod(jj, CHUNKS)
                            for h in range(2):
                                s = 2 * jj + h
                                if s >= 2:
                                    pe.wait_ge(S["sig_ok"], n * 2 * JJ + s - 1)
                                for part, qs in enumerate((q_hi, q_lo)):
                                    for i2 in range(2):
                                        c = (2 * ih + i2) * BLK
                                        last = nc.tensor.matmul(ps_s[h][:, i2 * BLK:(i2 + 1) * BLK], k_st[:, h, j * P:(j + 1) * P],
                                                                qs[:, h, c:c + BLK], start=part == 0, stop=part == 1)
                                last.then_inc(S["qk_mm"], 1)
                        if jj >= 1:
                            ih, j = divmod(jj - 1, CHUNKS)
                            pe.wait_ge(S["sig_ok"], n * 2 * JJ + 2 * jj)
                            if j == 0:
                                pe.wait_ge(S["o_read"], n * IH + ih + 1)
                            for i2 in range(2):
                                for h in range(2):
                                    last = nc.tensor.matmul(ps_o[h * D:(h + 1) * D, i2, :], v_st[:, j, h, :],
                                                            sig[:, (jj - 1) % 2, h, i2 * BLK:(i2 + 1) * BLK],
                                                            start=j == 0, stop=j == CHUNKS - 1)
                            last.then_inc(S["pv_mm"], 1)
                pe.wait_ge(S["o_read"], b * (PAIRS * IH) + PAIRS * IH + 1)
                for k in range(2):
                    for t in range(8):
                        for hp in range(PAIRS):
                            last = nc.tensor.matmul(ps_p[k][:, t * D:(t + 1) * D], ctxT[:, hp, (8 * k + t) * P:(8 * k + t + 1) * P],
                                                    wo[:, hp, :], start=hp == 0, stop=hp == PAIRS - 1)
                    last.then_inc(S["wo_mm"], 1)
                pe.wait_ge(S["wo_read"], 2 * b + 2)

        @block.scalar
        def _(act):
            act.preload_act_table(ACT.Sigmoid)
            with act.Fori(0, BATCH) as b, act.Fori(0, PAIRS) as hp:
                n = b * PAIRS + hp
                for i in range(KQ):
                    act.wait_ge(S["p_mm"], n * PB + i + 1)
                    dst = k_st if i < KQ // 2 else q_hi
                    h, c = divmod(i % (KQ // 2), QB)
                    nc.scalar.activation(dst[:, h, c * BLK:(c + 1) * BLK], ps_p[i % 2][:, :], ACT.Copy,
                                         scale=Q_UP / (X_UP * W_UP)).then_inc(S["p_hi"], 1)
                for s in range(2 * JJ):
                    jj, h = divmod(s, 2)
                    act.wait_ge(S["qk_mm"], n * 2 * JJ + s + 1)
                    if jj >= 2:
                        act.wait_ge(S["pv_mm"], n * JJ + jj - 1)
                    nc.scalar.activation(sig[:, jj % 2, h, :], ps_s[h][:, :], ACT.Sigmoid,
                                         scale=SCALE / (Q_UP * Q_UP)).then_inc(S["sig_ok"], 1)

        @block.vector
        def _(dve):
            dve.nop().then_inc(S["o_read"], 1)
            with dve.Fori(0, BATCH) as b:
                with dve.Fori(0, PAIRS) as hp:
                    n = b * PAIRS + hp
                    for i in range(PB):
                        if i < KQ:
                            h, c = divmod(i % (KQ // 2), QB)
                            cols = slice(c * BLK, (c + 1) * BLK)
                            dve.wait_ge(S["p_hi"], n * KQ + i + 1)
                            if i < KQ // 2:
                                dst = hi = k_st[D:P, h, cols]
                                src = ps_p[i % 2][D:P, :]
                            else:
                                dst, hi, src = q_lo[:, h, cols], q_hi[:, h, cols], ps_p[i % 2][:, :]
                            nc.vector.scalar_tensor_tensor(dst, src, Q_UP / (X_UP * W_UP), hi, ALU.mult, ALU.subtract).then_inc(S["p_read"], 1)
                        else:
                            dve.wait_ge(S["p_mm"], n * PB + i + 1)
                            c = (i - KQ) * 4
                            nc.vector.tensor_scalar(v_st[:, c:c + 4, :, :].rearrange("p c h f -> p (c h f)"), ps_p[i % 2][:, :],
                                                    1.0 / (X_UP * W_UP), None, ALU.mult).then_inc(S["p_read"], 1)
                    for ih in range(IH):
                        dve.wait_ge(S["pv_mm"], n * JJ + (ih + 1) * CHUNKS)
                        dst = ctxT[:, bass.ds(hp, 1), ih * 2 * BLK:(ih + 1) * 2 * BLK].squeeze(1)
                        nc.vector.tensor_copy(dst, ps_o[:, :, :].rearrange("p a b -> p (a b)")).then_inc(S["o_read"], 1)
                for k in range(2):
                    dve.wait_ge(S["wo_mm"], 2 * b + k + 1)
                    tiles = resid[:, bass.ds(b * CHUNKS + 8 * k, 8), :]
                    nc.vector.scalar_tensor_tensor(tiles, ps_p[k][:, :].rearrange("p (t o) -> p t o", o=D), 0.0, tiles,
                                                   ALU.max, ALU.add).then_inc(S["wo_read"], 1)


def routed_mlp(nc, m, A, resid, ident, flip):
    HID = A["L1_ffn_w1"].shape[1]
    MT = HID // P
    TAKE = SEQ // 2 - 1
    ROUNDS_PER = 5
    BLK = 4 * P
    HALF = TILES // 2
    NBLK = HALF * P // BLK
    ROUNDS = ROUNDS_PER * NBLK

    x = m.sb("x", [P, HALF, 2, D])
    x_t = x[:, :, :, :].rearrange("p t a d -> p a t d")
    xT = m.sb("xT", [P, HALF * P])
    y = m.sb("y", [P, TILES, D])
    w = m.sb("w", [P, TILES])
    w1 = m.sb("w1", [P, 2, HID])
    w2 = m.sb("w2", [P, MT, D])
    b1 = m.sb("b1", [P, MT])
    b2 = m.sb("b2", [P, D])
    wr = m.sb("wr", [P, D])
    br = m.sb("br", [P, 1])
    ones = m.sb("ones", [P, P])
    after = m.sb("after", [P, P])
    bound = m.sb("bound", [P, BATCH])
    step = m.sb("step", [P, BATCH])
    low = m.sb("low", [P, BATCH])

    with ExitStack() as stack:
        pm = Memory(nc, stack, "route")
        square = pm.sb("square", [P, TILES, D])
        stat = pm.sb("stat", [P, 3, TILES])
        stat4 = stat[:, :, :].rearrange("p s (a t) -> p s a t", a=2)
        top = pm.sb("top", [P, BATCH])
        ps_x = [pm.ps(f"ps_x{i}", [P, BLK]) for i in range(2)]
        loaded, made, root_in, root_out, x_ok, x_tr, xT_ok, top_in, top_out = map(pm.sem, (
            "loaded", "made", "root_in", "root_out", "x_ok", "x_tr", "xT_ok", "top_in", "top_out"))
        with nc.Block() as block:

            @block.sync
            def _(sp):
                loads = [(w2[:, :, :], A["L1_ffn_w2"].rearrange("(m p) d -> p m d", p=P)),
                         (b2[:, :], A["L1_ffn_b2"].partition_broadcast(P)),
                         (wr[:, :], A["L1_ffn_wr"].rearrange("d o -> (d o)").partition_broadcast(P)),
                         (br[:, :], A["L1_ffn_br"].partition_broadcast(P))]
                loads += [(b1[:, k:k + 1], A["L1_ffn_b1"][k * P:(k + 1) * P].unsqueeze(1)) for k in range(MT)]
                for dst, src in loads:
                    sp.dma_start(dst, src).then_inc(loaded, 16)
                sp.wait_ge(made, 1)
                for k in range(2):
                    sp.dma_start(w1[k * D:(k + 1) * D, k, :], A["L1_ffn_w1"]).then_inc(loaded, 16)
                sp.wait_ge(loaded, 16 * (6 + MT))

            @block.gpsimd
            def _(pool):
                nc.gpsimd.memset(w1[:, :, :], 0.0).then_inc(made, 1)
                pool.wait_ge(made, 1)
                nc.gpsimd.memset(ones[:, :], 1.0).then_inc(made, 1)
                pool.wait_ge(made, 2)
                nc.gpsimd.affine_select(out=after[:, :], in_=ones[:, :], compare_op=ALU.is_gt, fill=0.0,
                                        base=0, pattern=[[-1, P]], channel_multiplier=1).then_inc(made, 1)
                pool.wait_ge(made, 3)
                pool.wait_ge(top_in, 1)
                nc.gpsimd.partition_all_reduce(bound[:, :], top[:, :], P, bass.bass_isa.ReduceOp.max).then_inc(top_out, 1)
                pool.wait_ge(top_out, 1)
                nc.gpsimd.tensor_tensor(resid[:, 0:HALF, :], resid[:, 0:HALF, :], x[:, :, 0, :], ALU.add)
                nc.gpsimd.tensor_tensor(resid[:, HALF:TILES, :], resid[:, HALF:TILES, :], x[:, :, 1, :], ALU.add)

            @block.scalar
            def _(act):
                act.wait_ge(root_in, 1)
                nc.scalar.activation(stat[:, 2], stat[:, 1], ACT.Sqrt).then_inc(root_out, 1)
                for k in range(NBLK):
                    act.wait_ge(x_tr, k + 1)
                    nc.scalar.activation(xT[:, k * BLK:(k + 1) * BLK], ps_x[k % 2][:, :], ACT.Copy).then_inc(xT_ok, 1)

            @block.vector
            def _(dve):
                def root():
                    dve.drain()
                    dve.nop().then_inc(root_in, 1)
                    dve.wait_ge(root_out, 1)

                sq_t = square[:, :, :].rearrange("p (a t) d -> p a t d", a=2)
                layer_norm(nc, dve, x_t, resid[:, :, :].rearrange("p (a t) d -> p a t d", a=2), x_t, sq_t, stat4, LN_EPS, root)
                dve.drain()
                dve.nop().then_inc(x_ok, 1)
                dve.wait_ge(loaded, 16 * (6 + MT))
                for a in range(2):
                    nc.vector.tensor_tensor(sq_t[:, a], x_t[:, a], wr[:, :].unsqueeze(1).broadcast_to([P, HALF, D]), ALU.mult)
                dve.drain()
                nc.vector.tensor_reduce(out=w[:, :], in_=square[:, :, :], axis=AX.X, op=ALU.add)
                dve.drain()
                nc.vector.tensor_scalar(w[:, :], w[:, :], br[:, :], None, ALU.add)
                dve.drain()
                nc.vector.tensor_reduce(out=top[:, :], in_=w[:, :].rearrange("p (b c) -> p b c", c=CHUNKS), axis=AX.X,
                                        op=ALU.max, apply_absolute_value=True)
                dve.drain()
                dve.nop().then_inc(top_in, 1)
                dve.wait_ge(top_out, 1)
                nc.vector.tensor_scalar(bound[:, :], bound[:, :], 1.001, 1e-30, ALU.mult, ALU.add)
                dve.drain()
                nc.vector.tensor_scalar(low[:, :], bound[:, :], -1.0, None, ALU.mult)
                nc.vector.tensor_copy(step[:, :], bound[:, :])

            @block.tensor
            def _(pe):
                pe.wait_ge(x_ok, 1)
                for k in range(NBLK):
                    if k >= 2:
                        pe.wait_ge(xT_ok, k - 1)
                    for j in range(4):
                        last = nc.tensor.transpose(ps_x[k % 2][:, j * P:(j + 1) * P],
                                                   x[:, 4 * k + j, :, :].rearrange("p a d -> p (a d)"), ident[:, :])
                    last.then_inc(x_tr, 1)

    hT = m.sb("hT", [P, 2, MT, BLK])
    mid = m.sb("mid", [P, BATCH])
    least = m.sb("least", [P, TILES])
    over = m.sb("over", [P, TILES])
    n_here = m.sb("n_here", [P, BATCH])
    rise = m.sb("rise", [P, BATCH])
    n_over = m.sb("n_over", [P, BATCH])
    tied = m.sb("tied", [P, TILES])
    rank = m.sb("rank", [P, TILES])
    total = m.sb("total", [P, TILES])
    carry = m.sb("carry", [P, TILES])
    in_row = m.sb("in_row", [P, TILES])
    ps_h = [m.ps(f"ps_h{i}", [P, BLK]) for i in range(2)]
    ps_y = [m.ps(f"ps_y{i}", [P, 4, D]) for i in range(2)]
    ps_n = m.ps("ps_n", [P, BATCH])
    ps_r = m.ps("ps_r", [P, 2, TILES])
    names = ("h_mm", "h_ok", "y_mm", "y_ok", "count_in", "count_mm", "rank_in", "rank_mm")
    S = {n: m.sem(n) for n in names}

    with nc.Block() as block:

        @block.tensor
        def _(pe):
            with pe.Fori(0, NBLK) as k:
                rounds = iter(range(ROUNDS_PER))

                def count():
                    i = next(rounds, None)
                    if i is not None:
                        pe.wait_ge(S["count_in"], k * ROUNDS_PER + i + 1)
                        nc.tensor.matmul(ps_n[:, :], ones[:, :], n_here[:, :], start=True, stop=True).then_inc(S["count_mm"], 1)

                for a in range(2):
                    if a:
                        count()
                    for j in range(MT):
                        pe.wait_ge(S["h_ok"], k * (2 * MT) + a * MT + j + 1)
                        nc.tensor.matmul(ps_h[j][:, :], w1[:, a, j * P:(j + 1) * P], xT[:, bass.ts(k, BLK)],
                                         start=True, stop=True).then_inc(S["h_mm"], 1)
                        count()
                    pe.wait_ge(S["h_ok"], k * (2 * MT) + (a + 1) * MT + MT)
                    pe.wait_ge(S["y_ok"], k * 2 + a + 1)
                    for i in range(4):
                        for j in range(MT):
                            last = nc.tensor.matmul(ps_y[a][:, i, :], hT[:, a, j, i * P:(i + 1) * P], w2[:, j, :],
                                                    start=j == 0, stop=j == MT - 1)
                    last.then_inc(S["y_mm"], 1)
                assert next(rounds, None) is None
            pe.wait_ge(S["count_in"], ROUNDS + 1)
            nc.tensor.matmul(ps_n[:, :], ones[:, :], n_here[:, :], start=True, stop=True).then_inc(S["count_mm"], 1)
            pe.wait_ge(S["rank_in"], 1)
            nc.tensor.matmul(ps_r[:, 0, :], after[:, :], tied[:, :], start=True, stop=True)
            nc.tensor.matmul(ps_r[:, 1, :], ones[:, :], tied[:, :], start=True, stop=True).then_inc(S["rank_mm"], 1)

        @block.scalar
        def _(act):
            def copy_y(k, a):
                act.wait_ge(S["y_mm"], k * 2 + a + 1)
                nc.scalar.activation(y[:, bass.ds(k * 4 + a * HALF, 4), :], ps_y[a][:, :, :], ACT.Copy).then_inc(S["y_ok"], 1)

            act.preload_act_table(ACT.Gelu_apprx_tanh)
            act.nop().then_inc(S["h_ok"], MT)
            act.nop().then_inc(S["y_ok"], 2)
            with act.Fori(0, NBLK) as k:
                for a in range(2):
                    for j in range(MT):
                        act.wait_ge(S["h_mm"], k * (2 * MT) + a * MT + j + 1)
                        nc.scalar.activation(hT[:, a, j, :], ps_h[j][:, :], ACT.Gelu_apprx_tanh, bias=b1[:, j:j + 1]).then_inc(S["h_ok"], 1)
                    if a:
                        copy_y(k, 0)
                copy_y(k, 1)

        @block.vector
        def _(dve):
            w_b = w[:, :].rearrange("p (b c) -> p b c", c=CHUNKS)
            least_b = least[:, :].rearrange("p (b c) -> p b c", c=CHUNKS)
            over_b = over[:, :].rearrange("p (b c) -> p b c", c=CHUNKS)

            def count(marks, bar):
                nc.vector.tensor_tensor(marks, w_b, over_last(bar[:, :], CHUNKS), ALU.is_ge)
                dve.drain()
                nc.vector.tensor_reduce(out=n_here[:, :], in_=marks, axis=AX.X, op=ALU.add)
                dve.drain()
                dve.nop().then_inc(S["count_in"], 1)

            nc.vector.memset(in_row[:, :], 1.0)
            dve.drain()
            nc.vector.memset(in_row[:, :].rearrange("p (b c) -> p b c", c=CHUNKS)[:, :, 0], 0.0)
            with dve.Fori(0, ROUNDS) as r:
                nc.vector.tensor_tensor(mid[:, :], low[:, :], step[:, :], ALU.add)
                dve.drain()
                count(least_b, mid)
                dve.wait_ge(S["count_mm"], r + 1)
                nc.vector.scalar_tensor_tensor(rise[:, :], ps_n[:, :], float(TAKE), step[:, :], ALU.is_ge, ALU.mult)
                dve.drain()
                nc.vector.tensor_tensor(low[:, :], low[:, :], rise[:, :], ALU.add)
                nc.vector.tensor_scalar(step[:, :], step[:, :], 0.5, None, ALU.mult)
                dve.drain()
            nc.vector.scalar_tensor_tensor(mid[:, :], step[:, :], 2.0, low[:, :], ALU.mult, ALU.add)
            nc.vector.tensor_tensor(least_b, w_b, over_last(low[:, :], CHUNKS), ALU.is_ge)
            dve.drain()
            count(over_b, mid)
            nc.vector.tensor_tensor(tied[:, :], least[:, :], over[:, :], ALU.subtract)
            dve.drain()
            dve.nop().then_inc(S["rank_in"], 1)
            dve.wait_ge(S["count_mm"], ROUNDS + 1)
            nc.vector.tensor_scalar(n_over[:, :], ps_n[:, :], -1.0, float(TAKE), ALU.mult, ALU.add)
            dve.wait_ge(S["rank_mm"], 1)
            nc.vector.tensor_copy(total[:, :], ps_r[:, 1, :])
            dve.drain()
            nc.vector.tensor_tensor_scan(carry[:, :], in_row[:, :], total[:, :], 0.0, ALU.mult, ALU.add)
            dve.drain()
            nc.vector.tensor_tensor(carry[:, :], carry[:, :], total[:, :], ALU.subtract)
            dve.drain()
            nc.vector.tensor_tensor(rank[:, :], ps_r[:, 0, :], carry[:, :], ALU.add)
            dve.drain()
            nc.vector.tensor_tensor(rank[:, :].rearrange("p (b c) -> p b c", c=CHUNKS), rank[:, :].rearrange("p (b c) -> p b c", c=CHUNKS),
                                    over_last(n_over[:, :], CHUNKS), ALU.is_lt)
            dve.drain()
            nc.vector.tensor_tensor(tied[:, :], tied[:, :], rank[:, :], ALU.mult)
            dve.drain()
            nc.vector.tensor_tensor(tied[:, :], tied[:, :], over[:, :], ALU.add)
            dve.drain()
            nc.vector.tensor_tensor(w[:, :], w[:, :], tied[:, :], ALU.mult)
            dve.wait_ge(S["y_ok"], 2 * NBLK + 2)
            nc.vector.tensor_tensor(y[:, :, :], y[:, :, :], b2[:, :].unsqueeze(1).broadcast_to([P, TILES, D]), ALU.add)
            dve.drain()
            nc.vector.tensor_tensor(y[:, :, :], y[:, :, :], over_last(w[:, :], D), ALU.mult)
            dve.drain()
            nc.vector.tensor_tensor(resid[:, :, :], resid[:, :, :], y[:, :, :], ALU.add)


def store_result(nc, m, resid, flip, out):
    PER = 512 // D
    N = TILES // PER
    turned = m.sb("turned", [P, TILES, D])
    ps = [m.ps(f"ps{i}", [P, PER, D]) for i in range(4)]
    flipped, copied, stored = m.sem("flipped"), m.sem("copied"), m.sem("stored")
    out_v = out.rearrange("b (c p) d -> p (b c) d", p=P)
    with nc.Block() as block:

        @block.tensor
        def _(pe):
            for k in range(N):
                if k >= 4:
                    pe.wait_ge(copied, k - 3)
                nc.tensor.matmul(ps[k % 4][:, :, :], flip[:, :], resid[:, k * PER:(k + 1) * PER, :],
                                 start=True, stop=True).then_inc(flipped, 1)

        @block.vector
        def _(dve):
            for k in range(N):
                dve.wait_ge(flipped, k + 1)
                nc.vector.tensor_copy(turned[:, k * PER:(k + 1) * PER, :], ps[k % 4][:, :, :]).then_inc(copied, 1)

        @block.sync
        def _(sp):
            for k in range(N):
                sp.wait_ge(copied, k + 1)
                sp.dma_start(out_v[:, k * PER:(k + 1) * PER, :], turned[:, k * PER:(k + 1) * PER, :]).then_inc(stored, 16)
            sp.wait_ge(stored, 16 * N)


def tower(nc, A, out, phases=5):
    with ExitStack() as whole:
        shared = Memory(nc, whole, "all")
        resid = shared.sb("resid", [P, TILES, D])
        ident, flip = constants(nc, shared)
        todo = [embed_tokens, state_space_layers, expert_mixture, sigmoid_attention, routed_mlp][:phases]
        for phase in todo:
            with ExitStack() as stack:
                phase(nc, Memory(nc, stack, phase.__name__), A, resid, ident, flip)
        with ExitStack() as stack:
            store_result(nc, Memory(nc, stack, "end"), resid, flip, out)


def kernel(**inputs):
    import concourse.bacc as bacc
    import numpy as np
    from concourse.bass_utils import run_bass_kernel_spmd

    nc = bacc.Bacc("TRN2", target_bir_lowering=False, num_devices=1)
    arrays, args = {}, {}
    given = {k: np.ascontiguousarray(v) for k, v in inputs.items()}
    tables = ["L0_tok_emb_table", "L0_tok_geo_table", "L0_tok_visit_table"]
    given["rows"] = np.concatenate([given.pop(t) for t in tables], axis=1)
    for name, a in given.items():
        arrays[f"in_{name}"] = a
        args[name] = nc.dram_tensor(f"in_{name}", a.shape, mybir.dt.from_np(a.dtype), kind="ExternalInput").ap()
    out = nc.dram_tensor("out_h", (BATCH, SEQ, D), F32, kind="ExternalOutput").ap()
    tower(nc, args, out)
    r = run_bass_kernel_spmd(nc, [arrays], core_ids=[0])
    return r.results[0]["out_h"]
```

```python
from contextlib import ExitStack

import concourse.bass as bass
from concourse import mybir

F32 = mybir.dt.float32
F16 = mybir.dt.float16
BF16 = mybir.dt.bfloat16
I32 = mybir.dt.int32
ACT = mybir.ActivationFunctionType
ALU = mybir.AluOpType
AX = mybir.AxisListType

P = 128
BATCH, SEQ, D = 4, 2048, 64
CHUNKS = SEQ // P
TILES = BATCH * CHUNKS
VISIT = 24
ROW = D + D + VISIT
LAST_ID = 25000
LN_EPS = 1e-5


class Memory:

    def __init__(self, nc, stack, name):
        self.nc, self.stack, self.name = nc, stack, name

    def sb(self, name, shape, dt=F32):
        return self.stack.enter_context(self.nc.sbuf_tensor(f"{self.name}_{name}", shape, dt))

    def ps(self, name, shape, dt=F32):
        return self.stack.enter_context(self.nc.psum_tensor(f"{self.name}_{name}", shape, dt))

    def sem(self, name):
        return self.stack.enter_context(self.nc.semaphore(f"{self.name}_{name}"))


def over_last(ap, n):
    return ap.unsqueeze(len(ap.shape)).broadcast_to(list(ap.shape) + [n])


def layer_norm(nc, e, out, x, centred, square, stat, eps, scaled=None):
    n = x.shape[-1]
    nc.vector.tensor_reduce(out=stat[:, 0], in_=x, axis=AX.X, op=ALU.add)
    e.drain()
    nc.vector.tensor_scalar(stat[:, 0], stat[:, 0], 1.0 / n, None, ALU.mult)
    e.drain()
    nc.vector.tensor_tensor(centred, x, over_last(stat[:, 0], n), ALU.subtract)
    e.drain()
    nc.vector.tensor_tensor(square, centred, centred, ALU.mult)
    e.drain()
    nc.vector.tensor_reduce(out=stat[:, 1], in_=square, axis=AX.X, op=ALU.add)
    e.drain()
    nc.vector.tensor_scalar(stat[:, 1], stat[:, 1], 1.0 / n, eps, ALU.mult, ALU.add)
    scaled()
    nc.vector.reciprocal(stat[:, 0], stat[:, 2])
    e.drain()
    nc.vector.tensor_tensor(out, centred, over_last(stat[:, 0], n), ALU.mult)


def constants(nc, m):
    ident = m.sb("ident", [P, P])
    flip = m.sb("flip", [P, P])
    made = m.sem("ident_made")
    with nc.Block() as block:

        @block.gpsimd
        def _(pool):
            nc.gpsimd.memset(ident[:, :], 0.0).then_inc(made, 1)
            pool.wait_ge(made, 1)
            nc.gpsimd.affine_select(out=ident[:, :], in_=ident[:, :], compare_op=ALU.not_equal, fill=1.0,
                                    base=0, pattern=[[-1, P]], channel_multiplier=1).then_inc(made, 1)
            pool.wait_ge(made, 2)
            nc.gpsimd.memset(flip[:, :], 0.0).then_inc(made, 1)
            pool.wait_ge(made, 3)
            nc.gpsimd.affine_select(out=flip[:, :], in_=flip[:, :], compare_op=ALU.not_equal, fill=1.0,
                                    base=1 - P, pattern=[[1, P]], channel_multiplier=1).then_inc(made, 1)
            pool.wait_ge(made, 4)
    return ident, flip


def embed_tokens(nc, m, A, resid, ident, flip):
    GROUP = 4
    RING = 4
    NG = TILES // GROUP
    GT = GROUP * P

    ids = m.sb("ids", [TILES, P], I32)
    idf = m.sb("idf", [TILES, 2, P])
    index = m.sb("index", [P, TILES], I32)
    keep = m.sb("keep", [P, TILES])
    rows = m.sb("rows", [P, RING * GROUP, ROW])
    w_ig = m.sb("w_ig", [P, P])
    w_v = m.sb("w_v", [VISIT, D])
    w_f1 = m.sb("w_f1", [P, D])
    w_f2 = m.sb("w_f2", [D + 1, D])
    b_ig = m.sb("b_ig", [P, 1])
    b_v = m.sb("b_v", [D, 1])
    gamma = m.sb("gamma", [P, D])
    beta = m.sb("beta", [P, D])
    featT = m.sb("featT", [P, 2, GT])
    visitT = m.sb("visitT", [VISIT, 2, GT])
    hidT = m.sb("hidT", [P, 2, GT])
    hidvT = m.sb("hidvT", [D + 1, 2, GT])
    fused = m.sb("fused", [P, TILES, D])
    centred = m.sb("centred", [P, TILES, D])
    square = m.sb("square", [P, TILES, D])
    stat = m.sb("stat", [P, 3, TILES])
    ps_ids = m.ps("ps_ids", [P, 2, TILES])
    ps_feat = m.ps("ps_feat", [P, GT])
    ps_visit = m.ps("ps_visit", [VISIT, GT])
    ps_h = [m.ps(f"ps_h{i}", [P, GT]) for i in range(1)]
    ps_hv = [m.ps(f"ps_hv{i}", [D, GT]) for i in range(1)]
    ps_f = [m.ps(f"ps_f{i}", [P, GROUP, D]) for i in range(2)]

    zeroed, loaded, ids_in, clipped, ids_tr, index_ok = map(m.sem, ("zeroed", "loaded", "ids_in", "clipped", "ids_tr", "index_ok"))
    gathered = [m.sem(f"gathered{r}") for r in range(RING)]
    rows_used, feat_tr, feat_sb, proj, hid_ok, fuse_mm, fuse_ok, emb_ok, root_in, root_out = map(m.sem, (
        "rows_used", "feat_tr", "feat_sb", "proj", "hid_ok", "fuse_mm", "fuse_ok", "emb_ok", "root_in", "root_out"))
    N_LOADS = 11

    with nc.Block() as block:

        @block.sync
        def _(sp):
            sp.dma_start(ids[:, :], A["x"].rearrange("b (c p) -> (b c) p", p=P)).then_inc(ids_in, 16)
            sp.wait_ge(zeroed, 1)
            for dst, src in ((w_ig[0:D, 0:D], A["L0_tok_w_item"]), (w_ig[D:P, D:P], A["L0_tok_w_geo"]),
                             (w_v[:, :], A["L0_tok_w_visit"]),
                             (w_f1[:, :], A["L0_tok_w_fuse"][0:P, :]), (w_f2[0:D, :], A["L0_tok_w_fuse"][P:P + D, :]),
                             (w_f2[D:D + 1, :], A["L0_tok_b_fuse"].unsqueeze(0)),
                             (b_ig[0:D, :], A["L0_tok_b_item"].unsqueeze(1)), (b_ig[D:P, :], A["L0_tok_b_geo"].unsqueeze(1)),
                             (b_v[:, :], A["L0_tok_b_visit"].unsqueeze(1)),
                             (gamma[:, :], A["L0_tok_ln_gamma"].partition_broadcast(P)),
                             (beta[:, :], A["L0_tok_ln_beta"].partition_broadcast(P))):
                sp.dma_start(dst, src).then_inc(loaded, 16)

        @block.gpsimd
        def _(pool):
            nc.gpsimd.memset(w_ig[:, :], 0.0).then_inc(zeroed, 1)
            pool.wait_ge(zeroed, 1)
            nc.gpsimd.memset(hidvT[D:D + 1, :, :], 1.0).then_inc(zeroed, 1)
            pool.wait_ge(zeroed, 2)
            pool.wait_ge(index_ok, 1)
            for t in range(TILES):
                g, r = t // GROUP, t // GROUP % RING
                if t % GROUP == 0 and g >= RING:
                    pool.wait_ge(rows_used, 2 * (g - RING + 1))
                nc.gpsimd.indirect_dma_start(
                    out=rows[:, t % (RING * GROUP), :], out_offset=None, in_=A["rows"],
                    in_offset=bass.IndirectOffsetOnAxis(ap=index[:, t:t + 1], axis=0)).then_inc(gathered[r], 16)

        @block.tensor
        def _(pe):
            pe.wait_ge(clipped, 1)
            nc.tensor.transpose(ps_ids[:, 0, :], idf[:, 0, :], ident[0:TILES, 0:TILES])
            nc.tensor.transpose(ps_ids[:, 1, :], idf[:, 1, :], ident[0:TILES, 0:TILES]).then_inc(ids_tr, 1)
            pe.wait_ge(loaded, 16 * N_LOADS)
            pe.wait_ge(zeroed, 2)
            with pe.Fori(0, NG // RING) as it:
                for r in range(RING):
                    g = it * RING + r
                    pe.wait_ge(gathered[r], it * 16 * GROUP + 16 * GROUP)
                    for k in range(GROUP):
                        row = rows[:, r * GROUP + k, :]
                        nc.tensor.transpose(ps_feat[:, k * P:(k + 1) * P], row[:, 0:P], ident[:, :])
                    for k in range(GROUP):
                        row = rows[:, r * GROUP + k, :]
                        last = nc.tensor.transpose(ps_visit[:, k * P:(k + 1) * P], row[:, P:ROW], ident[:, :])
                    last.then_inc(feat_tr, 1)
                    pe.wait_ge(feat_sb, 2 * g + 2)
                    nc.tensor.matmul(ps_h[0][:, :], w_ig[:, :], featT[:, r % 2, :], start=True, stop=True)
                    nc.tensor.matmul(ps_hv[0][:, :], w_v[:, :], visitT[:, r % 2, :], start=True, stop=True).then_inc(proj, 1)
                    pe.wait_ge(hid_ok, g + 1)
                    for k in range(GROUP):
                        tok = slice(k * P, (k + 1) * P)
                        nc.tensor.matmul(ps_f[r % 2][:, k, :], hidT[:, r % 2, tok], w_f1[:, :], start=True, stop=False)
                        last = nc.tensor.matmul(ps_f[r % 2][:, k, :], hidvT[:, r % 2, tok], w_f2[:, :], start=False, stop=True)
                    last.then_inc(fuse_mm, 1)

        @block.scalar
        def _(act):
            act.wait_ge(loaded, 16 * N_LOADS)
            with act.Fori(0, NG // RING) as it:
                for r in range(RING):
                    g = it * RING + r
                    act.wait_ge(feat_tr, g + 1)
                    nc.scalar.activation(visitT[:, r % 2, :], ps_visit[:, :], ACT.Copy).then_inc(feat_sb, 1)
                    act.wait_ge(proj, g + 1)
                    nc.scalar.activation(hidT[:, r % 2, :], ps_h[0][:, :], ACT.Gelu, bias=b_ig[:, :])
                    nc.scalar.activation(hidvT[0:D, r % 2, :], ps_hv[0][:, :], ACT.Gelu, bias=b_v[:, :]).then_inc(hid_ok, 1)
                    act.wait_ge(fuse_mm, g + 1)
                    nc.scalar.activation(fused[:, bass.ts(g, GROUP), :], ps_f[r % 2][:, :, :], ACT.Gelu).then_inc(fuse_ok, 1)
            act.wait_ge(root_in, 1)
            nc.scalar.activation(stat[:, 2], stat[:, 1], ACT.Sqrt).then_inc(root_out, 1)

        @block.vector
        def _(dve):
            dve.wait_ge(ids_in, 16)
            nc.vector.tensor_scalar(idf[:, 0, :], ids[:, ::-1], 0.0, float(LAST_ID), ALU.max, ALU.min)
            nc.vector.tensor_scalar(idf[:, 1, :], ids[:, ::-1], 0.0, None, ALU.not_equal)
            dve.drain()
            dve.nop().then_inc(clipped, 1)
            dve.wait_ge(ids_tr, 1)
            nc.vector.tensor_copy(index[:, :], ps_ids[:, 0, :]).then_inc(index_ok, 1)
            nc.vector.tensor_copy(keep[:, :], ps_ids[:, 1, :])
            with dve.Fori(0, NG // RING) as it:
                for r in range(RING):
                    g = it * RING + r
                    dve.wait_ge(feat_tr, g + 1)
                    nc.vector.tensor_copy(resid[:, bass.ts(g, GROUP), :], rows[:, r * GROUP:(r + 1) * GROUP, 0:D]).then_inc(rows_used, 1)
                    nc.vector.tensor_copy(featT[:, r % 2, :], ps_feat[:, :]).then_inc(feat_sb, 1)
                    dve.nop().then_inc(rows_used, 1)
            dve.wait_ge(fuse_ok, NG)

            def root():
                dve.drain()
                dve.nop().then_inc(root_in, 1)
                dve.wait_ge(root_out, 1)

            layer_norm(nc, dve, fused[:, :, :], fused[:, :, :], centred[:, :, :], square[:, :, :], stat, LN_EPS, root)
            dve.drain()
            nc.vector.tensor_tensor(fused[:, :, :], fused[:, :, :], gamma[:, :].unsqueeze(1).broadcast_to([P, TILES, D]), ALU.mult)
            dve.drain()
            nc.vector.tensor_tensor(fused[:, :, :], fused[:, :, :], beta[:, :].unsqueeze(1).broadcast_to([P, TILES, D]), ALU.add)
            dve.drain()
            nc.vector.tensor_tensor(fused[:, :, :], fused[:, :, :], over_last(keep[:, :], D), ALU.mult)
            dve.drain()
            nc.vector.scalar_tensor_tensor(resid[:, :, :], fused[:, :, :], 0.1, resid[:, :, :], ALU.mult, ALU.add)


def state_space_layers(nc, m, A, resid, ident, flip):
    LAYERS = 4
    PAIRS = D // 2
    HALF = PAIRS // 2
    GP = 4
    GROUPS = PAIRS // GP
    TURNED = 4
    HCOLS = HALF * P
    MAGIC = 1.5 * 2 ** 23
    TURN = 6.2831845
    QUARTER = TURN / 4

    hs = m.sb("hs", [P, TILES, D])
    u = m.sb("u", [P, D, TILES])
    y = m.sb("y", [P, TILES, D])
    angle_c = m.sb("angle_c", [P, 2, HCOLS])
    decay_c = m.sb("decay_c", [P, HCOLS])
    turned = m.sb("turned", [P, TURNED, 2, GP, P])
    powers = m.sb("powers", [P, 2, PAIRS, 2, P])
    toep = m.sb("toep", [P, 2, 2 * GP, P])
    state = resid[:, :, :].rearrange("p t d -> p (t d)").rearrange("p (q r t) -> p q r t", q=PAIRS, r=2)
    padded = m.sb("padded", [P, 2, GP, 2, 2, TILES])
    cols = m.sb("cols", [P, 4, LAYERS, PAIRS])
    cdz = m.sb("cdz", [P, PAIRS, 2, 2])
    cds = m.sb("cds", [P, PAIRS, 2])
    cdw = m.sb("cdw", [P, 2, PAIRS])
    part = m.sb("part", [P, 8, PAIRS])
    w128 = m.sb("w128", [P, 2, PAIRS])
    wr = m.sb("wr", [P, PAIRS, 2, BATCH])
    ws = m.sb("ws", [P, PAIRS, 2, BATCH])
    s1 = m.sb("s1", [P, PAIRS, 2, BATCH])
    s2 = m.sb("s2", [P, PAIRS, 2, BATCH])
    rot = m.sb("rot", [P, GP, 2, TILES])
    stat = m.sb("stat", [P, 3, TILES])
    kk = m.sb("kk", [P, P])
    quarter = m.sb("quarter", [P, 1])
    scale_bc = m.sb("scale_bc", [P, D])
    bias_bc = m.sb("bias_bc", [P, D])
    kt = m.sb("kt", [P, P])
    krow = m.sb("krow", [D, P])
    zrow = m.sb("zrow", [P, 2, P])
    k0 = m.sb("k0", [P, 2])
    wout = m.sb("wout", [P, 2 * P])
    w_in = m.sb("w_in", [P, 2 * D])
    brow = m.sb("brow", [P, P])
    b_part = m.sb("b_part", [P, P], BF16)
    bias_parts = m.sb("bias_parts", [P, GP * P], BF16)
    ones = m.sb("ones", [P, P], BF16)
    yT = m.sb("yT", [P, 2, GP * P // 2])
    gate = m.sb("gate", [P, 2, GP, D])
    zz = rot[:, :, :, :].rearrange("p q r t -> p (q r t)").rearrange("p (s t d) -> p s t d", s=2, d=D)
    dram_resid = nc.dram_tensor("parked_resid", (P, TILES, D), F32).ap()
    dram_k = nc.dram_tensor("kernel_rows", (LAYERS, D, 2 * P), F32)
    k_ap = dram_k.ap()

    with ExitStack() as prep_stack:
        pm = Memory(nc, prep_stack, "prep")
        N2 = 2 * D

        names = ["alog", "aim", "cre", "cim", "x", "f", "r", "q1", "sn", "cs", "sh", "th", "zr", "zi", "den", "ta", "tb",
                 "qr", "qi", "cdr", "cdi", "ar"] + [f"twice{i}" for i in range(8)]
        slots = {n: angle_c[:, :, :].rearrange("p a b -> p (a b)")[:, i * N2:(i + 1) * N2] for i, n in enumerate(names)}

        def v3(n):
            return slots[n].rearrange("p (l n) -> p l n", n=D)

        ldt = pm.sb("ldt", [P, 2])
        dt = pm.sb("dt", [P, 2])
        dskip = pm.sb("dskip", [P, 2])
        ps_q = pm.ps("ps_q", [P, 4, P])
        loaded, made, zero, trig_in, trig_out, ready, tr_done, tr_read, parked = map(pm.sem, (
            "loaded", "made", "zero", "trig_in", "trig_out", "ready", "tr_done", "tr_read", "parked"))
        with nc.Block() as block:

            @block.sync
            def _(sp):
                for n, src in (("alog", "Alog"), ("aim", "Aim"), ("cre", "Cre"), ("cim", "Cim")):
                    sp.dma_start(v3(n), A["L0_attn_" + src].rearrange("(l k) h n -> (k h) l n", k=2)).then_inc(loaded, 16)
                for dst, src in ((ldt, "log_dt"), (dskip, "D")):
                    for i in range(2):
                        sp.dma_start(dst[:, i:i + 1], A["L0_attn_" + src][2 * i:2 * i + 2, :].rearrange("k h -> (k h)").unsqueeze(1)).then_inc(loaded, 16)
                sp.dma_start(dram_resid, resid[:, :, :]).then_inc(parked, 16)
                sp.wait_ge(zero, 1)
                sp.dma_start(k_ap.rearrange("(l k) h x -> (k h) l x", k=2)[:, :, 1:P + 1], zrow[:, :, :]).then_inc(parked, 16)
                sp.wait_ge(parked, 32)

            @block.gpsimd
            def _(pool):
                nc.gpsimd.iota(kk[:, :], pattern=[[1, P]], base=0, channel_multiplier=0,
                               allow_small_or_imprecise_dtypes=True).then_inc(made, 1)
                pool.wait_ge(made, 1)
                for i, (buf, val) in enumerate(((quarter[:, :], QUARTER), (ones[:, :], 1.0), (wout[:, :], 0.0),
                                                (cdz[:, :, :, :], 0.0), (bias_parts[:, :], 0.0), (kt[:, :], 0.0), (padded[:, :, :, :, :, :], 0.0))):
                    nc.gpsimd.memset(buf, val).then_inc(made, 1)
                    pool.wait_ge(made, 2 + i)

            @block.scalar
            def _(act):
                act.wait_ge(loaded, 128)
                nc.scalar.activation(dt[:, :], ldt[:, :], ACT.Exp)
                nc.scalar.activation(slots["ar"], slots["alog"], ACT.Exp).then_inc(trig_out, 1)
                act.wait_ge(trig_in, 1)
                nc.scalar.activation(slots["th"], slots["x"], ACT.Tanh, scale=0.5)
                nc.scalar.activation(slots["q1"], slots["r"], ACT.Abs)
                act.drain()
                act.wait_ge(made, 2)
                nc.scalar.activation(slots["cs"], slots["q1"], ACT.Sin, scale=-TURN, bias=quarter[:, :])
                nc.scalar.activation(slots["sn"], slots["r"], ACT.Sin, scale=TURN)
                nc.scalar.activation(slots["sh"], slots["r"], ACT.Sin, scale=TURN / 2)
                act.drain()
                act.nop().then_inc(trig_out, 1)

            @block.vector
            def _(dve):
                def tt(o, a, b, op):
                    nc.vector.tensor_tensor(slots[o], slots[a], slots[b], op)
                    dve.drain()

                def ts(o, a, c0, c1, op0, op1=None):
                    if op1 is None:
                        nc.vector.tensor_scalar(slots[o], slots[a], c0, c1, op0)
                    else:
                        nc.vector.tensor_scalar(slots[o], slots[a], c0, c1, op0, op1)
                    dve.drain()

                dve.wait_ge(loaded, 128)
                dve.wait_ge(trig_out, 1)
                ts("ar", "ar", -1.0, None, ALU.mult)
                nc.vector.tensor_tensor(v3("x"), v3("ar"), over_last(dt[:, :], D), ALU.mult)
                nc.vector.tensor_tensor(v3("f"), v3("aim"), over_last(dt[:, :], D), ALU.mult)
                dve.drain()
                ts("f", "f", 1.0 / 6.283185307179586, None, ALU.mult)
                ts("ta", "f", MAGIC, MAGIC, ALU.add, ALU.subtract)
                tt("r", "f", "ta", ALU.subtract)
                dve.nop().then_inc(trig_in, 1)
                tt("den", "ar", "ar", ALU.mult)
                tt("ta", "aim", "aim", ALU.mult)
                tt("den", "den", "ta", ALU.add)
                nc.vector.reciprocal(slots["den"], slots["den"])
                dve.drain()
                dve.wait_ge(trig_out, 2)
                ts("ta", "th", -1.0, 1.0, ALU.mult, ALU.add)
                nc.vector.reciprocal(slots["ta"], slots["ta"])
                dve.drain()
                tt("th", "th", "ta", ALU.mult)
                ts("th", "th", 2.0, None, ALU.mult)
                tt("zr", "th", "cs", ALU.mult)
                tt("sh", "sh", "sh", ALU.mult)
                nc.vector.scalar_tensor_tensor(slots["zr"], slots["sh"], -2.0, slots["zr"], ALU.mult, ALU.add)
                nc.vector.scalar_tensor_tensor(slots["zi"], slots["th"], 1.0, slots["sn"], ALU.add, ALU.mult)
                dve.drain()

                def complex_mul(orr, oi, ar_, ai, br, bi, conj):
                    tt("ta", ar_, br, ALU.mult)
                    tt("tb", ai, bi, ALU.mult)
                    tt(orr, "ta", "tb", ALU.add if conj else ALU.subtract)
                    tt("ta", ai, br, ALU.mult)
                    tt("tb", ar_, bi, ALU.mult)
                    tt(oi, "ta", "tb", ALU.subtract if conj else ALU.add)

                complex_mul("qr", "qi", "zr", "zi", "ar", "aim", True)
                tt("qr", "qr", "den", ALU.mult)
                tt("qi", "qi", "den", ALU.mult)
                complex_mul("cdr", "cdi", "cre", "cim", "qr", "qi", False)
                ts("cdr", "cdr", 2.0, None, ALU.mult)
                ts("cdi", "cdi", 2.0, None, ALU.mult)
                nc.vector.tensor_reduce(out=k0[:, :], in_=v3("cdr"), axis=AX.X, op=ALU.add)
                nc.vector.memset(zrow[:, :, :], 0.0)
                dve.drain()
                nc.vector.tensor_tensor(zrow[:, :, P - 1], k0[:, :], dskip[:, :], ALU.add)
                dve.drain()
                dve.nop().then_inc(zero, 1)
                for i, n in enumerate(("f", "x", "cdr", "cdi")):
                    for half in range(2):
                        nc.vector.tensor_copy(v3(f"twice{2 * i + half}"), v3(n)[:, half, :].unsqueeze(1).broadcast_to([P, 2, D]))
                dve.drain()
                dve.nop().then_inc(ready, 1)
                for half in range(2):
                    dve.wait_ge(tr_done, half + 1)
                    for par in range(2):
                        side = slice(par * D, (par + 1) * D)
                        for k in range(2):
                            nc.vector.tensor_copy(cols[side, :, 2 * half + k, :],
                                                  ps_q[side, :, k * D + par:(k + 1) * D:2])
                    dve.drain()
                    dve.nop().then_inc(tr_read, 1)

            @block.tensor
            def _(pe):
                pe.wait_ge(ready, 1)
                for half in range(2):
                    if half:
                        pe.wait_ge(tr_read, half)
                    for i in range(4):
                        last = nc.tensor.transpose(ps_q[:, i, :], slots[f"twice{2 * i + half}"], ident[:, :])
                    last.then_inc(tr_done, 1)

    ps_s = [m.ps(f"ps_s{i}", [P, GP, 2, TILES]) for i in range(2)]
    ps_k = m.ps("ps_k", [P, D + P])
    ps_y = [m.ps(f"ps_y{i}", [P, 2 * GP, TILES]) for i in range(2)]
    ps_t = m.ps("ps_t", [P, GP * P // 2])
    ps_z = [m.ps(f"ps_z{i}", [P, GP, P]) for i in range(2)]
    names = ("params", "wout_t", "wout_ok", "root_in", "root_out", "u_ok", "reduced", "trig", "powers_ok",
             "powers_used", "turn_mm", "turn_ok", "small_ok", "k_mm", "k_sb", "k_turned", "k_row", "k_out", "t0_used", "s_mm",
             "s_read", "scanned", "pad_ok", "y_mm", "y_ok", "yt_mm", "yt_ok", "z_mm", "gate_ok", "z_read",
             "layer_done", "y_read")
    S = {n: m.sem(n) for n in names}
    t0_in = [m.sem(f"t0_in{i}") for i in range(2)]
    NPARAM = 5
    BLOCKS = TILES // GP

    with nc.Block() as block:

        @block.sync
        def _(sp):
            with sp.Fori(0, LAYERS) as l:
                k_base = sp.snap(l * (D * 2 * P))
                sp.wait_ge(S["layer_done"], l + 1)
                sp.dma_start(scale_bc[:, :], A["L0_attn_ln_scale"][bass.ds(l, 1), :].partition_broadcast(P).squeeze(1)).then_inc(S["params"], 16)
                sp.dma_start(bias_bc[:, :], A["L0_attn_ln_bias"][bass.ds(l, 1), :].partition_broadcast(P).squeeze(1)).then_inc(S["params"], 16)
                sp.dma_start(brow[:, :], A["L0_attn_bout"][bass.ds(l, 1), :].partition_broadcast(P).squeeze(1)).then_inc(S["params"], 16)
                for k in range(2):
                    sp.dma_start(w_in[:, k * D:(k + 1) * D], A["L0_attn_Wout"][bass.ds(l, 1), :, :].squeeze(0)).then_inc(S["params"], 16)
                sp.wait_ge(S["k_row"], l + 1)
                sp.dma_start(k_ap[bass.ds(l, 1), :, P + 1:2 * P].squeeze(0), krow[:, 1:P]).then_inc(S["k_out"], 16)
                sp.wait_ge(S["k_out"], 16 * l + 16)
                for g in range(GROUPS):
                    if g >= 2:
                        sp.wait_ge(S["t0_used"], l * GROUPS + g - 1)
                    src = bass.AP(tensor=dram_k, offset=k_base + 1 + g * 2 * GP * 2 * P, ap=[[1, P], [2 * P, 2 * GP], [1, P]])
                    sp.dma_start(toep[:, g % 2, :, :], src).then_inc(t0_in[g % 2], 16)

        @block.gpsimd
        def _(pool):
            def make(l, parity, done):
                for half in range(2):
                    pairs = slice(half * HALF, (half + 1) * HALF)
                    turns = angle_c[:, 0, :].rearrange("p (q i) -> p q i", i=P)
                    other = angle_c[:, 1, :].rearrange("p (q i) -> p q i", i=P)
                    decay = decay_c[:, :].rearrange("p (q i) -> p q i", i=P)
                    k3 = kk[:, :].unsqueeze(1).broadcast_to([P, HALF, P])
                    if isinstance(l, int):
                        f, a = [cols[:, i, l, pairs] for i in range(2)]
                    else:
                        f, a = [cols[:, i, bass.ds(l, 1), pairs].squeeze(1) for i in range(2)]
                    nc.gpsimd.tensor_tensor(turns, k3, over_last(f, P), ALU.mult)
                    nc.gpsimd.tensor_tensor(decay, k3, over_last(a, P), ALU.mult)
                    pool.drain()
                    nc.gpsimd.tensor_scalar(other, turns, MAGIC, MAGIC, ALU.add, ALU.subtract)
                    pool.drain()
                    nc.gpsimd.tensor_tensor(turns, turns, other, ALU.subtract)
                    pool.drain()
                    pool.nop().then_inc(S["reduced"], 1)
                    pool.wait_ge(S["trig"], done + half + 1)
                    nc.gpsimd.tensor_tensor(powers[:, parity, pairs, 0, :], decay, other, ALU.mult)
                    nc.gpsimd.tensor_tensor(powers[:, parity, pairs, 1, :], decay, turns, ALU.mult)
                    pool.drain()
                    pool.nop().then_inc(S["powers_ok"], 1)

            make(0, 0, 0)
            with pool.Fori(0, LAYERS // 2) as ll:
                for parity in range(2):
                    l = ll * 2 + parity
                    pool.wait_ge(S["powers_used"], l + 1)
                    make(l + 1 if parity == 0 else (ll * 2 + 2) % LAYERS, 1 - parity, 2 * l + 2)

        @block.scalar
        def _(act):
            def gelu(l, g):
                act.wait_ge(S["y_mm"], l * GROUPS + g + 1)
                dst = y[:, :, g * 2 * GP:(g + 1) * 2 * GP].rearrange("p t h -> p h t")
                nc.scalar.activation(dst, ps_y[g % 2][:, :, :], ACT.Gelu_apprx_tanh).then_inc(S["y_read"], 1)

            def angles(done):
                act.wait_ge(S["reduced"], done + 1)
                nc.scalar.activation(angle_c[:, 1, :], angle_c[:, 0, :], ACT.Abs)
                act.drain()
                nc.scalar.activation(angle_c[:, 1, :], angle_c[:, 1, :], ACT.Sin, scale=-TURN, bias=quarter[:, :])
                nc.scalar.activation(angle_c[:, 0, :], angle_c[:, 0, :], ACT.Sin, scale=-TURN)
                nc.scalar.activation(decay_c[:, :], decay_c[:, :], ACT.Exp)
                act.drain()
                act.nop().then_inc(S["trig"], 1)

            def turn(l, g):
                if g >= TURNED:
                    act.wait_ge(S["s_mm"], l * GROUPS + g - TURNED + 1)
                act.wait_ge(S["turn_mm"], l * GROUPS + g + 1)
                for ri in range(2):
                    last = nc.scalar.activation(turned[:, g % TURNED, ri, :, :].rearrange("p q n -> p (q n)"),
                                                ps_z[ri][:, :, :].rearrange("p q n -> p (q n)"), ACT.Copy, scale=(1.0, -1.0)[ri])
                last.then_inc(S["turn_ok"], 1)

            act.wait_ge(S["root_in"], 1)
            nc.scalar.activation(stat[:, 2], stat[:, 1], ACT.Sqrt).then_inc(S["root_out"], 1)
            for half in range(2):
                angles(half)
            with act.Fori(0, LAYERS) as l:
                act.wait_ge(S["root_in"], l + 2)
                nc.scalar.activation(stat[:, 2], stat[:, 1], ACT.Sqrt).then_inc(S["root_out"], 1)
                for g in range(TURNED):
                    turn(l, g)
                act.wait_ge(S["wout_t"], l + 1)
                nc.scalar.activation(wout[0:D, 0:P], ps_k[0:D, 0:P], ACT.Copy)
                nc.scalar.activation(wout[D:P, P:2 * P], ps_k[D:P, 0:P], ACT.Copy).then_inc(S["wout_ok"], 1)
                for g in range(TURNED, GROUPS):
                    turn(l, g)
                act.wait_ge(S["k_mm"], l + 1)
                nc.scalar.activation(kt[:, 0:D], ps_k[:, 0:D], ACT.Copy).then_inc(S["k_sb"], 1)
                act.wait_ge(S["k_turned"], l + 1)
                nc.scalar.activation(krow[:, :], ps_k[0:D, D:D + P], ACT.Copy).then_inc(S["k_row"], 1)
                angles(2 * l + 2)
                for g in range(GROUPS):
                    if g % (GROUPS // 2) == 0:
                        act.wait_ge(S["scanned"], 2 * l + 1 + g // (GROUPS // 2))
                    if g >= 2:
                        act.wait_ge(S["y_mm"], l * GROUPS + g - 1)
                    for par in range(2):
                        side = slice(par * D, (par + 1) * D)
                        for ri in range(2):
                            dst = padded[side, g % 2, :, ri, par, :].rearrange("p q (b c) -> p q b c", c=CHUNKS)
                            src = state[side, g * GP:(g + 1) * GP, ri, :].rearrange("p q (b c) -> p q b c", c=CHUNKS)
                            nc.scalar.activation(dst[:, :, :, 1:CHUNKS], src[:, :, :, 0:CHUNKS - 1], ACT.Copy)
                    act.drain()
                    act.nop().then_inc(S["pad_ok"], 1)
                    if g >= 1:
                        gelu(l, g - 1)
                gelu(l, GROUPS - 1)
                act.drain()
                act.nop().then_inc(S["y_ok"], 1)
                for k in range(BLOCKS + 1):
                    if k < BLOCKS:
                        act.wait_ge(S["yt_mm"], l * BLOCKS + k + 1)
                        nc.scalar.activation(yT[:, k % 2, :].rearrange("p (j i) -> p j i", i=P),
                                             ps_t[:, :].rearrange("p (j i) -> p j i", i=P)[:, :, ::-1], ACT.Copy).then_inc(S["yt_ok"], 1)
                    if k >= 1:
                        j = k - 1
                        act.wait_ge(S["z_mm"], l * BLOCKS + j + 1)
                        if j >= 2:
                            act.wait_ge(S["z_read"], l * BLOCKS + j)
                        nc.scalar.activation(gate[:, j % 2, :, :], ps_z[j % 2][:, :, D:P], ACT.Sigmoid).then_inc(S["gate_ok"], 1)
                angles(2 * l + 3)

        @block.vector
        def _(dve):
            tile_bc = [P, TILES, D]

            def root(done):
                dve.drain()
                dve.nop().then_inc(S["root_in"], 1)
                dve.wait_ge(S["root_out"], done)

            def small(l, parity):
                for i in range(3):
                    row = slice(32 * i, 32 * i + 1)
                    nc.vector.tensor_copy(b_part[:, :], brow[:, :])
                    dve.drain()
                    for t in range(GP):
                        nc.vector.tensor_copy(bias_parts[row, t * P:(t + 1) * P], b_part[row, :])
                    if i < 2:
                        nc.vector.tensor_tensor(brow[:, :], brow[:, :], b_part[:, :], ALU.subtract)
                        dve.drain()
                for ri in range(2):
                    for par in range(2):
                        side = slice(par * D, (par + 1) * D)
                        nc.vector.tensor_copy(cdz[side, :, ri, par], cols[side, 2 + ri, bass.ds(l, 1), :].squeeze(1))
                dve.wait_ge(S["powers_ok"], 2 * l + 2)
                w, w127 = [[powers[:, parity, :, ri, i] for ri in range(2)] for i in (1, P - 1)]
                cd = [cols[:, 2 + ri, bass.ds(l, 1), :].squeeze(1) for ri in range(2)]
                for i, (a, b) in enumerate(((w[0], cd[0]), (w[1], cd[1]), (w[0], cd[1]), (w[1], cd[0]),
                                            (w[0], w127[0]), (w[1], w127[1]), (w[0], w127[1]), (w[1], w127[0]))):
                    nc.vector.tensor_tensor(part[:, i, :], a, b, ALU.mult)
                dve.drain()
                for dst, i, op in ((cdw[:, 0, :], 0, ALU.add), (cdw[:, 1, :], 2, ALU.subtract),
                                   (w128[:, 0, :], 4, ALU.subtract), (w128[:, 1, :], 6, ALU.add)):
                    nc.vector.tensor_tensor(dst, part[:, i, :], part[:, i + 1, :], op)
                dve.drain()
                dve.nop().then_inc(S["small_ok"], 1)
                nc.vector.tensor_scalar(cds[:, :, 0], cdw[:, 1, :], -1.0, None, ALU.mult)
                nc.vector.tensor_copy(cds[:, :, 1], cdw[:, 1, :])
                for ri in range(2):
                    nc.vector.tensor_copy(wr[:, :, ri, :], over_last(w128[:, 0, :], BATCH))
                    nc.vector.tensor_scalar(ws[:, :, ri, :], over_last(w128[:, 1, :], BATCH), (1.0, -1.0)[ri], None, ALU.mult)
                dve.drain()

            def scan(q):
                st = state[:, q, :, :].rearrange("p q r (b c) -> p q r b c", c=CHUNKS)
                for c in range(1, CHUNKS - 1):
                    prev, cur = st[:, :, :, :, c - 1], st[:, :, :, :, c]
                    nc.vector.tensor_tensor(s1[:, q], wr[:, q], prev, ALU.mult)
                    for ri in range(2):
                        nc.vector.tensor_tensor(s2[:, q, ri, :], ws[:, q, ri, :], prev[:, :, 1 - ri], ALU.mult)
                    dve.drain()
                    nc.vector.tensor_tensor(s1[:, q], s1[:, q], s2[:, q], ALU.add)
                    dve.drain()
                    nc.vector.tensor_tensor(cur, cur, s1[:, q], ALU.add)
                    dve.drain()

            dve.nop().then_inc(S["z_read"], 1)
            layer_norm(nc, dve, hs[:, :, :], resid[:, :, :], hs[:, :, :], y[:, :, :], stat, LN_EPS, lambda: root(1))
            dve.drain()
            dve.nop().then_inc(S["layer_done"], 1)
            with dve.Fori(0, LAYERS // 2) as ll:
                for parity in range(2):
                    l = ll * 2 + parity
                    u_t = u[:, :, :].rearrange("p h t -> p t h")
                    layer_norm(nc, dve, y[:, :, :], hs[:, :, :], y[:, :, :], u_t, stat, LN_EPS, lambda: root(l + 2))
                    dve.drain()
                    dve.wait_ge(S["params"], 16 * NPARAM * l + 16 * NPARAM)
                    nc.vector.tensor_tensor(y[:, :, :], y[:, :, :], scale_bc[:, :].unsqueeze(1).broadcast_to(tile_bc), ALU.mult)
                    dve.drain()
                    nc.vector.tensor_tensor(u_t, y[:, :, :], bias_bc[:, :].unsqueeze(1).broadcast_to(tile_bc), ALU.add)
                    dve.drain()
                    dve.nop().then_inc(S["u_ok"], 1)
                    for half in range(2):
                        if half == 0:
                            small(l, parity)
                        for g in range(half * GROUPS // 2, (half + 1) * GROUPS // 2):
                            dve.wait_ge(S["s_mm"], l * GROUPS + g + 1)
                            q = slice(g * GP, (g + 1) * GP)
                            for ri in range(2):
                                nc.vector.tensor_tensor(state[:, q, ri, :], ps_s[g % 2][:, :, ri, :], over_last(cdw[:, 0, q], TILES), ALU.mult)
                                nc.vector.tensor_tensor(rot[:, :, ri, :], ps_s[g % 2][:, :, 1 - ri, :], over_last(cds[:, q, ri], TILES), ALU.mult)
                            dve.drain()
                            dve.nop().then_inc(S["s_read"], 1)
                            nc.vector.tensor_tensor(state[:, q, :, :], state[:, q, :, :], rot[:, :, :, :], ALU.add)
                            dve.drain()
                        scan(slice(half * HALF, (half + 1) * HALF))
                        dve.nop().then_inc(S["scanned"], 1)
                    for j in range(BLOCKS):
                        dve.wait_ge(S["gate_ok"], l * BLOCKS + j + 1)
                        nc.vector.tensor_tensor(zz[:, j % 2, :, :], ps_z[j % 2][:, :, 0:D], gate[:, j % 2, :, :], ALU.mult).then_inc(S["z_read"], 1)
                        dve.drain()
                        t = slice(j * GP, (j + 1) * GP)
                        nc.vector.tensor_tensor(hs[:, t, :], hs[:, t, :], zz[:, j % 2, :, :], ALU.add)
                    dve.drain()
                    dve.nop().then_inc(S["layer_done"], 1)

        @block.tensor
        def _(pe):
            def turn(l, parity, g):
                if g == 0:
                    pe.wait_ge(S["z_read"], l * BLOCKS + 1)
                else:
                    pe.wait_ge(S["turn_ok"], l * GROUPS + g)
                for ri in range(2):
                    for q in range(GP):
                        last = nc.tensor.transpose(ps_z[ri][:, q, :], powers[:, parity, g * GP + q, ri, :], ident[:, :])
                last.then_inc(S["turn_mm"], 1)

            def into_state(l, g):
                pe.wait_ge(S["turn_ok"], l * GROUPS + g + 1)
                if g >= 2:
                    pe.wait_ge(S["s_read"], l * GROUPS + g - 1)
                for q in range(GP):
                    for ri in range(2):
                        for par in range(2):
                            last = nc.tensor.matmul(ps_s[g % 2][par * D:(par + 1) * D, q, ri, :],
                                                    turned[:, g % TURNED, ri, q, par * D:(par + 1) * D],
                                                    u[:, 2 * (g * GP + q) + par, :], start=True, stop=True)
                last.then_inc(S["s_mm"], 1)

            def layer(l, parity):
                pe.wait_ge(S["powers_ok"], 2 * l + 2)
                for g in range(TURNED):
                    turn(l, parity, g)
                pe.wait_ge(S["params"], 16 * NPARAM * l + 16 * NPARAM)
                nc.tensor.transpose(ps_k[:, 0:P], w_in[:, :], ident[:, :]).then_inc(S["wout_t"], 1)
                pe.wait_ge(S["u_ok"], l + 1)
                for g in range(GROUPS):
                    into_state(l, g)
                    if g + TURNED < GROUPS:
                        turn(l, parity, g + TURNED)
                pe.wait_ge(S["small_ok"], l + 1)
                pe.wait_ge(S["wout_ok"], l + 1)
                for pair in range(PAIRS):
                    for ri in range(2):
                        last = nc.tensor.matmul(ps_k[:, 2 * pair:2 * pair + 2], powers[:, parity, pair, ri, :], cdz[:, pair, ri, :],
                                                start=ri == 0, stop=ri == 1)
                last.then_inc(S["k_mm"], 1)
                pe.wait_ge(S["k_sb"], l + 1)
                nc.tensor.transpose(ps_k[:, D:D + P], kt[:, :], ident[:, :]).then_inc(S["k_turned"], 1)
                for g in range(GROUPS):
                    pe.wait_ge(S["pad_ok"], l * GROUPS + g + 1)
                    pe.wait_ge(t0_in[g % 2], 16 * (GROUPS // 2) * l + 16 * (g // 2) + 16)
                    if g >= 2:
                        pe.wait_ge(S["y_read"], l * GROUPS + g - 1)
                    for q in range(GP):
                        pair = g * GP + q
                        out = ps_y[g % 2][:, 2 * q:2 * q + 2, :]
                        for ri in range(2):
                            nc.tensor.matmul(out, powers[:, parity, pair, ri, :], padded[:, g % 2, q, ri, :, :],
                                             start=ri == 0, stop=False, skip_group_check=True)
                        for par in range(2):
                            last = nc.tensor.matmul(ps_y[g % 2][:, 2 * q + par, :], toep[:, g % 2, 2 * q + par, :],
                                                    u[:, 2 * pair + par, :], start=False, stop=par == 1, skip_group_check=True)
                    last.then_inc(S["y_mm"], 1)
                    pe.drain()
                    pe.nop().then_inc(S["t0_used"], 1)
                pe.nop().then_inc(S["powers_used"], 1)
                pe.wait_ge(S["y_ok"], l + 1)
                for k in range(BLOCKS + 1):
                    if k < BLOCKS:
                        if k >= 1:
                            pe.wait_ge(S["yt_ok"], l * BLOCKS + k)
                        for j in range(GP // 2):
                            t = k * GP + 2 * j
                            last = nc.tensor.transpose(ps_t[:, j * P:(j + 1) * P], y[:, t:t + 2, :].rearrange("p t h -> p (t h)"), ident[:, :])
                        last.then_inc(S["yt_mm"], 1)
                    if k >= 1:
                        i = k - 1
                        if k == BLOCKS:
                            pe.wait_ge(S["yt_ok"], l * BLOCKS + k)
                        if i >= 2:
                            pe.wait_ge(S["z_read"], l * BLOCKS + i)
                        nc.tensor.matmul(ps_z[i % 2][:, :, :].rearrange("p a b -> p (a b)"), ones[:, :], bias_parts[:, :], start=True, stop=False)
                        for j in range(GP // 2):
                            dst = ps_z[i % 2][:, 2 * j:2 * j + 2, :].rearrange("p a b -> p (a b)")
                            last = nc.tensor.matmul(dst, yT[:, i % 2, j * P:(j + 1) * P], wout[:, :], start=False, stop=j == GP // 2 - 1)
                        last.then_inc(S["z_mm"], 1)

            pe.nop().then_inc(S["powers_used"], 1)
            with pe.Fori(0, LAYERS // 2) as ll:
                for parity in range(2):
                    layer(ll * 2 + parity, parity)

    with ExitStack() as stack:
        em = Memory(nc, stack, "s4_end")
        back = em.sem("back")
        with nc.Block() as block:

            @block.sync
            def _(sp):
                sp.dma_start(resid[:, :, :], dram_resid).then_inc(back, 16)

            @block.vector
            def _(dve):
                dve.wait_ge(back, 16)
                nc.vector.tensor_tensor(resid[:, :, :], resid[:, :, :], hs[:, :, :], ALU.add)


def expert_mixture(nc, m, A, resid, ident, flip):
    E = A["L0_ffn_Wr"].shape[1]
    PAIRS = E // 2
    HB = BATCH // 2
    COLS = HB * SEQ
    BN_EPS = 1e-3
    BLK = 4 * P
    VEC = ("b1", "g1", "be1", "m1", "v1", "b2", "g2", "be2", "m2", "v2")

    xT = m.sb("xT", [P, COLS])
    w1 = m.sb("w1", [P, 2, PAIRS, P])
    w2 = m.sb("w2", [P, PAIRS, P])
    wo = m.sb("wo", [P, PAIRS, D])
    bo = m.sb("bo", [E, D])
    wr = m.sb("wr", [P, E])
    br = m.sb("br", [P, E])
    rowsv = m.sb("rowsv", [len(VEC) * PAIRS, P])
    vec = m.sb("vec", [P, len(VEC), PAIRS])
    fold = m.sb("fold", [P, 2, 2, PAIRS])
    sd = m.sb("sd", [P, 2, PAIRS])
    wb = m.sb("wb", [P, PAIRS, SEQ])
    ybo = m.sb("ybo", [P, CHUNKS, D])
    V = {n: i for i, n in enumerate(VEC)}

    with ExitStack() as stack:
        pm = Memory(nc, stack, "gate")
        x = pm.sb("x", [P, TILES // 2, 2, D])
        square = pm.sb("square", [P, 2, TILES // 2, D])
        stat = pm.sb("stat", [P, 3, TILES])
        stat4 = stat[:, :, :].rearrange("p s (a t) -> p s a t", a=2)
        lg = pm.sb("lg", [P, CHUNKS, E])
        ex = pm.sb("ex", [P, CHUNKS, E])
        red = pm.sb("red", [P, 2, CHUNKS])
        wT = pm.sb("wT", [E, SEQ])
        sel = pm.sb("sel", [E, PAIRS, P])
        ps_v = pm.ps("ps_v", [P, len(VEC) * PAIRS])
        ps_x = [pm.ps(f"ps_x{i}", [P, BLK]) for i in range(2)]
        ps_l = pm.ps("ps_l", [P, CHUNKS, E])
        ps_t = pm.ps("ps_t", [E, BLK])
        ps_b = [pm.ps(f"ps_b{i}", [P, BLK]) for i in range(2)]
        ps_y = pm.ps("ps_y", [P, 8, D])
        names = ("zeroed", "loaded", "vec_tr", "root_in", "root_out", "x_ok", "xt_mm", "xt_sb", "l_mm", "exp_in", "exp_out",
                 "soft_ok", "wt_mm", "wt_sb", "wb_mm", "wb_sb", "sel_ok", "yb_mm", "yb_sb")
        S = {n: pm.sem(n) for n in names}
        ffn = {k: A["L0_ffn_" + k] for k in ("Wr", "br", "W1", "W2", "Wo", "bo") + VEC}
        NB = COLS // BLK

        with nc.Block() as block:

            @block.sync
            def _(sp):
                n = 0
                for i, v in enumerate(VEC):
                    sp.dma_start(rowsv[i * PAIRS:(i + 1) * PAIRS, :], ffn[v].rearrange("(q e) h -> q (e h)", e=2)).then_inc(S["loaded"], 16)
                    n += 1
                for k in range(2):
                    sp.dma_start(wr[k * D:(k + 1) * D, :], ffn["Wr"]).then_inc(S["loaded"], 16)
                    n += 1
                sp.dma_start(br[:, :], ffn["br"].partition_broadcast(P)).then_inc(S["loaded"], 16)
                sp.dma_start(bo[:, :], ffn["bo"]).then_inc(S["loaded"], 16)
                sp.dma_start(wo[:, :, :], ffn["Wo"].rearrange("(q e) h d -> (e h) q d", e=2)).then_inc(S["loaded"], 16)
                sp.wait_ge(S["zeroed"], 1)
                for k in range(2):
                    side = slice(k * D, (k + 1) * D)
                    for e in range(2):
                        sp.dma_start(w1[side, k, :, e * D:(e + 1) * D], ffn["W1"].rearrange("(q e) d h -> e d q h", e=2)[e]).then_inc(S["loaded"], 16)
                    sp.dma_start(w2[side, :, side], ffn["W2"].rearrange("(q e) h k -> e h q k", e=2)[k]).then_inc(S["loaded"], 16)
                assert n + 3 + 6 == 21
                sp.wait_ge(S["loaded"], 16 * 21)

            @block.gpsimd
            def _(pool):
                nc.gpsimd.memset(w1[:, :, :, :], 0.0).then_inc(S["sel_ok"], 1)
                pool.wait_ge(S["sel_ok"], 1)
                nc.gpsimd.memset(w2[:, :, :], 0.0).then_inc(S["zeroed"], 1)
                pool.wait_ge(S["zeroed"], 1)
                nc.gpsimd.memset(sel[:, :, :], 0.0).then_inc(S["sel_ok"], 1)
                pool.wait_ge(S["sel_ok"], 2)
                nc.gpsimd.affine_select(out=sel[:, :, :], in_=sel[:, :, :], compare_op=ALU.not_equal, fill=1.0, base=0,
                                        pattern=[[-2, PAIRS], [-1, 2], [0, D]], channel_multiplier=1).then_inc(S["sel_ok"], 1)
                pool.wait_ge(S["sel_ok"], 3)

            @block.scalar
            def _(act):
                act.wait_ge(S["root_in"], 1)
                nc.scalar.activation(stat[:, 2], stat[:, 1], ACT.Sqrt)
                nc.scalar.activation(sd[:, :, :], sd[:, :, :], ACT.Sqrt)
                act.drain()
                act.nop().then_inc(S["root_out"], 1)
                for k in range(NB):
                    act.wait_ge(S["xt_mm"], k + 1)
                    nc.scalar.activation(xT[:, k * BLK:(k + 1) * BLK], ps_x[k % 2][:, :], ACT.Copy).then_inc(S["xt_sb"], 1)
                act.wait_ge(S["exp_in"], 1)
                nc.scalar.activation(ex[:, :, :], lg[:, :, :], ACT.Exp).then_inc(S["exp_out"], 1)
                for k in range(4):
                    for q in range(PAIRS):
                        n = k * PAIRS + q
                        act.wait_ge(S["wb_mm"], n + 1)
                        nc.scalar.activation(wb[:, q, k * BLK:(k + 1) * BLK], ps_b[n % 2][:, :], ACT.Copy).then_inc(S["wb_sb"], 1)

            @block.vector
            def _(dve):
                dve.wait_ge(S["vec_tr"], 1)
                nc.vector.tensor_copy(vec[:, :, :], ps_v[:, :].rearrange("p (v q) -> p v q", q=PAIRS))
                dve.drain()
                for i, k in enumerate("12"):
                    nc.vector.tensor_scalar(sd[:, i, :], vec[:, V["v" + k], :], BN_EPS, None, ALU.add)

                def root():
                    dve.drain()
                    dve.nop().then_inc(S["root_in"], 1)
                    dve.wait_ge(S["root_out"], 1)

                x_t = x[:, :, :, :].rearrange("p t a d -> p a t d")
                r_t = resid[:, :, :].rearrange("p (a t) d -> p a t d", a=2)
                layer_norm(nc, dve, x_t, r_t, x_t, square[:, :, :, :], stat4, LN_EPS, root)
                dve.drain()
                dve.nop().then_inc(S["x_ok"], 1)
                nc.vector.reciprocal(sd[:, :, :], sd[:, :, :])
                dve.drain()
                for i, k in enumerate("12"):
                    nc.vector.tensor_tensor(fold[:, i, 0, :], vec[:, V["g" + k], :], sd[:, i, :], ALU.mult)
                    nc.vector.tensor_tensor(fold[:, i, 1, :], vec[:, V["b" + k], :], vec[:, V["m" + k], :], ALU.subtract)
                    dve.drain()
                    nc.vector.tensor_tensor(fold[:, i, 1, :], fold[:, i, 1, :], fold[:, i, 0, :], ALU.mult)
                    dve.drain()
                    nc.vector.tensor_tensor(fold[:, i, 1, :], fold[:, i, 1, :], vec[:, V["be" + k], :], ALU.add)
                dve.wait_ge(S["l_mm"], 1)
                nc.vector.scalar_tensor_tensor(lg[:, :, :], ps_l[:, :, :], 1.0 / BATCH, br[:, :].unsqueeze(1).broadcast_to([P, CHUNKS, E]),
                                               ALU.mult, ALU.add)
                dve.drain()
                nc.vector.tensor_reduce(out=red[:, 0, :], in_=lg[:, :, :], axis=AX.X, op=ALU.max)
                dve.drain()
                nc.vector.tensor_tensor(lg[:, :, :], lg[:, :, :], over_last(red[:, 0, :], E), ALU.subtract)
                dve.drain()
                dve.nop().then_inc(S["exp_in"], 1)
                dve.wait_ge(S["exp_out"], 1)
                nc.vector.tensor_reduce(out=red[:, 1, :], in_=ex[:, :, :], axis=AX.X, op=ALU.add)
                dve.drain()
                nc.vector.reciprocal(red[:, 0, :], red[:, 1, :])
                dve.drain()
                nc.vector.tensor_tensor(ex[:, :, :], ex[:, :, :], over_last(red[:, 0, :], E), ALU.mult)
                dve.drain()
                dve.nop().then_inc(S["soft_ok"], 1)
                for k in range(4):
                    dve.wait_ge(S["wt_mm"], k + 1)
                    nc.vector.tensor_copy(wT[:, k * BLK:(k + 1) * BLK], ps_t[:, :]).then_inc(S["wt_sb"], 1)
                for k in range(2):
                    dve.wait_ge(S["yb_mm"], k + 1)
                    nc.vector.tensor_copy(ybo[:, k * 8:(k + 1) * 8, :], ps_y[:, :, :]).then_inc(S["yb_sb"], 1)

            @block.tensor
            def _(pe):
                pe.wait_ge(S["loaded"], 16 * 21)
                nv = len(VEC) * PAIRS
                nc.tensor.transpose(ps_v[:, :], rowsv[:, :], ident[0:nv, 0:nv]).then_inc(S["vec_tr"], 1)
                pe.wait_ge(S["x_ok"], 1)
                for k in range(NB):
                    if k >= 2:
                        pe.wait_ge(S["xt_sb"], k - 1)
                    for j in range(4):
                        t = 4 * k + j
                        last = nc.tensor.transpose(ps_x[k % 2][:, j * P:(j + 1) * P], x[:, t, :, :].rearrange("p a d -> p (a d)"), ident[:, :])
                    last.then_inc(S["xt_mm"], 1)
                pe.wait_ge(S["xt_sb"], NB)
                for c in range(CHUNKS):
                    for k in range(HB):
                        a = k * SEQ + c * P
                        last = nc.tensor.matmul(ps_l[:, c, :], xT[:, a:a + P], wr[:, :], start=k == 0, stop=k == HB - 1)
                last.then_inc(S["l_mm"], 1)
                pe.wait_ge(S["soft_ok"], 1)
                for k in range(4):
                    if k:
                        pe.wait_ge(S["wt_sb"], k)
                    for j in range(4):
                        last = nc.tensor.transpose(ps_t[:, j * P:(j + 1) * P], ex[:, 4 * k + j, :], ident[:, :])
                    last.then_inc(S["wt_mm"], 1)
                pe.wait_ge(S["wt_sb"], 4)
                pe.wait_ge(S["sel_ok"], 3)
                for k in range(4):
                    for q in range(PAIRS):
                        n = k * PAIRS + q
                        if n >= 2:
                            pe.wait_ge(S["wb_sb"], n - 1)
                        nc.tensor.matmul(ps_b[n % 2][:, :], sel[:, q, :], wT[:, k * BLK:(k + 1) * BLK], start=True, stop=True).then_inc(S["wb_mm"], 1)
                for k in range(2):
                    if k:
                        pe.wait_ge(S["yb_sb"], 1)
                    for j in range(8):
                        c = 8 * k + j
                        last = nc.tensor.matmul(ps_y[:, j, :], wT[:, c * P:(c + 1) * P], bo[:, :], start=True, stop=True)
                    last.then_inc(S["yb_mm"], 1)

    STEPS = BATCH * PAIRS
    NBLK = SEQ // BLK
    h1 = m.sb("h1", [P, 2, BLK])
    h2 = m.sb("h2", [P, 2, BLK])
    h2w = m.sb("h2w", [P, 2, PAIRS, BLK])
    add = m.sb("add", [P, 2, 4, D])
    ps1 = [m.ps(f"ps1{i}", [P, BLK]) for i in range(2)]
    ps2 = [m.ps(f"ps2{i}", [P, BLK]) for i in range(2)]
    ps_o = [m.ps(f"ps_o{i}", [P, 4, D]) for i in range(2)]
    names = ("h1_mm", "h1_ok", "h2_mm", "h2_ok", "h2w_ok", "wo_mm", "wo_read")
    S = {n: m.sem(n) for n in names}

    with nc.Block() as block:

        @block.tensor
        def _(pe):
            with pe.Fori(0, NBLK) as k:
                for s in range(STEPS + 2):
                    if s < STEPS:
                        b, q = divmod(s, PAIRS)
                        if s >= 2:
                            pe.wait_ge(S["h1_ok"], k * STEPS + s - 1)
                        base = b % HB * SEQ
                        nc.tensor.matmul(ps1[s % 2][:, :], w1[:, b // HB, q, :], xT[:, bass.ds(k * BLK + base, BLK)],
                                         start=True, stop=True).then_inc(S["h1_mm"], 1)
                    if s >= 2 and (s - 2) % PAIRS == PAIRS - 1:
                        b = (s - 2) // PAIRS
                        pe.wait_ge(S["h2w_ok"], k * STEPS + (b + 1) * PAIRS)
                        pe.wait_ge(S["wo_read"], k * BATCH + b + 1)
                        for j in range(4):
                            for q in range(PAIRS):
                                last = nc.tensor.matmul(ps_o[b % 2][:, j, :], h2w[:, b % 2, q, j * P:(j + 1) * P], wo[:, q, :],
                                                        start=q == 0, stop=q == PAIRS - 1)
                        last.then_inc(S["wo_mm"], 1)
                    if 1 <= s <= STEPS:
                        i = s - 1
                        pe.wait_ge(S["h1_ok"], k * STEPS + i + 1)
                        if i >= 2:
                            pe.wait_ge(S["h2_ok"], k * STEPS + i - 1)
                        nc.tensor.matmul(ps2[i % 2][:, :], w2[:, i % PAIRS, :], h1[:, i % 2, :], start=True, stop=True).then_inc(S["h2_mm"], 1)

        @block.scalar
        def _(act):
            with act.Fori(0, NBLK) as k:
                for s in range(STEPS + 1):
                    if s < STEPS:
                        q = s % PAIRS
                        act.wait_ge(S["h1_mm"], k * STEPS + s + 1)
                        if s >= 2:
                            act.wait_ge(S["h2_mm"], k * STEPS + s - 1)
                        nc.scalar.activation(h1[:, s % 2, :], ps1[s % 2][:, :], ACT.Relu, bias=fold[:, 0, 1, q:q + 1],
                                             scale=fold[:, 0, 0, q:q + 1]).then_inc(S["h1_ok"], 1)
                    if s >= 1:
                        i, q = s - 1, (s - 1) % PAIRS
                        act.wait_ge(S["h2_mm"], k * STEPS + i + 1)
                        if i >= 2:
                            act.wait_ge(S["h2w_ok"], k * STEPS + i - 1)
                        nc.scalar.activation(h2[:, i % 2, :], ps2[i % 2][:, :], ACT.Relu, bias=fold[:, 1, 1, q:q + 1],
                                             scale=fold[:, 1, 0, q:q + 1]).then_inc(S["h2_ok"], 1)

        @block.vector
        def _(dve):
            dve.nop().then_inc(S["wo_read"], 2)
            with dve.Fori(0, NBLK) as k:
                def finish(b):
                    dve.wait_ge(S["wo_mm"], k * BATCH + b + 1)
                    nc.vector.tensor_tensor(add[:, b % 2, :, :], ps_o[b % 2][:, :, :], ybo[:, bass.ts(k, 4), :], ALU.add).then_inc(S["wo_read"], 1)
                    dve.drain()
                    tiles = resid[:, bass.ds(k * 4 + b * CHUNKS, 4), :]
                    nc.vector.tensor_tensor(tiles, tiles, add[:, b % 2, :, :], ALU.add)

                for s in range(STEPS):
                    b, q = divmod(s, PAIRS)
                    dve.wait_ge(S["h2_ok"], k * STEPS + s + 1)
                    nc.vector.tensor_tensor(h2w[:, b % 2, q, :], h2[:, s % 2, :], wb[:, q, bass.ts(k, BLK)], ALU.mult).then_inc(S["h2w_ok"], 1)
                    if q == PAIRS - 1 and b >= 1:
                        finish(b - 1)
                finish(BATCH - 1)


def sigmoid_attention(nc, m, A, resid, ident, flip):
    HEADS = 8
    PAIRS = HEADS // 2
    SCALE = float(D) ** 0.5
    X_UP, W_UP, Q_UP = 2.0 ** 4, 2.0 ** 8, 2.0 ** 6
    BLK = 512
    QB = SEQ // BLK
    IH = 2
    N = TILES * P

    wq = m.sb("wq", [P, HEADS, 2, D], F16)
    wk = m.sb("wk", [P, HEADS, 2, D], F16)
    wv = m.sb("wv", [P, HEADS, D], F16)
    wo = m.sb("wo", [P, PAIRS, D])
    x_hi = m.sb("x_hi", [P, N], F16)
    x_lo = m.sb("x_lo", [P, N], F16)

    with ExitStack() as stack:
        pm = Memory(nc, stack, "split")
        x = pm.sb("x", [P, TILES, D])
        twice = pm.sb("twice", [P, TILES, 2, D])
        stat = pm.sb("stat", [P, 3, TILES])
        raw = [pm.sb(f"raw{i}", [P, HEADS * D]) for i in range(3)]
        ps = [pm.ps(f"ps{i}", [P, BLK]) for i in range(4)]
        loaded, root_in, root_out, x_ok, x_tr, hi_ok, lo_ok = map(pm.sem, (
            "loaded", "root_in", "root_out", "x_ok", "x_tr", "hi_ok", "lo_ok"))
        NB = N // BLK
        with nc.Block() as block:

            @block.sync
            def _(sp):
                for i, n in enumerate(("Wq", "Wk", "Wv")):
                    for k in range(2):
                        sp.dma_start(raw[i][k * D:(k + 1) * D, :], A["L1_attn_" + n]).then_inc(loaded, 16)
                wo_src = A["L1_attn_Wo"].rearrange("(f q a) o -> a f q o", a=2, q=PAIRS)
                for k in range(2):
                    sp.dma_start(wo[k * D:(k + 1) * D, :, :], wo_src[k]).then_inc(loaded, 16)
                sp.wait_ge(loaded, 128)

            @block.vector
            def _(dve):
                dve.wait_ge(loaded, 128)
                lo_rows = slice(D, P)
                for i, dst in enumerate((wq, wk, wv)):
                    nc.vector.tensor_scalar(raw[i][:, :], raw[i][:, :], W_UP, None, ALU.mult)
                dve.drain()
                parts = []
                for i, dst in enumerate((wq, wk, wv)):
                    src = raw[i][:, :].rearrange("p (f h) -> p h f", h=HEADS)
                    if i < 2:
                        src = src.unsqueeze(2).broadcast_to([P, HEADS, 2, D])
                        parts.append((dst[:, :, :, :], dst[lo_rows, :, :, :], src, src[lo_rows]))
                    else:
                        parts.append((dst[:, :, :], dst[lo_rows, :, :], src, src[lo_rows]))
                for dst, _, src, _ in parts:
                    nc.vector.tensor_copy(dst, src)
                dve.drain()
                for _, dst, _, src in parts:
                    nc.vector.tensor_tensor(dst, src, dst, ALU.subtract)

                def root():
                    dve.drain()
                    dve.nop().then_inc(root_in, 1)
                    dve.wait_ge(root_out, 1)

                layer_norm(nc, dve, x[:, :, :], resid[:, :, :], x[:, :, :], twice[:, :, 0, :], stat, LN_EPS, root)
                dve.drain()
                for k in range(2):
                    nc.vector.tensor_copy(twice[:, :, k, :], x[:, :, :])
                dve.drain()
                dve.nop().then_inc(x_ok, 1)
                for k in range(NB):
                    dve.wait_ge(hi_ok, k + 1)
                    c = slice(k * BLK, (k + 1) * BLK)
                    nc.vector.scalar_tensor_tensor(x_lo[:, c], ps[k % 4][:, :], X_UP, x_hi[:, c], ALU.mult, ALU.subtract).then_inc(lo_ok, 1)

            @block.scalar
            def _(act):
                act.wait_ge(root_in, 1)
                nc.scalar.activation(stat[:, 2], stat[:, 1], ACT.Sqrt).then_inc(root_out, 1)
                for k in range(NB):
                    act.wait_ge(x_tr, k + 1)
                    nc.scalar.activation(x_hi[:, k * BLK:(k + 1) * BLK], ps[k % 4][:, :], ACT.Copy, scale=X_UP).then_inc(hi_ok, 1)

            @block.tensor
            def _(pe):
                pe.wait_ge(x_ok, 1)
                for k in range(NB):
                    if k >= 4:
                        pe.wait_ge(lo_ok, k - 3)
                    for j in range(4):
                        last = nc.tensor.transpose(ps[k % 4][:, j * P:(j + 1) * P],
                                                   twice[:, 4 * k + j, :, :].rearrange("p a d -> p (a d)"), ident[:, :])
                    last.then_inc(x_tr, 1)

    k_st = m.sb("k_st", [P, 2, 2, SEQ], F16)
    q_hi = m.sb("q_hi", [P, 2, 2, SEQ], F16)
    q_lo = m.sb("q_lo", [P, 2, SEQ], F16)
    v_st = m.sb("v_st", [P, 2, CHUNKS, 2, D])
    sig = m.sb("sig", [P, 2, 2, 2 * BLK])
    ctxT = m.sb("ctxT", [P, PAIRS, SEQ])
    ps_s = [m.ps(f"ps_s{h}", [P, 2 * BLK]) for h in range(2)]
    ps_o = m.ps("ps_o", [P, 2, BLK])
    ps_p = [m.ps(f"ps_p{i}", [P, BLK]) for i in range(2)]
    names = ("p_mm", "p_read", "qk_mm", "sig_ok", "pv_mm", "o_read", "wo_mm", "wo_read")
    S = {n: m.sem(n) for n in names}
    KQ = 4 * QB
    PB = KQ + CHUNKS // 4
    JJ = IH * CHUNKS
    FIRST_JJ = 2
    DOWN = Q_UP / (X_UP * W_UP)


    with nc.Block() as block:

        @block.tensor
        def _(pe):
            def project(i, b, hp, done):
                if i >= 2:
                    pe.wait_ge(S["p_read"], done + i - 1)
                if i < KQ:
                    w = wk if i < KQ // 2 else wq
                    h, c = divmod(i % (KQ // 2), QB)
                    lhsT = w[:, bass.ds(hp * 2 + h, 1), :, :].rearrange("p a t f -> p (a t f)")
                    for part, xs in enumerate((x_hi, x_lo)):
                        last = nc.tensor.matmul(ps_p[i % 2][:, :], lhsT, xs[:, bass.ds(b * SEQ + c * BLK, BLK)],
                                                start=part == 0, stop=part == 1)
                else:
                    for j in range(4):
                        c = (i - KQ) * 4 + j
                        for part, xs in enumerate((x_hi, x_lo)):
                            last = nc.tensor.matmul(ps_p[i % 2][:, j * P:(j + 1) * P], xs[:, bass.ds(b * SEQ + c * P, P)],
                                                    wv[:, bass.ds(hp * 2, 2), :].rearrange("p a f -> p (a f)"),
                                                    start=part == 0, stop=part == 1)
                last.then_inc(S["p_mm"], 1)

            def pair(n, slot, next_b, next_hp):
                pe.wait_ge(S["p_read"], n * PB + PB)
                for jj in range(JJ + 1):
                    if jj < JJ:
                        ih, j = divmod(jj, CHUNKS)
                        for h in range(2):
                            s = 2 * jj + h
                            if s >= 2:
                                pe.wait_ge(S["sig_ok"], n * 2 * JJ + s - 1)
                            for i2 in range(2):
                                c = (2 * ih + i2) * BLK
                                nc.tensor.matmul(ps_s[h][:, i2 * BLK:(i2 + 1) * BLK], k_st[:, slot, h, j * P:(j + 1) * P],
                                                 q_hi[:, slot, h, c:c + BLK], start=True, stop=False)
                        for i2 in range(2):
                            c = (2 * ih + i2) * BLK
                            for h in range(2):
                                rows = slice(h * D, (h + 1) * D)
                                last = nc.tensor.matmul(ps_s[h][:, i2 * BLK:(i2 + 1) * BLK], k_st[rows, slot, h, j * P:(j + 1) * P],
                                                        q_lo[rows, slot, c:c + BLK], start=False, stop=True)
                                if i2:
                                    last.then_inc(S["qk_mm"], 1)
                    if 0 <= jj - FIRST_JJ < PB:
                        project(jj - FIRST_JJ, next_b, next_hp, n * PB + PB)
                    if jj >= 1:
                        ih, j = divmod(jj - 1, CHUNKS)
                        pe.wait_ge(S["sig_ok"], n * 2 * JJ + 2 * jj)
                        if j == 0:
                            pe.wait_ge(S["o_read"], n * IH + ih + 1)
                        for i2 in range(2):
                            for h in range(2):
                                last = nc.tensor.matmul(ps_o[h * D:(h + 1) * D, i2, :], v_st[:, slot, j, h, :],
                                                        sig[:, (jj - 1) % 2, h, i2 * BLK:(i2 + 1) * BLK],
                                                        start=j == 0, stop=j == CHUNKS - 1)
                        last.then_inc(S["pv_mm"], 1)

            for i in range(PB):
                project(i, 0, 0, 0)
            with pe.Fori(0, BATCH) as b:
                with pe.Fori(0, PAIRS // 2) as hh:
                    n = b * PAIRS + hh * 2
                    pair(n, 0, b, hh * 2 + 1)
                    pair(n + 1, 1, (b + hh) % BATCH, 2 - hh * 2)
                pe.wait_ge(S["o_read"], b * (PAIRS * IH) + PAIRS * IH + 1)
                for k in range(2):
                    for t in range(8):
                        for hp in range(PAIRS):
                            last = nc.tensor.matmul(ps_p[k][:, t * D:(t + 1) * D], ctxT[:, hp, (8 * k + t) * P:(8 * k + t + 1) * P],
                                                    wo[:, hp, :], start=hp == 0, stop=hp == PAIRS - 1)
                    last.then_inc(S["wo_mm"], 1)
                pe.wait_ge(S["wo_read"], 2 * b + 2)

        @block.scalar
        def _(act):
            act.preload_act_table(ACT.Sigmoid)
            with act.Fori(0, BATCH * PAIRS) as n:
                for s in range(2 * JJ):
                    jj, h = divmod(s, 2)
                    act.wait_ge(S["qk_mm"], n * 2 * JJ + s + 1)
                    if jj >= 2:
                        act.wait_ge(S["pv_mm"], n * JJ + jj - 1)
                    nc.scalar.activation(sig[:, jj % 2, h, :], ps_s[h][:, :], ACT.Sigmoid,
                                         scale=SCALE / (Q_UP * Q_UP)).then_inc(S["sig_ok"], 1)

        @block.vector
        def _(dve):
            def split(i, slot, done):
                dve.wait_ge(S["p_mm"], done + i + 1)
                if i < KQ:
                    h, c = divmod(i % (KQ // 2), QB)
                    cols = slice(c * BLK, (c + 1) * BLK)
                    hi = (k_st if i < KQ // 2 else q_hi)[:, slot, h, cols]
                    nc.vector.tensor_scalar(hi, ps_p[i % 2][:, :], DOWN, None, ALU.mult)
                    dve.drain()
                    if i < KQ // 2:
                        rows = slice((1 - h) * D, (2 - h) * D)
                        dst = hi = k_st[rows, slot, h, cols]
                    else:
                        rows = slice(h * D, (h + 1) * D)
                        dst, hi = q_lo[rows, slot, cols], hi[rows]
                    src = ps_p[i % 2][rows, :]
                    nc.vector.scalar_tensor_tensor(dst, src, DOWN, hi, ALU.mult, ALU.subtract).then_inc(S["p_read"], 1)
                else:
                    c = (i - KQ) * 4
                    nc.vector.tensor_scalar(v_st[:, slot, c:c + 4, :, :].rearrange("p c h f -> p (c h f)"), ps_p[i % 2][:, :],
                                            1.0 / (X_UP * W_UP), None, ALU.mult).then_inc(S["p_read"], 1)

            def pair(n, hp, slot):
                before = CHUNKS - FIRST_JJ
                for ih in range(IH):
                    for i in range(ih * before, (before, PB)[ih]):
                        split(i, 1 - slot, n * PB + PB)
                    dve.wait_ge(S["pv_mm"], n * JJ + (ih + 1) * CHUNKS)
                    dst = ctxT[:, bass.ds(hp, 1), ih * 2 * BLK:(ih + 1) * 2 * BLK].squeeze(1)
                    nc.vector.tensor_copy(dst, ps_o[:, :, :].rearrange("p a b -> p (a b)")).then_inc(S["o_read"], 1)

            dve.nop().then_inc(S["o_read"], 1)
            for i in range(PB):
                split(i, 0, 0)
            with dve.Fori(0, BATCH) as b:
                with dve.Fori(0, PAIRS // 2) as hh:
                    n = b * PAIRS + hh * 2
                    pair(n, hh * 2, 0)
                    pair(n + 1, hh * 2 + 1, 1)
                for k in range(2):
                    dve.wait_ge(S["wo_mm"], 2 * b + k + 1)
                    tiles = resid[:, bass.ds(b * CHUNKS + 8 * k, 8), :]
                    nc.vector.scalar_tensor_tensor(tiles, ps_p[k][:, :].rearrange("p (t o) -> p t o", o=D), 0.0, tiles,
                                                   ALU.max, ALU.add).then_inc(S["wo_read"], 1)


def routed_mlp(nc, m, A, resid, ident, flip):
    HID = A["L1_ffn_w1"].shape[1]
    MT = HID // P
    TAKE = SEQ // 2 - 1
    ROUNDS_PER = 5
    BLK = 4 * P
    HALF = TILES // 2
    NBLK = HALF * P // BLK
    ROUNDS = ROUNDS_PER * NBLK

    x = m.sb("x", [P, HALF, 2, D])
    x_t = x[:, :, :, :].rearrange("p t a d -> p a t d")
    xT = m.sb("xT", [P, HALF * P])
    y = m.sb("y", [P, TILES, D])
    w = m.sb("w", [P, TILES])
    w1 = m.sb("w1", [P, 2, HID])
    w2 = m.sb("w2", [P, MT, D])
    b1 = m.sb("b1", [P, MT])
    b2 = m.sb("b2", [P, D])
    wr = m.sb("wr", [P, D])
    br = m.sb("br", [P, 1])
    ones = m.sb("ones", [P, P])
    after = m.sb("after", [P, P])
    bound = m.sb("bound", [P, BATCH])
    step = m.sb("step", [P, BATCH])
    low = m.sb("low", [P, BATCH])

    with ExitStack() as stack:
        pm = Memory(nc, stack, "route")
        square = pm.sb("square", [P, TILES, D])
        stat = pm.sb("stat", [P, 3, TILES])
        stat4 = stat[:, :, :].rearrange("p s (a t) -> p s a t", a=2)
        top = pm.sb("top", [P, BATCH])
        ps_x = [pm.ps(f"ps_x{i}", [P, BLK]) for i in range(2)]
        loaded, made, root_in, root_out, x_ok, x_tr, xT_ok, top_in, top_out = map(pm.sem, (
            "loaded", "made", "root_in", "root_out", "x_ok", "x_tr", "xT_ok", "top_in", "top_out"))
        with nc.Block() as block:

            @block.sync
            def _(sp):
                loads = [(w2[:, :, :], A["L1_ffn_w2"].rearrange("(m p) d -> p m d", p=P)),
                         (b2[:, :], A["L1_ffn_b2"].partition_broadcast(P)),
                         (wr[:, :], A["L1_ffn_wr"].rearrange("d o -> (d o)").partition_broadcast(P)),
                         (br[:, :], A["L1_ffn_br"].partition_broadcast(P))]
                loads += [(b1[:, k:k + 1], A["L1_ffn_b1"][k * P:(k + 1) * P].unsqueeze(1)) for k in range(MT)]
                for dst, src in loads:
                    sp.dma_start(dst, src).then_inc(loaded, 16)
                sp.wait_ge(made, 1)
                for k in range(2):
                    sp.dma_start(w1[k * D:(k + 1) * D, k, :], A["L1_ffn_w1"]).then_inc(loaded, 16)
                sp.wait_ge(loaded, 16 * (6 + MT))

            @block.gpsimd
            def _(pool):
                nc.gpsimd.memset(w1[:, :, :], 0.0).then_inc(made, 1)
                pool.wait_ge(made, 1)
                nc.gpsimd.memset(ones[:, :], 1.0).then_inc(made, 1)
                pool.wait_ge(made, 2)
                nc.gpsimd.affine_select(out=after[:, :], in_=ones[:, :], compare_op=ALU.is_gt, fill=0.0,
                                        base=0, pattern=[[-1, P]], channel_multiplier=1).then_inc(made, 1)
                pool.wait_ge(made, 3)
                pool.wait_ge(top_in, 1)
                nc.gpsimd.partition_all_reduce(bound[:, :], top[:, :], P, bass.bass_isa.ReduceOp.max).then_inc(top_out, 1)
                pool.wait_ge(top_out, 1)
                nc.gpsimd.tensor_tensor(resid[:, 0:HALF, :], resid[:, 0:HALF, :], x[:, :, 0, :], ALU.add)
                nc.gpsimd.tensor_tensor(resid[:, HALF:TILES, :], resid[:, HALF:TILES, :], x[:, :, 1, :], ALU.add)

            @block.scalar
            def _(act):
                act.wait_ge(root_in, 1)
                nc.scalar.activation(stat[:, 2], stat[:, 1], ACT.Sqrt).then_inc(root_out, 1)
                for k in range(NBLK):
                    act.wait_ge(x_tr, k + 1)
                    nc.scalar.activation(xT[:, k * BLK:(k + 1) * BLK], ps_x[k % 2][:, :], ACT.Copy).then_inc(xT_ok, 1)

            @block.vector
            def _(dve):
                def root():
                    dve.drain()
                    dve.nop().then_inc(root_in, 1)
                    dve.wait_ge(root_out, 1)

                sq_t = square[:, :, :].rearrange("p (a t) d -> p a t d", a=2)
                layer_norm(nc, dve, x_t, resid[:, :, :].rearrange("p (a t) d -> p a t d", a=2), x_t, sq_t, stat4, LN_EPS, root)
                dve.drain()
                dve.nop().then_inc(x_ok, 1)
                dve.wait_ge(loaded, 16 * (6 + MT))
                for a in range(2):
                    nc.vector.tensor_tensor(sq_t[:, a], x_t[:, a], wr[:, :].unsqueeze(1).broadcast_to([P, HALF, D]), ALU.mult)
                dve.drain()
                nc.vector.tensor_reduce(out=w[:, :], in_=square[:, :, :], axis=AX.X, op=ALU.add)
                dve.drain()
                nc.vector.tensor_scalar(w[:, :], w[:, :], br[:, :], None, ALU.add)
                dve.drain()
                nc.vector.tensor_reduce(out=top[:, :], in_=w[:, :].rearrange("p (b c) -> p b c", c=CHUNKS), axis=AX.X,
                                        op=ALU.max, apply_absolute_value=True)
                dve.drain()
                dve.nop().then_inc(top_in, 1)
                dve.wait_ge(top_out, 1)
                nc.vector.tensor_scalar(bound[:, :], bound[:, :], 1.001, 1e-30, ALU.mult, ALU.add)
                dve.drain()
                nc.vector.tensor_scalar(low[:, :], bound[:, :], -1.0, None, ALU.mult)
                nc.vector.tensor_copy(step[:, :], bound[:, :])

            @block.tensor
            def _(pe):
                pe.wait_ge(x_ok, 1)
                for k in range(NBLK):
                    if k >= 2:
                        pe.wait_ge(xT_ok, k - 1)
                    for j in range(4):
                        last = nc.tensor.transpose(ps_x[k % 2][:, j * P:(j + 1) * P],
                                                   x[:, 4 * k + j, :, :].rearrange("p a d -> p (a d)"), ident[:, :])
                    last.then_inc(x_tr, 1)

    hT = m.sb("hT", [P, 2, MT, BLK])
    mid = m.sb("mid", [P, BATCH])
    least = m.sb("least", [P, TILES])
    over = m.sb("over", [P, TILES])
    n_here = m.sb("n_here", [P, BATCH])
    rise = m.sb("rise", [P, BATCH])
    n_over = m.sb("n_over", [P, BATCH])
    tied = m.sb("tied", [P, TILES])
    rank = m.sb("rank", [P, TILES])
    total = m.sb("total", [P, TILES])
    carry = m.sb("carry", [P, TILES])
    in_row = m.sb("in_row", [P, TILES])
    ps_h = [m.ps(f"ps_h{i}", [P, BLK]) for i in range(2)]
    ps_y = [m.ps(f"ps_y{i}", [P, 4, D]) for i in range(2)]
    ps_n = m.ps("ps_n", [P, BATCH])
    ps_r = m.ps("ps_r", [P, 2, TILES])
    names = ("h_mm", "h_ok", "y_mm", "y_ok", "count_in", "count_mm", "rank_in", "rank_mm")
    S = {n: m.sem(n) for n in names}

    with nc.Block() as block:

        @block.tensor
        def _(pe):
            with pe.Fori(0, NBLK) as k:
                rounds = iter(range(ROUNDS_PER))

                def count():
                    i = next(rounds, None)
                    if i is not None:
                        pe.wait_ge(S["count_in"], k * ROUNDS_PER + i + 1)
                        nc.tensor.matmul(ps_n[:, :], ones[:, :], n_here[:, :], start=True, stop=True).then_inc(S["count_mm"], 1)

                for a in range(2):
                    if a:
                        count()
                    for j in range(MT):
                        pe.wait_ge(S["h_ok"], k * (2 * MT) + a * MT + j + 1)
                        nc.tensor.matmul(ps_h[j][:, :], w1[:, a, j * P:(j + 1) * P], xT[:, bass.ts(k, BLK)],
                                         start=True, stop=True).then_inc(S["h_mm"], 1)
                        count()
                    pe.wait_ge(S["h_ok"], k * (2 * MT) + (a + 1) * MT + MT)
                    pe.wait_ge(S["y_ok"], k * 2 + a + 1)
                    for i in range(4):
                        for j in range(MT):
                            last = nc.tensor.matmul(ps_y[a][:, i, :], hT[:, a, j, i * P:(i + 1) * P], w2[:, j, :],
                                                    start=j == 0, stop=j == MT - 1)
                    last.then_inc(S["y_mm"], 1)
                assert next(rounds, None) is None
            pe.wait_ge(S["count_in"], ROUNDS + 1)
            nc.tensor.matmul(ps_n[:, :], ones[:, :], n_here[:, :], start=True, stop=True).then_inc(S["count_mm"], 1)
            pe.wait_ge(S["rank_in"], 1)
            nc.tensor.matmul(ps_r[:, 0, :], after[:, :], tied[:, :], start=True, stop=True)
            nc.tensor.matmul(ps_r[:, 1, :], ones[:, :], tied[:, :], start=True, stop=True).then_inc(S["rank_mm"], 1)

        @block.scalar
        def _(act):
            def copy_y(k, a):
                act.wait_ge(S["y_mm"], k * 2 + a + 1)
                nc.scalar.activation(y[:, bass.ds(k * 4 + a * HALF, 4), :], ps_y[a][:, :, :], ACT.Copy).then_inc(S["y_ok"], 1)

            act.preload_act_table(ACT.Gelu_apprx_tanh)
            act.nop().then_inc(S["h_ok"], MT)
            act.nop().then_inc(S["y_ok"], 2)
            with act.Fori(0, NBLK) as k:
                for a in range(2):
                    for j in range(MT):
                        act.wait_ge(S["h_mm"], k * (2 * MT) + a * MT + j + 1)
                        nc.scalar.activation(hT[:, a, j, :], ps_h[j][:, :], ACT.Gelu_apprx_tanh, bias=b1[:, j:j + 1]).then_inc(S["h_ok"], 1)
                    if a:
                        copy_y(k, 0)
                copy_y(k, 1)

        @block.vector
        def _(dve):
            w_b = w[:, :].rearrange("p (b c) -> p b c", c=CHUNKS)
            least_b = least[:, :].rearrange("p (b c) -> p b c", c=CHUNKS)
            over_b = over[:, :].rearrange("p (b c) -> p b c", c=CHUNKS)

            def count(marks, bar):
                nc.vector.tensor_tensor(marks, w_b, over_last(bar[:, :], CHUNKS), ALU.is_ge)
                dve.drain()
                nc.vector.tensor_reduce(out=n_here[:, :], in_=marks, axis=AX.X, op=ALU.add)
                dve.drain()
                dve.nop().then_inc(S["count_in"], 1)

            nc.vector.memset(in_row[:, :], 1.0)
            dve.drain()
            nc.vector.memset(in_row[:, :].rearrange("p (b c) -> p b c", c=CHUNKS)[:, :, 0], 0.0)
            with dve.Fori(0, ROUNDS) as r:
                nc.vector.tensor_tensor(mid[:, :], low[:, :], step[:, :], ALU.add)
                dve.drain()
                count(least_b, mid)
                dve.wait_ge(S["count_mm"], r + 1)
                nc.vector.scalar_tensor_tensor(rise[:, :], ps_n[:, :], float(TAKE), step[:, :], ALU.is_ge, ALU.mult)
                dve.drain()
                nc.vector.tensor_tensor(low[:, :], low[:, :], rise[:, :], ALU.add)
                nc.vector.tensor_scalar(step[:, :], step[:, :], 0.5, None, ALU.mult)
                dve.drain()
            nc.vector.scalar_tensor_tensor(mid[:, :], step[:, :], 2.0, low[:, :], ALU.mult, ALU.add)
            nc.vector.tensor_tensor(least_b, w_b, over_last(low[:, :], CHUNKS), ALU.is_ge)
            dve.drain()
            count(over_b, mid)
            nc.vector.tensor_tensor(tied[:, :], least[:, :], over[:, :], ALU.subtract)
            dve.drain()
            dve.nop().then_inc(S["rank_in"], 1)
            dve.wait_ge(S["count_mm"], ROUNDS + 1)
            nc.vector.tensor_scalar(n_over[:, :], ps_n[:, :], -1.0, float(TAKE), ALU.mult, ALU.add)
            dve.wait_ge(S["rank_mm"], 1)
            nc.vector.tensor_copy(total[:, :], ps_r[:, 1, :])
            dve.drain()
            nc.vector.tensor_tensor_scan(carry[:, :], in_row[:, :], total[:, :], 0.0, ALU.mult, ALU.add)
            dve.drain()
            nc.vector.tensor_tensor(carry[:, :], carry[:, :], total[:, :], ALU.subtract)
            dve.drain()
            nc.vector.tensor_tensor(rank[:, :], ps_r[:, 0, :], carry[:, :], ALU.add)
            dve.drain()
            nc.vector.tensor_tensor(rank[:, :].rearrange("p (b c) -> p b c", c=CHUNKS), rank[:, :].rearrange("p (b c) -> p b c", c=CHUNKS),
                                    over_last(n_over[:, :], CHUNKS), ALU.is_lt)
            dve.drain()
            nc.vector.tensor_tensor(tied[:, :], tied[:, :], rank[:, :], ALU.mult)
            dve.drain()
            nc.vector.tensor_tensor(tied[:, :], tied[:, :], over[:, :], ALU.add)
            dve.drain()
            nc.vector.tensor_tensor(w[:, :], w[:, :], tied[:, :], ALU.mult)
            dve.wait_ge(S["y_ok"], 2 * NBLK + 2)
            nc.vector.tensor_tensor(y[:, :, :], y[:, :, :], b2[:, :].unsqueeze(1).broadcast_to([P, TILES, D]), ALU.add)
            dve.drain()
            nc.vector.tensor_tensor(y[:, :, :], y[:, :, :], over_last(w[:, :], D), ALU.mult)
            dve.drain()
            nc.vector.tensor_tensor(resid[:, :, :], resid[:, :, :], y[:, :, :], ALU.add)


def store_result(nc, m, resid, flip, out):
    PER = 512 // D
    N = TILES // PER
    turned = m.sb("turned", [P, TILES, D])
    ps = [m.ps(f"ps{i}", [P, PER, D]) for i in range(4)]
    flipped, copied, stored = m.sem("flipped"), m.sem("copied"), m.sem("stored")
    out_v = out.rearrange("b (c p) d -> p (b c) d", p=P)
    with nc.Block() as block:

        @block.tensor
        def _(pe):
            for k in range(N):
                if k >= 4:
                    pe.wait_ge(copied, k - 3)
                nc.tensor.matmul(ps[k % 4][:, :, :], flip[:, :], resid[:, k * PER:(k + 1) * PER, :],
                                 start=True, stop=True).then_inc(flipped, 1)

        @block.vector
        def _(dve):
            for k in range(N):
                dve.wait_ge(flipped, k + 1)
                nc.vector.tensor_copy(turned[:, k * PER:(k + 1) * PER, :], ps[k % 4][:, :, :]).then_inc(copied, 1)

        @block.sync
        def _(sp):
            for k in range(N):
                sp.wait_ge(copied, k + 1)
                sp.dma_start(out_v[:, k * PER:(k + 1) * PER, :], turned[:, k * PER:(k + 1) * PER, :]).then_inc(stored, 16)
            sp.wait_ge(stored, 16 * N)


def tower(nc, A, out, phases=5):
    with ExitStack() as whole:
        shared = Memory(nc, whole, "all")
        resid = shared.sb("resid", [P, TILES, D])
        ident, flip = constants(nc, shared)
        todo = [embed_tokens, state_space_layers, expert_mixture, sigmoid_attention, routed_mlp][:phases]
        for phase in todo:
            with ExitStack() as stack:
                phase(nc, Memory(nc, stack, phase.__name__), A, resid, ident, flip)
        with ExitStack() as stack:
            store_result(nc, Memory(nc, stack, "end"), resid, flip, out)


def kernel(**inputs):
    import concourse.bacc as bacc
    import numpy as np
    from concourse.bass_utils import run_bass_kernel_spmd

    nc = bacc.Bacc("TRN2", target_bir_lowering=False, num_devices=1)
    arrays, args = {}, {}
    given = {k: np.ascontiguousarray(v) for k, v in inputs.items()}
    tables = ["L0_tok_emb_table", "L0_tok_geo_table", "L0_tok_visit_table"]
    given["rows"] = np.concatenate([given.pop(t) for t in tables], axis=1)
    for name, a in given.items():
        arrays[f"in_{name}"] = a
        args[name] = nc.dram_tensor(f"in_{name}", a.shape, mybir.dt.from_np(a.dtype), kind="ExternalInput").ap()
    out = nc.dram_tensor("out_h", (BATCH, SEQ, D), F32, kind="ExternalOutput").ap()
    tower(nc, args, out)
    r = run_bass_kernel_spmd(nc, [arrays], core_ids=[0])
    return r.results[0]["out_h"]
```

```python
from contextlib import ExitStack

import concourse.bass as bass
from concourse import mybir

F32 = mybir.dt.float32
F16 = mybir.dt.float16
BF16 = mybir.dt.bfloat16
I32 = mybir.dt.int32
ACT = mybir.ActivationFunctionType
ALU = mybir.AluOpType
AX = mybir.AxisListType

P = 128
BATCH, SEQ, D = 4, 2048, 64
CHUNKS = SEQ // P
TILES = BATCH * CHUNKS
VISIT = 24
ROW = D + D + VISIT
LAST_ID = 25000
LN_EPS = 1e-5


class Memory:

    def __init__(self, nc, stack, name):
        self.nc, self.stack, self.name = nc, stack, name

    def sb(self, name, shape, dt=F32):
        return self.stack.enter_context(self.nc.sbuf_tensor(f"{self.name}_{name}", shape, dt))

    def ps(self, name, shape, dt=F32):
        return self.stack.enter_context(self.nc.psum_tensor(f"{self.name}_{name}", shape, dt))

    def sem(self, name):
        return self.stack.enter_context(self.nc.semaphore(f"{self.name}_{name}"))


def over_last(ap, n):
    return ap.unsqueeze(len(ap.shape)).broadcast_to(list(ap.shape) + [n])


def layer_norm(nc, e, out, x, centred, square, stat, eps, scaled=None):
    n = x.shape[-1]
    nc.vector.tensor_reduce(out=stat[:, 0], in_=x, axis=AX.X, op=ALU.add)
    e.drain()
    nc.vector.tensor_scalar(stat[:, 0], stat[:, 0], 1.0 / n, None, ALU.mult)
    e.drain()
    nc.vector.tensor_tensor(centred, x, over_last(stat[:, 0], n), ALU.subtract)
    e.drain()
    nc.vector.tensor_tensor(square, centred, centred, ALU.mult)
    e.drain()
    nc.vector.tensor_reduce(out=stat[:, 1], in_=square, axis=AX.X, op=ALU.add)
    e.drain()
    nc.vector.tensor_scalar(stat[:, 1], stat[:, 1], 1.0 / n, eps, ALU.mult, ALU.add)
    scaled()
    nc.vector.reciprocal(stat[:, 0], stat[:, 2])
    e.drain()
    nc.vector.tensor_tensor(out, centred, over_last(stat[:, 0], n), ALU.mult)


def constants(nc, m):
    ident = m.sb("ident", [P, P])
    flip = m.sb("flip", [P, P])
    made = m.sem("ident_made")
    with nc.Block() as block:

        @block.gpsimd
        def _(pool):
            nc.gpsimd.memset(ident[:, :], 0.0).then_inc(made, 1)
            pool.wait_ge(made, 1)
            nc.gpsimd.affine_select(out=ident[:, :], in_=ident[:, :], compare_op=ALU.not_equal, fill=1.0,
                                    base=0, pattern=[[-1, P]], channel_multiplier=1).then_inc(made, 1)
            pool.wait_ge(made, 2)
            nc.gpsimd.memset(flip[:, :], 0.0).then_inc(made, 1)
            pool.wait_ge(made, 3)
            nc.gpsimd.affine_select(out=flip[:, :], in_=flip[:, :], compare_op=ALU.not_equal, fill=1.0,
                                    base=1 - P, pattern=[[1, P]], channel_multiplier=1).then_inc(made, 1)
            pool.wait_ge(made, 4)
    return ident, flip


LAYERS = 4
MAGIC = 1.5 * 2 ** 23
TURN = 6.2831845
QUARTER = TURN / 4


def of_layer(columns, l):
    return columns[:, l, :] if isinstance(l, int) else columns[:, bass.ds(l, 1), :].squeeze(1)


class PolePowers:
    PAIRS = D // 2
    HALF = PAIRS // 2

    def __init__(self, nc, m):
        self.nc = nc
        self.powers = m.sb("powers", [P, 2, self.PAIRS, 2, P])
        self.angle = m.sb("angle", [P, 2, self.HALF * P])
        self.decay = m.sb("decay", [P, self.HALF * P])
        self.cols = m.sb("cols", [P, 4, LAYERS, self.PAIRS])
        self.kk = m.sb("kk", [P, P])
        self.quarter = m.sb("quarter", [P, 1])
        self.reduced, self.trig, self.powers_ok = m.sem("reduced"), m.sem("trig"), m.sem("powers_ok")

    def gpsimd(self, pool, l, parity, half, done):
        nc, HALF = self.nc, self.HALF
        pairs = slice(half * HALF, (half + 1) * HALF)
        turns = self.angle[:, 0, :].rearrange("p (q i) -> p q i", i=P)
        other = self.angle[:, 1, :].rearrange("p (q i) -> p q i", i=P)
        decay = self.decay[:, :].rearrange("p (q i) -> p q i", i=P)
        k3 = self.kk[:, :].unsqueeze(1).broadcast_to([P, HALF, P])
        f, a = [of_layer(self.cols[:, i], l)[:, pairs] for i in range(2)]
        nc.gpsimd.tensor_tensor(turns, k3, over_last(f, P), ALU.mult)
        nc.gpsimd.tensor_tensor(decay, k3, over_last(a, P), ALU.mult)
        pool.drain()
        nc.gpsimd.tensor_scalar(other, turns, MAGIC, MAGIC, ALU.add, ALU.subtract)
        pool.drain()
        nc.gpsimd.tensor_tensor(turns, turns, other, ALU.subtract)
        pool.drain()
        pool.nop().then_inc(self.reduced, 1)
        pool.wait_ge(self.trig, done + 1)
        nc.gpsimd.tensor_tensor(self.powers[:, parity, pairs, 0, :], decay, other, ALU.mult)
        nc.gpsimd.tensor_tensor(self.powers[:, parity, pairs, 1, :], decay, turns, ALU.mult)
        pool.drain()
        pool.nop().then_inc(self.powers_ok, 1)

    def scalar(self, act, done):
        nc, angle = self.nc, self.angle
        act.wait_ge(self.reduced, done + 1)
        nc.scalar.activation(angle[:, 1, :], angle[:, 0, :], ACT.Abs)
        act.drain()
        nc.scalar.activation(angle[:, 1, :], angle[:, 1, :], ACT.Sin, scale=-TURN, bias=self.quarter[:, :])
        nc.scalar.activation(angle[:, 0, :], angle[:, 0, :], ACT.Sin, scale=-TURN)
        nc.scalar.activation(self.decay[:, :], self.decay[:, :], ACT.Exp)
        act.drain()
        act.nop().then_inc(self.trig, 1)


def pole_parameters(nc, m, A, ident, pw):
    PAIRS = D // 2
    N2 = 2 * D
    cols, kk, quarter = pw.cols, pw.kk, pw.quarter
    dram_k = nc.dram_tensor("kernel_rows", (LAYERS, D, 2 * P), F32)
    k_ap = dram_k.ap()
    zrow = m.sb("zrow", [P, 2, P])
    k0 = m.sb("k0", [P, 2])
    names = ["alog", "aim", "cre", "cim", "x", "f", "r", "q1", "sn", "cs", "sh", "th", "zr", "zi", "den", "ta", "tb",
             "qr", "qi", "cdr", "cdi", "ar"] + [f"twice{i}" for i in range(8)]
    slots = {n: m.sb(n, [P, N2])[:, :] for n in names}

    def v3(n):
        return slots[n].rearrange("p (l n) -> p l n", n=D)

    ldt = m.sb("ldt", [P, 2])
    dt = m.sb("dt", [P, 2])
    dskip = m.sb("dskip", [P, 2])
    ps_q = m.ps("ps_q", [P, 4, P])
    loaded, made, zero, trig_in, trig_out, ready, tr_done, tr_read, zeros_out = map(m.sem, (
        "loaded", "made", "zero", "trig_in", "trig_out", "ready", "tr_done", "tr_read", "zeros_out"))

    def load(sp):
        for n, src in (("alog", "Alog"), ("aim", "Aim"), ("cre", "Cre"), ("cim", "Cim")):
            sp.dma_start(v3(n), A["L0_attn_" + src].rearrange("(l k) h n -> (k h) l n", k=2)).then_inc(loaded, 16)
        for dst, src in ((ldt, "log_dt"), (dskip, "D")):
            for i in range(2):
                sp.dma_start(dst[:, i:i + 1], A["L0_attn_" + src][2 * i:2 * i + 2, :].rearrange("k h -> (k h)").unsqueeze(1)).then_inc(loaded, 16)

    def store_zeros(sp):
        sp.wait_ge(zero, 1)
        sp.dma_start(k_ap.rearrange("(l k) h x -> (k h) l x", k=2)[:, :, 1:P + 1], zrow[:, :, :]).then_inc(zeros_out, 16)
        sp.wait_ge(zeros_out, 16)

    def gpsimd(pool):
        nc.gpsimd.iota(kk[:, :], pattern=[[1, P]], base=0, channel_multiplier=0,
                       allow_small_or_imprecise_dtypes=True).then_inc(made, 1)
        pool.wait_ge(made, 1)
        nc.gpsimd.memset(quarter[:, :], QUARTER).then_inc(made, 1)
        pool.wait_ge(made, 2)

    def scalar(act):
        act.wait_ge(loaded, 128)
        nc.scalar.activation(dt[:, :], ldt[:, :], ACT.Exp)
        nc.scalar.activation(slots["ar"], slots["alog"], ACT.Exp).then_inc(trig_out, 1)
        act.wait_ge(trig_in, 1)
        nc.scalar.activation(slots["th"], slots["x"], ACT.Tanh, scale=0.5)
        nc.scalar.activation(slots["q1"], slots["r"], ACT.Abs)
        act.drain()
        act.wait_ge(made, 2)
        nc.scalar.activation(slots["cs"], slots["q1"], ACT.Sin, scale=-TURN, bias=quarter[:, :])
        nc.scalar.activation(slots["sn"], slots["r"], ACT.Sin, scale=TURN)
        nc.scalar.activation(slots["sh"], slots["r"], ACT.Sin, scale=TURN / 2)
        act.drain()
        act.nop().then_inc(trig_out, 1)

    def vector(dve):
        def tt(o, a, b, op):
            nc.vector.tensor_tensor(slots[o], slots[a], slots[b], op)
            dve.drain()

        def ts(o, a, c0, c1, op0, op1=None):
            if op1 is None:
                nc.vector.tensor_scalar(slots[o], slots[a], c0, c1, op0)
            else:
                nc.vector.tensor_scalar(slots[o], slots[a], c0, c1, op0, op1)
            dve.drain()

        dve.wait_ge(loaded, 128)
        dve.wait_ge(trig_out, 1)
        ts("ar", "ar", -1.0, None, ALU.mult)
        nc.vector.tensor_tensor(v3("x"), v3("ar"), over_last(dt[:, :], D), ALU.mult)
        nc.vector.tensor_tensor(v3("f"), v3("aim"), over_last(dt[:, :], D), ALU.mult)
        dve.drain()
        ts("f", "f", 1.0 / 6.283185307179586, None, ALU.mult)
        ts("ta", "f", MAGIC, MAGIC, ALU.add, ALU.subtract)
        tt("r", "f", "ta", ALU.subtract)
        dve.nop().then_inc(trig_in, 1)
        tt("den", "ar", "ar", ALU.mult)
        tt("ta", "aim", "aim", ALU.mult)
        tt("den", "den", "ta", ALU.add)
        nc.vector.reciprocal(slots["den"], slots["den"])
        dve.drain()
        dve.wait_ge(trig_out, 2)
        ts("ta", "th", -1.0, 1.0, ALU.mult, ALU.add)
        nc.vector.reciprocal(slots["ta"], slots["ta"])
        dve.drain()
        tt("th", "th", "ta", ALU.mult)
        ts("th", "th", 2.0, None, ALU.mult)
        tt("zr", "th", "cs", ALU.mult)
        tt("sh", "sh", "sh", ALU.mult)
        nc.vector.scalar_tensor_tensor(slots["zr"], slots["sh"], -2.0, slots["zr"], ALU.mult, ALU.add)
        nc.vector.scalar_tensor_tensor(slots["zi"], slots["th"], 1.0, slots["sn"], ALU.add, ALU.mult)
        dve.drain()

        def complex_mul(orr, oi, ar_, ai, br, bi, conj):
            tt("ta", ar_, br, ALU.mult)
            tt("tb", ai, bi, ALU.mult)
            tt(orr, "ta", "tb", ALU.add if conj else ALU.subtract)
            tt("ta", ai, br, ALU.mult)
            tt("tb", ar_, bi, ALU.mult)
            tt(oi, "ta", "tb", ALU.subtract if conj else ALU.add)

        complex_mul("qr", "qi", "zr", "zi", "ar", "aim", True)
        tt("qr", "qr", "den", ALU.mult)
        tt("qi", "qi", "den", ALU.mult)
        complex_mul("cdr", "cdi", "cre", "cim", "qr", "qi", False)
        ts("cdr", "cdr", 2.0, None, ALU.mult)
        ts("cdi", "cdi", 2.0, None, ALU.mult)
        nc.vector.tensor_reduce(out=k0[:, :], in_=v3("cdr"), axis=AX.X, op=ALU.add)
        nc.vector.memset(zrow[:, :, :], 0.0)
        dve.drain()
        nc.vector.tensor_tensor(zrow[:, :, P - 1], k0[:, :], dskip[:, :], ALU.add)
        dve.drain()
        dve.nop().then_inc(zero, 1)
        for i, n in enumerate(("f", "x", "cdr", "cdi")):
            for half in range(2):
                nc.vector.tensor_copy(v3(f"twice{2 * i + half}"), v3(n)[:, half, :].unsqueeze(1).broadcast_to([P, 2, D]))
        dve.drain()
        dve.nop().then_inc(ready, 1)
        for half in range(2):
            dve.wait_ge(tr_done, half + 1)
            for par in range(2):
                side = slice(par * D, (par + 1) * D)
                for k in range(2):
                    nc.vector.tensor_copy(cols[side, :, 2 * half + k, :],
                                          ps_q[side, :, k * D + par:(k + 1) * D:2])
            dve.drain()
            dve.nop().then_inc(tr_read, 1)

    def tensor(pe):
        pe.wait_ge(ready, 1)
        for half in range(2):
            if half:
                pe.wait_ge(tr_read, half)
            for i in range(4):
                last = nc.tensor.transpose(ps_q[:, i, :], slots[f"twice{2 * i + half}"], ident[:, :])
            last.then_inc(tr_done, 1)

    return dram_k, (load, store_zeros, gpsimd, scalar, vector, tensor)


def embed_tokens(nc, m, A, resid, ident, pole_programs, pw):
    poles_load, poles_zeros, poles_gpsimd, poles_scalar, poles_vector, poles_tensor = pole_programs
    GROUP = 4
    RING = 4
    NG = TILES // GROUP
    GT = GROUP * P

    ids = m.sb("ids", [TILES, P], I32)
    idf = m.sb("idf", [TILES, 2, P])
    index = m.sb("index", [P, TILES], I32)
    keep = m.sb("keep", [P, TILES])
    rows = m.sb("rows", [P, RING * GROUP, ROW])
    w_ig = m.sb("w_ig", [P, P])
    w_v = m.sb("w_v", [VISIT, D])
    w_f1 = m.sb("w_f1", [P, D])
    w_f2 = m.sb("w_f2", [D + 1, D])
    b_ig = m.sb("b_ig", [P, 1])
    b_v = m.sb("b_v", [D, 1])
    gamma = m.sb("gamma", [P, D])
    beta = m.sb("beta", [P, D])
    featT = m.sb("featT", [P, 2, GT])
    visitT = m.sb("visitT", [VISIT, 2, GT])
    hidT = m.sb("hidT", [P, 2, GT])
    hidvT = m.sb("hidvT", [D + 1, 2, GT])
    fused = m.sb("fused", [P, TILES, D])
    square = m.sb("square", [P, GROUP, D])
    shift = m.sb("shift", [P, GROUP, D])
    stat = m.sb("stat", [P, 3, TILES])
    ps_ids = m.ps("ps_ids", [P, 2, TILES])
    ps_feat = m.ps("ps_feat", [P, GT])
    ps_visit = m.ps("ps_visit", [VISIT, GT])
    ps_h = [m.ps(f"ps_h{i}", [P, GT]) for i in range(1)]
    ps_hv = [m.ps(f"ps_hv{i}", [D, GT]) for i in range(1)]
    ps_f = [m.ps(f"ps_f{i}", [P, GROUP, D]) for i in range(2)]

    zeroed, loaded, ids_in, clipped, ids_tr, index_ok = map(m.sem, ("zeroed", "loaded", "ids_in", "clipped", "ids_tr", "index_ok"))
    gathered = [m.sem(f"gathered{r}") for r in range(RING)]
    rows_used, feat_tr, feat_sb, proj, hid_ok, fuse_mm, fuse_ok, emb_ok, root_in, root_out = map(m.sem, (
        "rows_used", "feat_tr", "feat_sb", "proj", "hid_ok", "fuse_mm", "fuse_ok", "emb_ok", "root_in", "root_out"))
    N_LOADS = 11

    with nc.Block() as block:

        @block.sync
        def _(sp):
            sp.dma_start(ids[:, :], A["x"].rearrange("b (c p) -> (b c) p", p=P)).then_inc(ids_in, 16)
            poles_load(sp)
            sp.wait_ge(zeroed, 1)
            for dst, src in ((w_ig[0:D, 0:D], A["L0_tok_w_item"]), (w_ig[D:P, D:P], A["L0_tok_w_geo"]),
                             (w_v[:, :], A["L0_tok_w_visit"]),
                             (w_f1[:, :], A["L0_tok_w_fuse"][0:P, :]), (w_f2[0:D, :], A["L0_tok_w_fuse"][P:P + D, :]),
                             (w_f2[D:D + 1, :], A["L0_tok_b_fuse"].unsqueeze(0)),
                             (b_ig[0:D, :], A["L0_tok_b_item"].unsqueeze(1)), (b_ig[D:P, :], A["L0_tok_b_geo"].unsqueeze(1)),
                             (b_v[:, :], A["L0_tok_b_visit"].unsqueeze(1)),
                             (gamma[:, :], A["L0_tok_ln_gamma"].partition_broadcast(P)),
                             (beta[:, :], A["L0_tok_ln_beta"].partition_broadcast(P))):
                sp.dma_start(dst, src).then_inc(loaded, 16)
            poles_zeros(sp)

        @block.gpsimd
        def _(pool):
            nc.gpsimd.memset(w_ig[:, :], 0.0).then_inc(zeroed, 1)
            pool.wait_ge(zeroed, 1)
            nc.gpsimd.memset(hidvT[D:D + 1, :, :], 1.0).then_inc(zeroed, 1)
            pool.wait_ge(zeroed, 2)
            poles_gpsimd(pool)
            pool.wait_ge(index_ok, 1)
            for t in range(TILES):
                g, r = t // GROUP, t // GROUP % RING
                if t % GROUP == 0 and g >= RING:
                    pool.wait_ge(rows_used, 2 * (g - RING + 1))
                nc.gpsimd.indirect_dma_start(
                    out=rows[:, t % (RING * GROUP), :], out_offset=None, in_=A["rows"],
                    in_offset=bass.IndirectOffsetOnAxis(ap=index[:, t:t + 1], axis=0)).then_inc(gathered[r], 16)
            pw.gpsimd(pool, 0, 0, 0, 0)

        @block.tensor
        def _(pe):
            pe.wait_ge(clipped, 1)
            nc.tensor.transpose(ps_ids[:, 0, :], idf[:, 0, :], ident[0:TILES, 0:TILES])
            nc.tensor.transpose(ps_ids[:, 1, :], idf[:, 1, :], ident[0:TILES, 0:TILES]).then_inc(ids_tr, 1)
            poles_tensor(pe)
            pe.wait_ge(loaded, 16 * N_LOADS)
            pe.wait_ge(zeroed, 2)

            def turn(r, count):
                pe.wait_ge(gathered[r], count)
                for k in range(GROUP):
                    nc.tensor.transpose(ps_feat[:, k * P:(k + 1) * P], rows[:, r * GROUP + k, 0:P], ident[:, :])
                for k in range(GROUP):
                    last = nc.tensor.transpose(ps_visit[:, k * P:(k + 1) * P], rows[:, r * GROUP + k, P:ROW], ident[:, :])
                last.then_inc(feat_tr, 1)

            def rounds(it, last_round):
                for r in range(RING):
                    g = it * RING + r
                    pe.wait_ge(feat_sb, 2 * g + 2)
                    nc.tensor.matmul(ps_h[0][:, :], w_ig[:, :], featT[:, r % 2, :], start=True, stop=True)
                    nc.tensor.matmul(ps_hv[0][:, :], w_v[:, :], visitT[:, r % 2, :], start=True, stop=True).then_inc(proj, 1)
                    if r < RING - 1:
                        turn(r + 1, (it + 1) * (16 * GROUP))
                    elif not last_round:
                        turn(0, (it + 2) * (16 * GROUP))
                    pe.wait_ge(hid_ok, g + 1)
                    for k in range(GROUP):
                        tok = slice(k * P, (k + 1) * P)
                        nc.tensor.matmul(ps_f[r % 2][:, k, :], hidT[:, r % 2, tok], w_f1[:, :], start=True, stop=False)
                        last = nc.tensor.matmul(ps_f[r % 2][:, k, :], hidvT[:, r % 2, tok], w_f2[:, :], start=False, stop=True)
                    last.then_inc(fuse_mm, 1)

            turn(0, 16 * GROUP)
            with pe.Fori(0, NG // RING - 1) as it:
                rounds(it, False)
            rounds(NG // RING - 1, True)

        @block.scalar
        def _(act):
            def visit(g, slot):
                act.wait_ge(feat_tr, g + 1)
                nc.scalar.activation(visitT[:, slot, :], ps_visit[:, :], ACT.Copy).then_inc(feat_sb, 1)

            def rounds(it, last_round):
                for r in range(RING):
                    g = it * RING + r
                    act.wait_ge(proj, g + 1)
                    nc.scalar.activation(hidT[:, r % 2, :], ps_h[0][:, :], ACT.Gelu, bias=b_ig[:, :])
                    nc.scalar.activation(hidvT[0:D, r % 2, :], ps_hv[0][:, :], ACT.Gelu, bias=b_v[:, :]).then_inc(hid_ok, 1)
                    if not (last_round and r == RING - 1):
                        visit(g + 1, (r + 1) % 2)
                    act.wait_ge(fuse_mm, g + 1)
                    tiles = slice(g * GROUP, (g + 1) * GROUP) if last_round else bass.ts(g, GROUP)
                    nc.scalar.activation(fused[:, tiles, :], ps_f[r % 2][:, :, :], ACT.Gelu).then_inc(fuse_ok, 1)

            poles_scalar(act)
            act.wait_ge(loaded, 16 * N_LOADS)
            visit(0, 0)
            with act.Fori(0, NG // RING - 1) as it:
                rounds(it, False)
            rounds(NG // RING - 1, True)
            act.wait_ge(root_in, 1)
            nc.scalar.activation(stat[:, 2], stat[:, 1], ACT.Sqrt).then_inc(root_out, 1)
            pw.scalar(act, 0)

        @block.vector
        def _(dve):
            dve.wait_ge(ids_in, 16)
            nc.vector.tensor_scalar(idf[:, 0, :], ids[:, ::-1], 0.0, float(LAST_ID), ALU.max, ALU.min)
            nc.vector.tensor_scalar(idf[:, 1, :], ids[:, ::-1], 0.0, None, ALU.not_equal)
            dve.drain()
            dve.nop().then_inc(clipped, 1)
            dve.wait_ge(ids_tr, 1)
            nc.vector.tensor_copy(index[:, :], ps_ids[:, 0, :]).then_inc(index_ok, 1)
            nc.vector.tensor_copy(keep[:, :], ps_ids[:, 1, :])
            dve.drain()
            nc.vector.tensor_scalar(keep[:, :], keep[:, :], 0.1, None, ALU.mult)
            poles_vector(dve)
            dve.wait_ge(loaded, 16 * N_LOADS)

            def take(g, r, tiles):
                dve.wait_ge(feat_tr, g + 1)
                nc.vector.tensor_copy(featT[:, r % 2, :], ps_feat[:, :]).then_inc(feat_sb, 1)
                nc.vector.tensor_copy(resid[:, tiles, :], rows[:, r * GROUP:(r + 1) * GROUP, 0:D]).then_inc(rows_used, 2)

            def norm(g, tiles):
                dve.wait_ge(fuse_ok, g + 1)
                mean, var, x = stat[:, 0, tiles], stat[:, 1, tiles], fused[:, tiles, :]
                bc = [P, GROUP, D]
                nc.vector.tensor_reduce(out=mean, in_=x, axis=AX.X, op=ALU.add)
                nc.vector.tensor_tensor(shift[:, :, :], beta[:, :].unsqueeze(1).broadcast_to(bc), over_last(keep[:, tiles], D), ALU.mult)
                dve.drain()
                nc.vector.tensor_scalar(mean, mean, 1.0 / D, None, ALU.mult)
                nc.vector.tensor_tensor(resid[:, tiles, :], resid[:, tiles, :], shift[:, :, :], ALU.add)
                dve.drain()
                nc.vector.tensor_tensor(x, x, over_last(mean, D), ALU.subtract)
                dve.drain()
                nc.vector.tensor_tensor(square[:, :, :], x, x, ALU.mult)
                dve.drain()
                nc.vector.tensor_reduce(out=var, in_=square[:, :, :], axis=AX.X, op=ALU.add)
                nc.vector.tensor_tensor(x, x, gamma[:, :].unsqueeze(1).broadcast_to(bc), ALU.mult)

            def group(n):
                return bass.ts(n, GROUP) if not isinstance(n, int) else slice(n * GROUP, (n + 1) * GROUP)

            LAG = 2
            for g in range(RING):
                take(g, g, group(g))
                if g >= LAG:
                    norm(g - LAG, group(g - LAG))
            with dve.Fori(1, NG // RING) as it:
                for r in range(RING):
                    g = it * RING + r
                    take(g, r, group(g))
                    norm(g - LAG, bass.ds((g - LAG) * GROUP, GROUP))
            for g in range(NG - LAG, NG):
                norm(g, group(g))
            dve.drain()
            nc.vector.tensor_scalar(stat[:, 1], stat[:, 1], 1.0 / D, LN_EPS, ALU.mult, ALU.add)
            dve.drain()
            dve.nop().then_inc(root_in, 1)
            dve.wait_ge(root_out, 1)
            nc.vector.reciprocal(stat[:, 0], stat[:, 2])
            dve.drain()
            nc.vector.tensor_tensor(stat[:, 0], stat[:, 0], keep[:, :], ALU.mult)
            dve.drain()
            nc.vector.tensor_tensor(fused[:, :, :], fused[:, :, :], over_last(stat[:, 0], D), ALU.mult)
            dve.drain()
            nc.vector.tensor_tensor(resid[:, :, :], resid[:, :, :], fused[:, :, :], ALU.add)


def state_space_layers(nc, m, A, resid, ident, dram_k, pw):
    PAIRS = D // 2
    GP = 4
    GROUPS = PAIRS // GP
    TURNED = 4

    hs = m.sb("hs", [P, TILES, D])
    u = m.sb("u", [P, D, TILES])
    y = m.sb("y", [P, TILES, D])
    turned = m.sb("turned", [P, TURNED, 2, GP, P])
    toep = turned[:, :, :, :, :].rearrange("p s r q n -> p s (r q) n")
    state = resid[:, :, :].rearrange("p t d -> p (t d)").rearrange("p (q r t) -> p q r t", q=PAIRS, r=2)
    padded = m.sb("padded", [P, 2, GP, 2, 2, TILES])
    cols, powers = pw.cols, pw.powers
    k_ap = dram_k.ap()
    cdz = m.sb("cdz", [P, PAIRS, 2, 2])
    cds = m.sb("cds", [P, PAIRS, 2])
    cdw = m.sb("cdw", [P, 2, PAIRS])
    part = m.sb("part", [P, 8, PAIRS])
    w128 = m.sb("w128", [P, 2, PAIRS])
    wr = m.sb("wr", [P, PAIRS, 2, BATCH])
    ws = m.sb("ws", [P, PAIRS, 2, BATCH])
    s1 = m.sb("s1", [P, PAIRS, 2, BATCH])
    s2 = m.sb("s2", [P, PAIRS, 2, BATCH])
    rot = m.sb("rot", [P, GP, 2, TILES])
    stat = m.sb("stat", [P, 3, TILES])
    scale_bc = m.sb("scale_bc", [P, D])
    bias_bc = m.sb("bias_bc", [P, D])
    kt = m.sb("kt", [P, P])
    krow = m.sb("krow", [D, P])
    wout = m.sb("wout", [P, 2 * P])
    w_in = m.sb("w_in", [P, 2 * D])
    brow = m.sb("brow", [P, P])
    b_part = m.sb("b_part", [P, P], BF16)
    bias_parts = m.sb("bias_parts", [P, GP * P], BF16)
    ones = m.sb("ones", [P, P], BF16)
    yT = m.sb("yT", [P, 2, GP * P // 2])
    gate = m.sb("gate", [P, 2, GP, D])
    zz = rot[:, :, :, :].rearrange("p q r t -> p (q r t)").rearrange("p (s t d) -> p s t d", s=2, d=D)
    dram_resid = nc.dram_tensor("parked_resid", (P, TILES, D), F32).ap()
    ps_s = [m.ps(f"ps_s{i}", [P, GP, 2, TILES]) for i in range(2)]
    ps_k = m.ps("ps_k", [P, D + P])
    ps_y = [m.ps(f"ps_y{i}", [P, 2 * GP, TILES]) for i in range(2)]
    ps_t = m.ps("ps_t", [P, GP * P // 2])
    ps_z = [m.ps(f"ps_z{i}", [P, GP, P]) for i in range(2)]
    names = ("params", "wout_t", "wout_ok", "root_in", "root_out", "u_ok", 
             "powers_used", "turn_mm", "turn_ok", "small_ok", "k_mm", "k_sb", "k_turned", "k_row", "k_out", "t0_used", "s_mm",
             "s_read", "scanned", "pad_ok", "y_mm", "y_ok", "yt_mm", "yt_ok", "z_mm", "gate_ok", "z_read",
             "layer_done", "y_read", "back", "parked", "zeroed")
    S = {n: m.sem(n) for n in names}

    t0_in = [m.sem(f"t0_in{i}") for i in range(TURNED)]
    NPARAM = 5
    BLOCKS = TILES // GP

    with nc.Block() as block:

        @block.sync
        def _(sp):
            sp.dma_start(dram_resid, resid[:, :, :]).then_inc(S["parked"], 16)
            with sp.Fori(0, LAYERS) as l:
                k_base = sp.snap(l * (D * 2 * P))
                sp.wait_ge(S["layer_done"], l + 1)
                sp.dma_start(scale_bc[:, :], A["L0_attn_ln_scale"][bass.ds(l, 1), :].partition_broadcast(P).squeeze(1)).then_inc(S["params"], 16)
                sp.dma_start(bias_bc[:, :], A["L0_attn_ln_bias"][bass.ds(l, 1), :].partition_broadcast(P).squeeze(1)).then_inc(S["params"], 16)
                sp.dma_start(brow[:, :], A["L0_attn_bout"][bass.ds(l, 1), :].partition_broadcast(P).squeeze(1)).then_inc(S["params"], 16)
                for k in range(2):
                    sp.dma_start(w_in[:, k * D:(k + 1) * D], A["L0_attn_Wout"][bass.ds(l, 1), :, :].squeeze(0)).then_inc(S["params"], 16)
                sp.wait_ge(S["k_row"], l + 1)
                sp.dma_start(k_ap[bass.ds(l, 1), :, P + 1:2 * P].squeeze(0), krow[:, 1:P]).then_inc(S["k_out"], 16)
                sp.wait_ge(S["k_out"], 16 * l + 16)
                sp.wait_ge(S["s_mm"], l * GROUPS + GROUPS)
                for g in range(GROUPS):
                    if g >= TURNED:
                        sp.wait_ge(S["t0_used"], l * GROUPS + g - TURNED + 1)
                    src = bass.AP(tensor=dram_k, offset=k_base + 1 + g * 2 * GP * 2 * P, ap=[[1, P], [2 * P, 2 * GP], [1, P]])
                    sp.dma_start(toep[:, g % TURNED, :, :], src).then_inc(t0_in[g % TURNED], 16)
            sp.wait_ge(S["powers_used"], LAYERS + 1)
            sp.dma_start(resid[:, :, :], dram_resid).then_inc(S["back"], 16)
            sp.wait_ge(S["back"], 16)

        zeroed = ((ones[:, :], 1.0), (wout[:, :], 0.0), (cdz[:, :, :, :], 0.0), (bias_parts[:, :], 0.0), (kt[:, :], 0.0),
                  (padded[:, :, :, :, :, :], 0.0))

        @block.gpsimd
        def _(pool):
            for i, (buf, val) in enumerate(zeroed):
                nc.gpsimd.memset(buf, val).then_inc(S["zeroed"], 1)
                pool.wait_ge(S["zeroed"], i + 1)
            pw.gpsimd(pool, 0, 0, 1, 1)
            with pool.Fori(0, LAYERS // 2) as ll:
                for parity in range(2):
                    l = ll * 2 + parity
                    pool.wait_ge(S["powers_used"], l + 1)
                    for half in range(2):
                        pw.gpsimd(pool, (l + 1) % LAYERS, 1 - parity, half, 2 * l + 2 + half)

        @block.scalar
        def _(act):
            def gelu(l, g):
                act.wait_ge(S["y_mm"], l * GROUPS + g + 1)
                dst = y[:, :, g * 2 * GP:(g + 1) * 2 * GP].rearrange("p t h -> p h t")
                nc.scalar.activation(dst, ps_y[g % 2][:, :, :], ACT.Gelu_apprx_tanh).then_inc(S["y_read"], 1)

            def turn(l, g):
                if g >= TURNED:
                    act.wait_ge(S["s_mm"], l * GROUPS + g - TURNED + 1)
                act.wait_ge(S["turn_mm"], l * GROUPS + g + 1)
                for ri in range(2):
                    last = nc.scalar.activation(turned[:, g % TURNED, ri, :, :].rearrange("p q n -> p (q n)"),
                                                ps_z[ri][:, :, :].rearrange("p q n -> p (q n)"), ACT.Copy, scale=(1.0, -1.0)[ri])
                last.then_inc(S["turn_ok"], 1)

            act.wait_ge(S["root_in"], 1)
            nc.scalar.activation(stat[:, 2], stat[:, 1], ACT.Sqrt).then_inc(S["root_out"], 1)
            act.wait_ge(S["zeroed"], len(zeroed))
            pw.scalar(act, 1)
            with act.Fori(0, LAYERS) as l:
                act.wait_ge(S["wout_t"], l + 1)
                nc.scalar.activation(wout[0:D, 0:P], ps_k[0:D, 0:P], ACT.Copy)
                nc.scalar.activation(wout[D:P, P:2 * P], ps_k[D:P, 0:P], ACT.Copy).then_inc(S["wout_ok"], 1)
                pw.scalar(act, 2 * l + 2)
                act.wait_ge(S["root_in"], l + 2)
                nc.scalar.activation(stat[:, 2], stat[:, 1], ACT.Sqrt).then_inc(S["root_out"], 1)
                for g in range(GROUPS):
                    turn(l, g)
                pw.scalar(act, 2 * l + 3)
                act.wait_ge(S["k_mm"], l + 1)
                nc.scalar.activation(kt[:, 0:D], ps_k[:, 0:D], ACT.Copy).then_inc(S["k_sb"], 1)
                act.wait_ge(S["k_turned"], l + 1)
                nc.scalar.activation(krow[:, :], ps_k[0:D, D:D + P], ACT.Copy).then_inc(S["k_row"], 1)
                for g in range(GROUPS):
                    if g % (GROUPS // 2) == 0:
                        act.wait_ge(S["scanned"], 2 * l + 1 + g // (GROUPS // 2))
                    if g >= 2:
                        act.wait_ge(S["y_mm"], l * GROUPS + g - 1)
                    for par in range(2):
                        side = slice(par * D, (par + 1) * D)
                        for ri in range(2):
                            dst = padded[side, g % 2, :, ri, par, :].rearrange("p q (b c) -> p q b c", c=CHUNKS)
                            src = state[side, g * GP:(g + 1) * GP, ri, :].rearrange("p q (b c) -> p q b c", c=CHUNKS)
                            nc.scalar.activation(dst[:, :, :, 1:CHUNKS], src[:, :, :, 0:CHUNKS - 1], ACT.Copy)
                    act.drain()
                    act.nop().then_inc(S["pad_ok"], 1)
                    if g >= 1:
                        gelu(l, g - 1)
                gelu(l, GROUPS - 1)
                act.drain()
                act.nop().then_inc(S["y_ok"], 1)
                for k in range(BLOCKS + 1):
                    if k < BLOCKS:
                        act.wait_ge(S["yt_mm"], l * BLOCKS + k + 1)
                        nc.scalar.activation(yT[:, k % 2, :].rearrange("p (j i) -> p j i", i=P),
                                             ps_t[:, :].rearrange("p (j i) -> p j i", i=P)[:, :, ::-1], ACT.Copy).then_inc(S["yt_ok"], 1)
                    if k >= 1:
                        j = k - 1
                        act.wait_ge(S["z_mm"], l * BLOCKS + j + 1)
                        if j >= 2:
                            act.wait_ge(S["z_read"], l * BLOCKS + j)
                        nc.scalar.activation(gate[:, j % 2, :, :], ps_z[j % 2][:, :, D:P], ACT.Sigmoid).then_inc(S["gate_ok"], 1)

        @block.vector
        def _(dve):
            tile_bc = [P, TILES, D]

            def root(done):
                dve.drain()
                dve.nop().then_inc(S["root_in"], 1)
                dve.wait_ge(S["root_out"], done)

            def split_bias():
                for i in range(3):
                    row = slice(32 * i, 32 * i + 1)
                    nc.vector.tensor_copy(b_part[:, :], brow[:, :])
                    dve.drain()
                    for t in range(GP):
                        nc.vector.tensor_copy(bias_parts[row, t * P:(t + 1) * P], b_part[row, :])
                    if i < 2:
                        nc.vector.tensor_tensor(brow[:, :], brow[:, :], b_part[:, :], ALU.subtract)
                        dve.drain()

            def pole_factors(l, parity, count):
                for ri in range(2):
                    for par in range(2):
                        side = slice(par * D, (par + 1) * D)
                        nc.vector.tensor_copy(cdz[side, :, ri, par], of_layer(cols[side, 2 + ri], l))
                dve.wait_ge(pw.powers_ok, count)
                w, w127 = [[powers[:, parity, :, ri, i] for ri in range(2)] for i in (1, P - 1)]
                cd = [of_layer(cols[:, 2 + ri], l) for ri in range(2)]
                for i, (a, b) in enumerate(((w[0], cd[0]), (w[1], cd[1]), (w[0], cd[1]), (w[1], cd[0]),
                                            (w[0], w127[0]), (w[1], w127[1]), (w[0], w127[1]), (w[1], w127[0]))):
                    nc.vector.tensor_tensor(part[:, i, :], a, b, ALU.mult)
                dve.drain()
                for dst, i, op in ((cdw[:, 0, :], 0, ALU.add), (cdw[:, 1, :], 2, ALU.subtract),
                                   (w128[:, 0, :], 4, ALU.subtract), (w128[:, 1, :], 6, ALU.add)):
                    nc.vector.tensor_tensor(dst, part[:, i, :], part[:, i + 1, :], op)
                dve.drain()
                dve.nop().then_inc(S["small_ok"], 1)
                nc.vector.tensor_scalar(cds[:, :, 0], cdw[:, 1, :], -1.0, None, ALU.mult)
                nc.vector.tensor_copy(cds[:, :, 1], cdw[:, 1, :])
                for ri in range(2):
                    nc.vector.tensor_copy(wr[:, :, ri, :], over_last(w128[:, 0, :], BATCH))
                    nc.vector.tensor_scalar(ws[:, :, ri, :], over_last(w128[:, 1, :], BATCH), (1.0, -1.0)[ri], None, ALU.mult)
                dve.drain()

            def scan(q):
                st = state[:, q, :, :].rearrange("p q r (b c) -> p q r b c", c=CHUNKS)
                for c in range(1, CHUNKS - 1):
                    prev, cur = st[:, :, :, :, c - 1], st[:, :, :, :, c]
                    nc.vector.tensor_tensor(s1[:, q], wr[:, q], prev, ALU.mult)
                    nc.vector.tensor_tensor(s2[:, q], ws[:, q], prev[:, :, ::-1, :], ALU.mult)
                    dve.drain()
                    nc.vector.tensor_tensor(s1[:, q], s1[:, q], s2[:, q], ALU.add)
                    dve.drain()
                    nc.vector.tensor_tensor(cur, cur, s1[:, q], ALU.add)
                    dve.drain()

            dve.nop().then_inc(S["z_read"], 1)
            layer_norm(nc, dve, hs[:, :, :], resid[:, :, :], hs[:, :, :], y[:, :, :], stat, LN_EPS, lambda: root(1))
            dve.drain()
            dve.nop().then_inc(S["layer_done"], 1)
            dve.wait_ge(S["zeroed"], len(zeroed))
            pole_factors(0, 0, 2)
            dve.wait_ge(S["parked"], 16)
            with dve.Fori(0, LAYERS // 2) as ll:
                for parity in range(2):
                    l = ll * 2 + parity
                    u_t = u[:, :, :].rearrange("p h t -> p t h")
                    layer_norm(nc, dve, y[:, :, :], hs[:, :, :], y[:, :, :], u_t, stat, LN_EPS, lambda: root(l + 2))
                    dve.drain()
                    dve.wait_ge(S["params"], 16 * NPARAM * l + 16 * NPARAM)
                    nc.vector.tensor_tensor(y[:, :, :], y[:, :, :], scale_bc[:, :].unsqueeze(1).broadcast_to(tile_bc), ALU.mult)
                    dve.drain()
                    nc.vector.tensor_tensor(u_t, y[:, :, :], bias_bc[:, :].unsqueeze(1).broadcast_to(tile_bc), ALU.add)
                    dve.drain()
                    dve.nop().then_inc(S["u_ok"], 1)
                    split_bias()
                    for g in range(GROUPS):
                        dve.wait_ge(S["s_mm"], l * GROUPS + g + 1)
                        q = slice(g * GP, (g + 1) * GP)
                        whole = [P, GP, 2, TILES]
                        cd_r = cdw[:, 0, q].unsqueeze(2).unsqueeze(3).broadcast_to(whole)
                        nc.vector.tensor_tensor(state[:, q, :, :], ps_s[g % 2][:, :, :, :], cd_r, ALU.mult)
                        nc.vector.tensor_tensor(rot[:, :, :, :], ps_s[g % 2][:, :, ::-1, :], over_last(cds[:, q, :], TILES), ALU.mult)
                        dve.drain()
                        dve.nop().then_inc(S["s_read"], 1)
                        nc.vector.tensor_tensor(state[:, q, :, :], state[:, q, :, :], rot[:, :, :, :], ALU.add)
                        dve.drain()
                    for half in range(2):
                        scan(slice(half * PAIRS // 2, (half + 1) * PAIRS // 2))
                        dve.nop().then_inc(S["scanned"], 1)
                    dve.wait_ge(S["k_mm"], l + 1)
                    pole_factors((l + 1) % LAYERS, 1 - parity, 2 * l + 4)
                    for j in range(BLOCKS):
                        dve.wait_ge(S["gate_ok"], l * BLOCKS + j + 1)
                        nc.vector.tensor_tensor(zz[:, j % 2, :, :], ps_z[j % 2][:, :, 0:D], gate[:, j % 2, :, :], ALU.mult).then_inc(S["z_read"], 1)
                        dve.drain()
                        t = slice(j * GP, (j + 1) * GP)
                        nc.vector.tensor_tensor(hs[:, t, :], hs[:, t, :], zz[:, j % 2, :, :], ALU.add)
                    dve.drain()
                    dve.nop().then_inc(S["layer_done"], 1)
            dve.wait_ge(S["back"], 16)
            nc.vector.tensor_tensor(resid[:, :, :], resid[:, :, :], hs[:, :, :], ALU.add)

        @block.tensor
        def _(pe):
            def turn(l, parity, g):
                if g == 0:
                    pe.wait_ge(S["z_read"], l * BLOCKS + 1)
                else:
                    pe.wait_ge(S["turn_ok"], l * GROUPS + g)
                for ri in range(2):
                    for q in range(GP):
                        last = nc.tensor.transpose(ps_z[ri][:, q, :], powers[:, parity, g * GP + q, ri, :], ident[:, :])
                last.then_inc(S["turn_mm"], 1)

            def into_state(l, g):
                pe.wait_ge(S["turn_ok"], l * GROUPS + g + 1)
                if g >= 2:
                    pe.wait_ge(S["s_read"], l * GROUPS + g - 1)
                for q in range(GP):
                    for ri in range(2):
                        for par in range(2):
                            last = nc.tensor.matmul(ps_s[g % 2][par * D:(par + 1) * D, q, ri, :],
                                                    turned[:, g % TURNED, ri, q, par * D:(par + 1) * D],
                                                    u[:, 2 * (g * GP + q) + par, :], start=True, stop=True)
                last.then_inc(S["s_mm"], 1)

            def taps(parity, half):
                for pair in range(half * PAIRS // 2, (half + 1) * PAIRS // 2):
                    for ri in range(2):
                        last = nc.tensor.matmul(ps_k[:, 2 * pair:2 * pair + 2], powers[:, parity, pair, ri, :], cdz[:, pair, ri, :],
                                                start=ri == 0, stop=ri == 1)
                return last

            def layer(l, parity):
                pe.wait_ge(pw.powers_ok, 2 * l + 2)
                pe.wait_ge(S["params"], 16 * NPARAM * l + 16 * NPARAM)
                nc.tensor.transpose(ps_k[:, 0:P], w_in[:, :], ident[:, :]).then_inc(S["wout_t"], 1)
                pe.wait_ge(S["small_ok"], l + 1)
                pe.wait_ge(S["wout_ok"], l + 1)
                taps(parity, 0)
                for g in range(TURNED):
                    turn(l, parity, g)
                pe.wait_ge(S["u_ok"], l + 1)
                for g in range(TURNED):
                    into_state(l, g)
                    turn(l, parity, g + TURNED)
                for g in range(TURNED, GROUPS):
                    into_state(l, g)
                taps(parity, 1).then_inc(S["k_mm"], 1)
                pe.wait_ge(S["k_sb"], l + 1)
                nc.tensor.transpose(ps_k[:, D:D + P], kt[:, :], ident[:, :]).then_inc(S["k_turned"], 1)
                for g in range(GROUPS):
                    pe.wait_ge(S["pad_ok"], l * GROUPS + g + 1)
                    pe.wait_ge(t0_in[g % TURNED], 16 * (GROUPS // TURNED) * l + 16 * (g // TURNED) + 16)
                    if g >= 2:
                        pe.wait_ge(S["y_read"], l * GROUPS + g - 1)
                    for q in range(GP):
                        pair = g * GP + q
                        out = ps_y[g % 2][:, 2 * q:2 * q + 2, :]
                        for ri in range(2):
                            nc.tensor.matmul(out, powers[:, parity, pair, ri, :], padded[:, g % 2, q, ri, :, :],
                                             start=ri == 0, stop=False, skip_group_check=True)
                        for par in range(2):
                            last = nc.tensor.matmul(ps_y[g % 2][:, 2 * q + par, :], toep[:, g % TURNED, 2 * q + par, :],
                                                    u[:, 2 * pair + par, :], start=False, stop=par == 1, skip_group_check=True)
                    last.then_inc(S["y_mm"], 1)
                    pe.drain()
                    pe.nop().then_inc(S["t0_used"], 1)
                pe.nop().then_inc(S["powers_used"], 1)
                pe.wait_ge(S["y_ok"], l + 1)
                for k in range(BLOCKS + 1):
                    if k < BLOCKS:
                        if k >= 1:
                            pe.wait_ge(S["yt_ok"], l * BLOCKS + k)
                        for j in range(GP // 2):
                            t = k * GP + 2 * j
                            last = nc.tensor.transpose(ps_t[:, j * P:(j + 1) * P], y[:, t:t + 2, :].rearrange("p t h -> p (t h)"), ident[:, :])
                        last.then_inc(S["yt_mm"], 1)
                    if k >= 1:
                        i = k - 1
                        if k == BLOCKS:
                            pe.wait_ge(S["yt_ok"], l * BLOCKS + k)
                        if i >= 2:
                            pe.wait_ge(S["z_read"], l * BLOCKS + i)
                        nc.tensor.matmul(ps_z[i % 2][:, :, :].rearrange("p a b -> p (a b)"), ones[:, :], bias_parts[:, :], start=True, stop=False)
                        for j in range(GP // 2):
                            dst = ps_z[i % 2][:, 2 * j:2 * j + 2, :].rearrange("p a b -> p (a b)")
                            last = nc.tensor.matmul(dst, yT[:, i % 2, j * P:(j + 1) * P], wout[:, :], start=False, stop=j == GP // 2 - 1)
                        last.then_inc(S["z_mm"], 1)

            pe.nop().then_inc(S["powers_used"], 1)
            with pe.Fori(0, LAYERS // 2) as ll:
                for parity in range(2):
                    layer(ll * 2 + parity, parity)


def expert_mixture(nc, m, A, resid, ident, flip):
    E = A["L0_ffn_Wr"].shape[1]
    PAIRS = E // 2
    HB = BATCH // 2
    COLS = HB * SEQ
    BN_EPS = 1e-3
    BLK = 4 * P
    VEC = ("b1", "g1", "be1", "m1", "v1", "b2", "g2", "be2", "m2", "v2")

    xT = m.sb("xT", [P, COLS])
    w1 = m.sb("w1", [P, 2, PAIRS, P])
    w2 = m.sb("w2", [P, PAIRS, P])
    wo = m.sb("wo", [P, PAIRS, D])
    bo = m.sb("bo", [3 * 32, D])
    wr = m.sb("wr", [P, E])
    br = m.sb("br", [P, E])
    rowsv = m.sb("rowsv", [len(VEC) * PAIRS, P])
    vec = m.sb("vec", [P, len(VEC), PAIRS])
    fold = m.sb("fold", [P, 2, 2, PAIRS])
    sd = m.sb("sd", [P, 2, PAIRS])
    wb = m.sb("wb", [P, PAIRS, SEQ])
    ybo = m.sb("ybo", [P, CHUNKS, D])
    V = {n: i for i, n in enumerate(VEC)}

    with ExitStack() as stack:
        pm = Memory(nc, stack, "gate")
        x = pm.sb("x", [P, TILES // 2, 2, D])
        square = pm.sb("square", [P, 2, TILES // 2, D])
        stat = pm.sb("stat", [P, 3, TILES])
        stat4 = stat[:, :, :].rearrange("p s (a t) -> p s a t", a=2)
        lg = pm.sb("lg", [P, CHUNKS, E])
        ex = pm.sb("ex", [P, CHUNKS, E])
        red = pm.sb("red", [P, 2, CHUNKS])
        ROWS = 3 * 32
        parts = pm.sb("parts", [P, CHUNKS, ROWS])
        part16 = pm.sb("part16", [P, CHUNKS, E], BF16)
        wT = pm.sb("wT", [ROWS, SEQ])
        wT16 = pm.sb("wT16", [ROWS, SEQ], BF16)
        sel = pm.sb("sel", [ROWS, PAIRS, P])
        sel16 = pm.sb("sel16", [ROWS, PAIRS, P], BF16)
        ps_v = pm.ps("ps_v", [P, len(VEC) * PAIRS])
        ps_x = [pm.ps(f"ps_x{i}", [P, BLK]) for i in range(2)]
        ps_l = pm.ps("ps_l", [P, CHUNKS, E])
        ps_t = pm.ps("ps_t", [ROWS, BLK])
        ps_b = [pm.ps(f"ps_b{i}", [P, BLK]) for i in range(2)]
        ps_y = pm.ps("ps_y", [P, 8, D])
        names = ("zeroed", "loaded", "vec_tr", "root_in", "root_out", "x_ok", "xt_mm", "xt_sb", "l_mm", "exp_in", "exp_out",
                 "soft_ok", "wt_mm", "wt_sb", "wb_mm", "wb_sb", "sel_ok", "yb_mm", "yb_sb")
        S = {n: pm.sem(n) for n in names}
        ffn = {k: A["L0_ffn_" + k] for k in ("Wr", "br", "W1", "W2", "Wo", "bo") + VEC}
        NB = COLS // BLK
        LOADS = 23

        with nc.Block() as block:

            @block.sync
            def _(sp):
                n = 0
                for i, v in enumerate(VEC):
                    sp.dma_start(rowsv[i * PAIRS:(i + 1) * PAIRS, :], ffn[v].rearrange("(q e) h -> q (e h)", e=2)).then_inc(S["loaded"], 16)
                    n += 1
                for k in range(2):
                    sp.dma_start(wr[k * D:(k + 1) * D, :], ffn["Wr"]).then_inc(S["loaded"], 16)
                    n += 1
                sp.dma_start(br[:, :], ffn["br"].partition_broadcast(P)).then_inc(S["loaded"], 16)
                sp.dma_start(wo[:, :, :], ffn["Wo"].rearrange("(q e) h d -> (e h) q d", e=2)).then_inc(S["loaded"], 16)
                sp.wait_ge(S["zeroed"], 1)
                for k in range(3):
                    sp.dma_start(bo[32 * k:32 * k + E, :], ffn["bo"]).then_inc(S["loaded"], 16)
                for k in range(2):
                    side = slice(k * D, (k + 1) * D)
                    for e in range(2):
                        sp.dma_start(w1[side, k, :, e * D:(e + 1) * D], ffn["W1"].rearrange("(q e) d h -> e d q h", e=2)[e]).then_inc(S["loaded"], 16)
                    sp.dma_start(w2[side, :, side], ffn["W2"].rearrange("(q e) h k -> e h q k", e=2)[k]).then_inc(S["loaded"], 16)
                assert n + 5 + 6 == LOADS
                sp.wait_ge(S["loaded"], 16 * LOADS)

            @block.gpsimd
            def _(pool):
                nc.gpsimd.memset(w1[:, :, :, :], 0.0).then_inc(S["sel_ok"], 1)
                pool.wait_ge(S["sel_ok"], 1)
                nc.gpsimd.memset(bo[:, :], 0.0).then_inc(S["sel_ok"], 1)
                pool.wait_ge(S["sel_ok"], 2)
                nc.gpsimd.memset(w2[:, :, :], 0.0).then_inc(S["zeroed"], 1)
                pool.wait_ge(S["zeroed"], 1)
                nc.gpsimd.memset(parts[:, :, :], 0.0).then_inc(S["sel_ok"], 1)
                pool.wait_ge(S["sel_ok"], 3)
                nc.gpsimd.memset(sel[:, :, :], 0.0).then_inc(S["sel_ok"], 1)
                pool.wait_ge(S["sel_ok"], 4)
                for k in range(3):
                    nc.gpsimd.affine_select(out=sel[:, :, :], in_=sel[:, :, :], compare_op=ALU.not_equal, fill=1.0, base=-32 * k,
                                            pattern=[[-2, PAIRS], [-1, 2], [0, D]], channel_multiplier=1).then_inc(S["sel_ok"], 1)
                    pool.wait_ge(S["sel_ok"], 5 + k)

            @block.scalar
            def _(act):
                act.wait_ge(S["root_in"], 1)
                nc.scalar.activation(stat[:, 2], stat[:, 1], ACT.Sqrt)
                nc.scalar.activation(sd[:, :, :], sd[:, :, :], ACT.Sqrt)
                act.drain()
                act.nop().then_inc(S["root_out"], 1)
                for k in range(NB):
                    act.wait_ge(S["xt_mm"], k + 1)
                    nc.scalar.activation(xT[:, k * BLK:(k + 1) * BLK], ps_x[k % 2][:, :], ACT.Copy).then_inc(S["xt_sb"], 1)
                act.wait_ge(S["sel_ok"], 7)
                nc.scalar.activation(sel16[:, :, :], sel[:, :, :], ACT.Copy).then_inc(S["sel_ok"], 1)
                act.wait_ge(S["exp_in"], 1)
                nc.scalar.activation(ex[:, :, :], lg[:, :, :], ACT.Exp).then_inc(S["exp_out"], 1)
                for k in range(4):
                    act.wait_ge(S["wt_mm"], k + 1)
                    nc.scalar.activation(wT16[:, k * BLK:(k + 1) * BLK], ps_t[:, :], ACT.Copy).then_inc(S["wt_sb"], 1)
                for k in range(4):
                    for q in range(PAIRS):
                        n = k * PAIRS + q
                        act.wait_ge(S["wb_mm"], n + 1)
                        nc.scalar.activation(wb[:, q, k * BLK:(k + 1) * BLK], ps_b[n % 2][:, :], ACT.Copy).then_inc(S["wb_sb"], 1)

            @block.vector
            def _(dve):
                def root():
                    dve.wait_ge(S["vec_tr"], 1)
                    nc.vector.tensor_copy(vec[:, :, :], ps_v[:, :].rearrange("p (v q) -> p v q", q=PAIRS))
                    dve.drain()
                    for i, k in enumerate("12"):
                        nc.vector.tensor_scalar(sd[:, i, :], vec[:, V["v" + k], :], BN_EPS, None, ALU.add)
                    dve.drain()
                    dve.nop().then_inc(S["root_in"], 1)
                    dve.wait_ge(S["root_out"], 1)

                x_t = x[:, :, :, :].rearrange("p t a d -> p a t d")
                r_t = resid[:, :, :].rearrange("p (a t) d -> p a t d", a=2)
                layer_norm(nc, dve, x_t, r_t, x_t, square[:, :, :, :], stat4, LN_EPS, root)
                dve.drain()
                dve.nop().then_inc(S["x_ok"], 1)
                nc.vector.reciprocal(sd[:, :, :], sd[:, :, :])
                dve.drain()
                for i, k in enumerate("12"):
                    nc.vector.tensor_tensor(fold[:, i, 0, :], vec[:, V["g" + k], :], sd[:, i, :], ALU.mult)
                    nc.vector.tensor_tensor(fold[:, i, 1, :], vec[:, V["b" + k], :], vec[:, V["m" + k], :], ALU.subtract)
                    dve.drain()
                    nc.vector.tensor_tensor(fold[:, i, 1, :], fold[:, i, 1, :], fold[:, i, 0, :], ALU.mult)
                    dve.drain()
                    nc.vector.tensor_tensor(fold[:, i, 1, :], fold[:, i, 1, :], vec[:, V["be" + k], :], ALU.add)
                dve.wait_ge(S["l_mm"], 1)
                nc.vector.scalar_tensor_tensor(lg[:, :, :], ps_l[:, :, :], 1.0 / BATCH, br[:, :].unsqueeze(1).broadcast_to([P, CHUNKS, E]),
                                               ALU.mult, ALU.add)
                dve.drain()
                nc.vector.tensor_reduce(out=red[:, 0, :], in_=lg[:, :, :], axis=AX.X, op=ALU.max)
                dve.drain()
                nc.vector.tensor_tensor(lg[:, :, :], lg[:, :, :], over_last(red[:, 0, :], E), ALU.subtract)
                dve.drain()
                dve.nop().then_inc(S["exp_in"], 1)
                dve.wait_ge(S["exp_out"], 1)
                nc.vector.tensor_reduce(out=red[:, 1, :], in_=ex[:, :, :], axis=AX.X, op=ALU.add)
                dve.drain()
                nc.vector.reciprocal(red[:, 0, :], red[:, 1, :])
                dve.drain()
                nc.vector.tensor_tensor(ex[:, :, :], ex[:, :, :], over_last(red[:, 0, :], E), ALU.mult)
                dve.drain()
                dve.wait_ge(S["sel_ok"], 3)
                for k in range(3):
                    nc.vector.tensor_copy(part16[:, :, :], ex[:, :, :])
                    dve.drain()
                    nc.vector.tensor_copy(parts[:, :, 32 * k:32 * k + E], part16[:, :, :])
                    if k < 2:
                        nc.vector.tensor_tensor(ex[:, :, :], ex[:, :, :], part16[:, :, :], ALU.subtract)
                        dve.drain()
                dve.drain()
                dve.nop().then_inc(S["soft_ok"], 1)
                for k in range(4):
                    dve.wait_ge(S["wt_mm"], k + 1)
                    dve.wait_ge(S["wt_sb"], 2 * k + 1)
                    nc.vector.tensor_copy(wT[:, k * BLK:(k + 1) * BLK], ps_t[:, :]).then_inc(S["wt_sb"], 1)
                for k in range(2):
                    dve.wait_ge(S["yb_mm"], k + 1)
                    nc.vector.tensor_copy(ybo[:, k * 8:(k + 1) * 8, :], ps_y[:, :, :]).then_inc(S["yb_sb"], 1)

            @block.tensor
            def _(pe):
                pe.wait_ge(S["loaded"], 16 * LOADS)
                nv = len(VEC) * PAIRS
                nc.tensor.transpose(ps_v[:, :], rowsv[:, :], ident[0:nv, 0:nv]).then_inc(S["vec_tr"], 1)
                pe.wait_ge(S["x_ok"], 1)
                for k in range(NB):
                    if k >= 2:
                        pe.wait_ge(S["xt_sb"], k - 1)
                    for j in range(4):
                        t = 4 * k + j
                        last = nc.tensor.transpose(ps_x[k % 2][:, j * P:(j + 1) * P], x[:, t, :, :].rearrange("p a d -> p (a d)"), ident[:, :])
                    last.then_inc(S["xt_mm"], 1)
                pe.wait_ge(S["xt_sb"], NB)
                for c in range(CHUNKS):
                    for k in range(HB):
                        a = k * SEQ + c * P
                        last = nc.tensor.matmul(ps_l[:, c, :], xT[:, a:a + P], wr[:, :], start=k == 0, stop=k == HB - 1)
                last.then_inc(S["l_mm"], 1)
                pe.wait_ge(S["soft_ok"], 1)
                for k in range(4):
                    if k:
                        pe.wait_ge(S["wt_sb"], 2 * k)
                    for j in range(4):
                        last = nc.tensor.transpose(ps_t[:, j * P:(j + 1) * P], parts[:, 4 * k + j, :], ident[:, :])
                    last.then_inc(S["wt_mm"], 1)
                pe.wait_ge(S["wt_sb"], 8)
                pe.wait_ge(S["sel_ok"], 8)
                for k in range(4):
                    for q in range(PAIRS):
                        n = k * PAIRS + q
                        if n >= 2:
                            pe.wait_ge(S["wb_sb"], n - 1)
                        nc.tensor.matmul(ps_b[n % 2][:, :], sel16[:, q, :], wT16[:, k * BLK:(k + 1) * BLK], start=True, stop=True).then_inc(S["wb_mm"], 1)
                for k in range(2):
                    if k:
                        pe.wait_ge(S["yb_sb"], 1)
                    for j in range(8):
                        c = 8 * k + j
                        last = nc.tensor.matmul(ps_y[:, j, :], wT[:, c * P:(c + 1) * P], bo[:, :], start=True, stop=True)
                    last.then_inc(S["yb_mm"], 1)

    STEPS = BATCH * PAIRS
    NBLK = SEQ // BLK
    h1 = m.sb("h1", [P, 2, BLK])
    h2 = m.sb("h2", [P, 2, BLK])
    h2w = m.sb("h2w", [P, 2, PAIRS, BLK])
    outT = m.sb("outT", [P, 2, BLK])
    add = m.sb("add", [P, 2, 4, 2, D])
    TURNS = (2 * PAIRS + 4, STEPS + 2)
    ps1 = [m.ps(f"ps1{i}", [P, BLK]) for i in range(2)]
    ps2 = [m.ps(f"ps2{i}", [P, BLK]) for i in range(2)]
    ps_w = [m.ps(f"ps_w{i}", [P, BLK]) for i in range(2)]
    ps_o = [m.ps(f"ps_o{i}", [P, BLK]) for i in range(2)]
    names = ("h1_mm", "h1_ok", "h2_mm", "h2_ok", "h2w_ok", "wo_mm", "wo_sb", "wo_turned", "wo_read")
    S = {n: m.sem(n) for n in names}

    with nc.Block() as block:

        @block.tensor
        def _(pe):
            with pe.Fori(0, NBLK) as k:
                for s in range(STEPS + 3):
                    if s < STEPS:
                        b, q = divmod(s, PAIRS)
                        if s >= 2:
                            pe.wait_ge(S["h1_ok"], k * STEPS + s - 1)
                        base = b % HB * SEQ
                        nc.tensor.matmul(ps1[s % 2][:, :], w1[:, b // HB, q, :], xT[:, bass.ds(k * BLK + base, BLK)],
                                         start=True, stop=True).then_inc(S["h1_mm"], 1)
                    if 1 <= s <= STEPS:
                        i = s - 1
                        pe.wait_ge(S["h1_ok"], k * STEPS + i + 1)
                        if i >= 2:
                            pe.wait_ge(S["h2_ok"], k * STEPS + i - 1)
                        nc.tensor.matmul(ps2[i % 2][:, :], w2[:, i % PAIRS, :], h1[:, i % 2, :], start=True, stop=True).then_inc(S["h2_mm"], 1)
                    if s >= 2 and (s - 2) % PAIRS == PAIRS - 1:
                        b = (s - 2) // PAIRS
                        pe.wait_ge(S["h2w_ok"], k * STEPS + (b + 1) * PAIRS)
                        for q in range(PAIRS):
                            last = nc.tensor.matmul(ps_w[b // 2][b % 2 * D:(b % 2 + 1) * D, :], wo[:, q, :], h2w[:, b % 2, q, :],
                                                    start=q == 0, stop=q == PAIRS - 1)
                        last.then_inc(S["wo_mm"], 1)
                    if s in TURNS:
                        i = TURNS.index(s)
                        pe.wait_ge(S["wo_sb"], k * 2 + i + 1)
                        pe.wait_ge(S["wo_read"], k * 2 + i + 1)
                        for j in range(4):
                            last = nc.tensor.transpose(ps_o[i][:, j * P:(j + 1) * P], outT[:, i, j * P:(j + 1) * P], ident[:, :])
                        last.then_inc(S["wo_turned"], 1)

        @block.scalar
        def _(act):
            with act.Fori(0, NBLK) as k:
                for s in range(STEPS + 1):
                    if s < STEPS:
                        q = s % PAIRS
                        act.wait_ge(S["h1_mm"], k * STEPS + s + 1)
                        if s >= 2:
                            act.wait_ge(S["h2_mm"], k * STEPS + s - 1)
                        nc.scalar.activation(h1[:, s % 2, :], ps1[s % 2][:, :], ACT.Relu, bias=fold[:, 0, 1, q:q + 1],
                                             scale=fold[:, 0, 0, q:q + 1]).then_inc(S["h1_ok"], 1)
                    if s >= 1:
                        i, q = s - 1, (s - 1) % PAIRS
                        act.wait_ge(S["h2_mm"], k * STEPS + i + 1)
                        if i >= 2:
                            act.wait_ge(S["h2w_ok"], k * STEPS + i - 1)
                        nc.scalar.activation(h2[:, i % 2, :], ps2[i % 2][:, :], ACT.Relu, bias=fold[:, 1, 1, q:q + 1],
                                             scale=fold[:, 1, 0, q:q + 1]).then_inc(S["h2_ok"], 1)

        @block.vector
        def _(dve):
            dve.nop().then_inc(S["wo_read"], 2)
            with dve.Fori(0, NBLK) as k:
                def copy_out(i):
                    dve.wait_ge(S["wo_mm"], k * BATCH + 2 * i + 2)
                    nc.vector.tensor_copy(outT[:, i, :], ps_w[i][:, :]).then_inc(S["wo_sb"], 1)

                def finish(i):
                    dve.wait_ge(S["wo_turned"], k * 2 + i + 1)
                    bo_sum = ybo[:, bass.ts(k, 4), :].unsqueeze(2).broadcast_to([P, 4, 2, D])
                    nc.vector.tensor_tensor(add[:, i, :, :, :], ps_o[i][:, :].rearrange("p (j a d) -> p j a d", a=2, d=D), bo_sum,
                                            ALU.add).then_inc(S["wo_read"], 1)
                    dve.drain()
                    tiles = resid[:, :, :].rearrange("p (b c) d -> p b c d", c=CHUNKS)[:, 2 * i:2 * i + 2, bass.ts(k, 4), :]
                    nc.vector.tensor_tensor(tiles, tiles, add[:, i, :, :, :].rearrange("p j a d -> p a j d"), ALU.add)

                for s in range(STEPS):
                    b, q = divmod(s, PAIRS)
                    if q == 0 and b >= 2:
                        dve.wait_ge(S["wo_mm"], k * BATCH + b - 1)
                    dve.wait_ge(S["h2_ok"], k * STEPS + s + 1)
                    nc.vector.tensor_tensor(h2w[:, b % 2, q, :], h2[:, s % 2, :], wb[:, q, bass.ts(k, BLK)], ALU.mult).then_inc(S["h2w_ok"], 1)
                    if s == TURNS[0] - 3:
                        copy_out(0)
                    if s == TURNS[0]:
                        finish(0)
                copy_out(1)
                finish(1)


def sigmoid_attention(nc, m, A, resid, ident, flip):
    HEADS = 8
    PAIRS = HEADS // 2
    SCALE = float(D) ** 0.5
    X_UP, W_UP, Q_UP = 2.0 ** 4, 2.0 ** 8, 2.0 ** 6
    BLK = 512
    QB = SEQ // BLK
    IH = 2
    N = TILES * P

    wq = m.sb("wq", [P, HEADS, 2, D], F16)
    wk = m.sb("wk", [P, HEADS, 2, D], F16)
    wv = m.sb("wv", [P, HEADS, D], F16)
    wo = m.sb("wo", [P, PAIRS, D])
    x_hi = m.sb("x_hi", [P, N], F16)
    x_lo = m.sb("x_lo", [P, N], F16)

    with ExitStack() as stack:
        pm = Memory(nc, stack, "split")
        x = pm.sb("x", [P, TILES, D])
        twice = pm.sb("twice", [P, TILES, 2, D])
        stat = pm.sb("stat", [P, 3, TILES])
        raw = [pm.sb(f"raw{i}", [P, HEADS * D]) for i in range(3)]
        ps = [pm.ps(f"ps{i}", [P, BLK]) for i in range(4)]
        loaded, root_in, root_out, x_ok, x_tr, hi_ok, lo_ok = map(pm.sem, (
            "loaded", "root_in", "root_out", "x_ok", "x_tr", "hi_ok", "lo_ok"))
        NB = N // BLK
        with nc.Block() as block:

            @block.sync
            def _(sp):
                for i, n in enumerate(("Wq", "Wk", "Wv")):
                    for k in range(2):
                        sp.dma_start(raw[i][k * D:(k + 1) * D, :], A["L1_attn_" + n]).then_inc(loaded, 16)
                wo_src = A["L1_attn_Wo"].rearrange("(f q a) o -> a f q o", a=2, q=PAIRS)
                for k in range(2):
                    sp.dma_start(wo[k * D:(k + 1) * D, :, :], wo_src[k]).then_inc(loaded, 16)
                sp.wait_ge(loaded, 128)

            @block.vector
            def _(dve):
                def root():
                    dve.drain()
                    dve.nop().then_inc(root_in, 1)
                    dve.wait_ge(root_out, 1)

                layer_norm(nc, dve, x[:, :, :], resid[:, :, :], x[:, :, :], twice[:, :, 0, :], stat, LN_EPS, root)
                dve.drain()
                for k in range(2):
                    nc.vector.tensor_copy(twice[:, :, k, :], x[:, :, :])
                dve.drain()
                dve.nop().then_inc(x_ok, 1)
                dve.wait_ge(loaded, 128)
                lo_rows = slice(D, P)
                for i, dst in enumerate((wq, wk, wv)):
                    nc.vector.tensor_scalar(raw[i][:, :], raw[i][:, :], W_UP, None, ALU.mult)
                dve.drain()
                parts = []
                for i, dst in enumerate((wq, wk, wv)):
                    src = raw[i][:, :].rearrange("p (f h) -> p h f", h=HEADS)
                    if i < 2:
                        src = src.unsqueeze(2).broadcast_to([P, HEADS, 2, D])
                        parts.append((dst[:, :, :, :], dst[lo_rows, :, :, :], src, src[lo_rows]))
                    else:
                        parts.append((dst[:, :, :], dst[lo_rows, :, :], src, src[lo_rows]))
                for dst, _, src, _ in parts:
                    nc.vector.tensor_copy(dst, src)
                dve.drain()
                for _, dst, _, src in parts:
                    nc.vector.tensor_tensor(dst, src, dst, ALU.subtract)
                for k in range(NB):
                    dve.wait_ge(hi_ok, k + 1)
                    c = slice(k * BLK, (k + 1) * BLK)
                    nc.vector.scalar_tensor_tensor(x_lo[:, c], ps[k % 4][:, :], X_UP, x_hi[:, c], ALU.mult, ALU.subtract).then_inc(lo_ok, 1)

            @block.scalar
            def _(act):
                act.wait_ge(root_in, 1)
                nc.scalar.activation(stat[:, 2], stat[:, 1], ACT.Sqrt).then_inc(root_out, 1)
                for k in range(NB):
                    act.wait_ge(x_tr, k + 1)
                    nc.scalar.activation(x_hi[:, k * BLK:(k + 1) * BLK], ps[k % 4][:, :], ACT.Copy, scale=X_UP).then_inc(hi_ok, 1)

            @block.tensor
            def _(pe):
                pe.wait_ge(x_ok, 1)
                for k in range(NB):
                    if k >= 4:
                        pe.wait_ge(lo_ok, k - 3)
                    for j in range(4):
                        last = nc.tensor.transpose(ps[k % 4][:, j * P:(j + 1) * P],
                                                   twice[:, 4 * k + j, :, :].rearrange("p a d -> p (a d)"), ident[:, :])
                    last.then_inc(x_tr, 1)

    k_st = m.sb("k_st", [P, 2, 2, SEQ], F16)
    q_hi = m.sb("q_hi", [P, 2, 2, SEQ], F16)
    q_lo = m.sb("q_lo", [P, 2, SEQ], F16)
    v_st = m.sb("v_st", [P, 2, CHUNKS, 2, D])
    sig = m.sb("sig", [P, 2, 2, 2 * BLK])
    ctxT = m.sb("ctxT", [P, PAIRS, SEQ])
    outT = m.sb("outT", [P, 2, BLK])
    ps_s = [m.ps(f"ps_s{h}", [P, 2 * BLK]) for h in range(2)]
    ps_o = m.ps("ps_o", [P, 2, BLK])
    ps_p = [m.ps(f"ps_p{i}", [P, BLK]) for i in range(2)]
    names = ("p_mm", "hi_ok", "p_read", "qk_mm", "sig_ok", "pv_mm", "o_read", "wo_mm", "wo_sb", "wo_turned", "wo_read")
    S = {n: m.sem(n) for n in names}
    KQ = 4 * QB
    PB = KQ + CHUNKS // 4
    JJ = IH * CHUNKS
    FIRST_JJ = 2
    DOWN = Q_UP / (X_UP * W_UP)


    with nc.Block() as block:

        @block.tensor
        def _(pe):
            def project(i, b, hp, done):
                if i >= 2:
                    pe.wait_ge(S["p_read"], done + i - 1)
                if i < KQ:
                    w = wk if i < KQ // 2 else wq
                    h, c = divmod(i % (KQ // 2), QB)
                    lhsT = w[:, bass.ds(hp * 2 + h, 1), :, :].rearrange("p a t f -> p (a t f)")
                    for part, xs in enumerate((x_hi, x_lo)):
                        last = nc.tensor.matmul(ps_p[i % 2][:, :], lhsT, xs[:, bass.ds(b * SEQ + c * BLK, BLK)],
                                                start=part == 0, stop=part == 1)
                else:
                    for j in range(4):
                        c = (i - KQ) * 4 + j
                        for part, xs in enumerate((x_hi, x_lo)):
                            last = nc.tensor.matmul(ps_p[i % 2][:, j * P:(j + 1) * P], xs[:, bass.ds(b * SEQ + c * P, P)],
                                                    wv[:, bass.ds(hp * 2, 2), :].rearrange("p a f -> p (a f)"),
                                                    start=part == 0, stop=part == 1)
                last.then_inc(S["p_mm"], 1)

            def pair(n, slot, next_b, next_hp):
                pe.wait_ge(S["p_read"], n * PB + PB)
                for jj in range(JJ + 1):
                    if jj < JJ:
                        ih, j = divmod(jj, CHUNKS)
                        for h in range(2):
                            s = 2 * jj + h
                            if s >= 2:
                                pe.wait_ge(S["sig_ok"], n * 2 * JJ + s - 1)
                            for i2 in range(2):
                                c = (2 * ih + i2) * BLK
                                nc.tensor.matmul(ps_s[h][:, i2 * BLK:(i2 + 1) * BLK], k_st[:, slot, h, j * P:(j + 1) * P],
                                                 q_hi[:, slot, h, c:c + BLK], start=True, stop=False)
                        for i2 in range(2):
                            c = (2 * ih + i2) * BLK
                            for h in range(2):
                                rows = slice(h * D, (h + 1) * D)
                                last = nc.tensor.matmul(ps_s[h][:, i2 * BLK:(i2 + 1) * BLK], k_st[rows, slot, h, j * P:(j + 1) * P],
                                                        q_lo[rows, slot, c:c + BLK], start=False, stop=True)
                                if i2:
                                    last.then_inc(S["qk_mm"], 1)
                    if 0 <= jj - FIRST_JJ < PB:
                        project(jj - FIRST_JJ, next_b, next_hp, n * PB + PB)
                    if jj >= 1:
                        ih, j = divmod(jj - 1, CHUNKS)
                        pe.wait_ge(S["sig_ok"], n * 2 * JJ + 2 * jj)
                        if j == 0:
                            pe.wait_ge(S["o_read"], n * IH + ih + 1)
                        for i2 in range(2):
                            for h in range(2):
                                last = nc.tensor.matmul(ps_o[h * D:(h + 1) * D, i2, :], v_st[:, slot, j, h, :],
                                                        sig[:, (jj - 1) % 2, h, i2 * BLK:(i2 + 1) * BLK],
                                                        start=j == 0, stop=j == CHUNKS - 1)
                        last.then_inc(S["pv_mm"], 1)

            for i in range(PB):
                project(i, 0, 0, 0)
            with pe.Fori(0, BATCH) as b:
                with pe.Fori(0, PAIRS // 2) as hh:
                    n = b * PAIRS + hh * 2
                    pair(n, 0, b, hh * 2 + 1)
                    pair(n + 1, 1, (b + hh) % BATCH, 2 - hh * 2)
                pe.wait_ge(S["o_read"], b * (PAIRS * IH) + PAIRS * IH + 1)
                for k in range(2):
                    for hp in range(PAIRS):
                        for a in range(2):
                            last = nc.tensor.matmul(ps_p[k][a * D:(a + 1) * D, :], wo[:, hp, :],
                                                    ctxT[:, hp, (2 * k + a) * BLK:(2 * k + a + 1) * BLK],
                                                    start=hp == 0, stop=hp == PAIRS - 1)
                    last.then_inc(S["wo_mm"], 1)
                for k in range(2):
                    pe.wait_ge(S["wo_sb"], 2 * b + k + 1)
                    for i in range(4):
                        last = nc.tensor.transpose(ps_p[k][:, i * P:(i + 1) * P], outT[:, k, i * P:(i + 1) * P], ident[:, :])
                    last.then_inc(S["wo_turned"], 1)
                pe.wait_ge(S["wo_read"], 2 * b + 2)

        @block.scalar
        def _(act):
            for i in range(KQ):
                act.wait_ge(S["p_mm"], i + 1)
                h, c = divmod(i % (KQ // 2), QB)
                hi = (k_st if i < KQ // 2 else q_hi)[:, 0, h, c * BLK:(c + 1) * BLK]
                nc.scalar.activation(hi, ps_p[i % 2][:, :], ACT.Copy, scale=DOWN).then_inc(S["hi_ok"], 1)
            act.preload_act_table(ACT.Sigmoid)
            with act.Fori(0, BATCH * PAIRS) as n:
                for s in range(2 * JJ):
                    jj, h = divmod(s, 2)
                    act.wait_ge(S["qk_mm"], n * 2 * JJ + s + 1)
                    if jj >= 2:
                        act.wait_ge(S["pv_mm"], n * JJ + jj - 1)
                    nc.scalar.activation(sig[:, jj % 2, h, :], ps_s[h][:, :], ACT.Sigmoid,
                                         scale=SCALE / (Q_UP * Q_UP)).then_inc(S["sig_ok"], 1)

        @block.vector
        def _(dve):
            def split(i, slot, done, first=False):
                dve.wait_ge(S["p_mm"], done + i + 1)
                if i < KQ:
                    h, c = divmod(i % (KQ // 2), QB)
                    cols = slice(c * BLK, (c + 1) * BLK)
                    hi = (k_st if i < KQ // 2 else q_hi)[:, slot, h, cols]
                    if first:
                        dve.wait_ge(S["hi_ok"], i + 1)
                    else:
                        nc.vector.tensor_scalar(hi, ps_p[i % 2][:, :], DOWN, None, ALU.mult)
                        dve.drain()
                    if i < KQ // 2:
                        rows = slice((1 - h) * D, (2 - h) * D)
                        dst = hi = k_st[rows, slot, h, cols]
                    else:
                        rows = slice(h * D, (h + 1) * D)
                        dst, hi = q_lo[rows, slot, cols], hi[rows]
                    src = ps_p[i % 2][rows, :]
                    nc.vector.scalar_tensor_tensor(dst, src, DOWN, hi, ALU.mult, ALU.subtract).then_inc(S["p_read"], 1)
                else:
                    c = (i - KQ) * 4
                    nc.vector.tensor_scalar(v_st[:, slot, c:c + 4, :, :].rearrange("p c h f -> p (c h f)"), ps_p[i % 2][:, :],
                                            1.0 / (X_UP * W_UP), None, ALU.mult).then_inc(S["p_read"], 1)

            def pair(n, hp, slot):
                before = CHUNKS - FIRST_JJ
                for ih in range(IH):
                    for i in range(ih * before, (before, PB)[ih]):
                        split(i, 1 - slot, n * PB + PB)
                    dve.wait_ge(S["pv_mm"], n * JJ + (ih + 1) * CHUNKS)
                    dst = ctxT[:, bass.ds(hp, 1), ih * 2 * BLK:(ih + 1) * 2 * BLK].squeeze(1)
                    nc.vector.tensor_copy(dst, ps_o[:, :, :].rearrange("p a b -> p (a b)")).then_inc(S["o_read"], 1)

            dve.nop().then_inc(S["o_read"], 1)
            for i in range(PB):
                split(i, 0, 0, True)
            with dve.Fori(0, BATCH) as b:
                with dve.Fori(0, PAIRS // 2) as hh:
                    n = b * PAIRS + hh * 2
                    pair(n, hh * 2, 0)
                    pair(n + 1, hh * 2 + 1, 1)
                for k in range(2):
                    dve.wait_ge(S["wo_mm"], 2 * b + k + 1)
                    nc.vector.tensor_scalar(outT[:, k, :], ps_p[k][:, :], 0.0, None, ALU.max).then_inc(S["wo_sb"], 1)
                for k in range(2):
                    dve.wait_ge(S["wo_turned"], 2 * b + k + 1)
                    tiles = resid[:, bass.ds(b * CHUNKS + 8 * k, 8), :].rearrange("p (a i) o -> p i a o", a=2)
                    nc.vector.tensor_tensor(tiles, ps_p[k][:, :].rearrange("p (i a o) -> p i a o", a=2, o=D), tiles,
                                            ALU.add).then_inc(S["wo_read"], 1)


def routed_mlp(nc, m, A, resid, ident, flip):
    HID = A["L1_ffn_w1"].shape[1]
    MT = HID // P
    TAKE = SEQ // 2 - 1
    CUTS = 7
    ROUNDS_PER = 2
    BLK = 4 * P
    HALF = TILES // 2
    NBLK = HALF * P // BLK
    ROUNDS = ROUNDS_PER * NBLK

    x = m.sb("x", [P, HALF, 2, D])
    x_t = x[:, :, :, :].rearrange("p t a d -> p a t d")
    xT = m.sb("xT", [P, HALF * P])
    y = m.sb("y", [P, TILES, D])
    w = m.sb("w", [P, TILES])
    w1 = m.sb("w1", [P, 2, HID])
    w2 = m.sb("w2", [P, MT, D])
    b1 = m.sb("b1", [P, MT])
    b2 = m.sb("b2", [P, D])
    wr = m.sb("wr", [P, D])
    br = m.sb("br", [P, 1])
    ones = m.sb("ones", [P, P])
    after = m.sb("after", [P, P])
    bound = m.sb("bound", [P, BATCH])
    step = m.sb("step", [P, BATCH])
    low = m.sb("low", [P, BATCH])

    with ExitStack() as stack:
        pm = Memory(nc, stack, "route")
        square = pm.sb("square", [P, TILES, D])
        stat = pm.sb("stat", [P, 3, TILES])
        stat4 = stat[:, :, :].rearrange("p s (a t) -> p s a t", a=2)
        top = pm.sb("top", [P, BATCH])
        ps_x = [pm.ps(f"ps_x{i}", [P, BLK]) for i in range(2)]
        loaded, made, root_in, root_out, x_ok, x_tr, xT_ok, top_in, top_out = map(pm.sem, (
            "loaded", "made", "root_in", "root_out", "x_ok", "x_tr", "xT_ok", "top_in", "top_out"))
        with nc.Block() as block:

            @block.sync
            def _(sp):
                loads = [(w2[:, :, :], A["L1_ffn_w2"].rearrange("(m p) d -> p m d", p=P)),
                         (b2[:, :], A["L1_ffn_b2"].partition_broadcast(P)),
                         (wr[:, :], A["L1_ffn_wr"].rearrange("d o -> (d o)").partition_broadcast(P)),
                         (br[:, :], A["L1_ffn_br"].partition_broadcast(P))]
                loads += [(b1[:, k:k + 1], A["L1_ffn_b1"][k * P:(k + 1) * P].unsqueeze(1)) for k in range(MT)]
                for dst, src in loads:
                    sp.dma_start(dst, src).then_inc(loaded, 16)
                sp.wait_ge(made, 1)
                for k in range(2):
                    sp.dma_start(w1[k * D:(k + 1) * D, k, :], A["L1_ffn_w1"]).then_inc(loaded, 16)
                sp.wait_ge(loaded, 16 * (6 + MT))

            @block.gpsimd
            def _(pool):
                nc.gpsimd.memset(w1[:, :, :], 0.0).then_inc(made, 1)
                pool.wait_ge(made, 1)
                nc.gpsimd.memset(ones[:, :], 1.0).then_inc(made, 1)
                pool.wait_ge(made, 2)
                nc.gpsimd.affine_select(out=after[:, :], in_=ones[:, :], compare_op=ALU.is_gt, fill=0.0,
                                        base=0, pattern=[[-1, P]], channel_multiplier=1).then_inc(made, 1)
                pool.wait_ge(made, 3)
                pool.wait_ge(top_in, 1)
                nc.gpsimd.partition_all_reduce(bound[:, :], top[:, :], P, bass.bass_isa.ReduceOp.max).then_inc(top_out, 1)
                pool.wait_ge(top_out, 1)
                nc.gpsimd.tensor_tensor(resid[:, 0:HALF, :], resid[:, 0:HALF, :], x[:, :, 0, :], ALU.add)
                nc.gpsimd.tensor_tensor(resid[:, HALF:TILES, :], resid[:, HALF:TILES, :], x[:, :, 1, :], ALU.add)

            @block.scalar
            def _(act):
                act.wait_ge(root_in, 1)
                nc.scalar.activation(stat[:, 2], stat[:, 1], ACT.Sqrt).then_inc(root_out, 1)
                for k in range(NBLK):
                    act.wait_ge(x_tr, k + 1)
                    nc.scalar.activation(xT[:, k * BLK:(k + 1) * BLK], ps_x[k % 2][:, :], ACT.Copy).then_inc(xT_ok, 1)

            @block.vector
            def _(dve):
                def root():
                    dve.drain()
                    dve.nop().then_inc(root_in, 1)
                    dve.wait_ge(root_out, 1)

                sq_t = square[:, :, :].rearrange("p (a t) d -> p a t d", a=2)
                layer_norm(nc, dve, x_t, resid[:, :, :].rearrange("p (a t) d -> p a t d", a=2), x_t, sq_t, stat4, LN_EPS, root)
                dve.drain()
                dve.nop().then_inc(x_ok, 1)
                dve.wait_ge(loaded, 16 * (6 + MT))
                for a in range(2):
                    nc.vector.tensor_tensor(sq_t[:, a], x_t[:, a], wr[:, :].unsqueeze(1).broadcast_to([P, HALF, D]), ALU.mult)
                dve.drain()
                nc.vector.tensor_reduce(out=w[:, :], in_=square[:, :, :], axis=AX.X, op=ALU.add)
                dve.drain()
                nc.vector.tensor_scalar(w[:, :], w[:, :], br[:, :], None, ALU.add)
                dve.drain()
                nc.vector.tensor_reduce(out=top[:, :], in_=w[:, :].rearrange("p (b c) -> p b c", c=CHUNKS), axis=AX.X,
                                        op=ALU.max, apply_absolute_value=True)
                dve.drain()
                dve.nop().then_inc(top_in, 1)
                dve.wait_ge(top_out, 1)
                nc.vector.tensor_scalar(bound[:, :], bound[:, :], 1.001, 1e-30, ALU.mult, ALU.add)
                dve.drain()
                nc.vector.tensor_scalar(low[:, :], bound[:, :], -1.0, None, ALU.mult)
                nc.vector.tensor_scalar(step[:, :], bound[:, :], 2.0 / (CUTS + 1), None, ALU.mult)

            @block.tensor
            def _(pe):
                pe.wait_ge(x_ok, 1)
                for k in range(NBLK):
                    if k >= 2:
                        pe.wait_ge(xT_ok, k - 1)
                    for j in range(4):
                        last = nc.tensor.transpose(ps_x[k % 2][:, j * P:(j + 1) * P],
                                                   x[:, 4 * k + j, :, :].rearrange("p a d -> p (a d)"), ident[:, :])
                    last.then_inc(x_tr, 1)

    hT = m.sb("hT", [P, 2, MT, BLK])
    mid = m.sb("mid", [P, BATCH])
    least = m.sb("least", [P, TILES])
    over = m.sb("over", [P, TILES])
    n_here = m.sb("n_here", [P, CUTS, BATCH])
    steps = m.sb("steps", [P, CUTS, BATCH])
    offset = m.sb("offset", [P, CUTS, BATCH])
    cut = m.sb("cut", [P, CUTS, BATCH])
    risen = m.sb("risen", [P, CUTS, BATCH])
    marks = m.sb("marks", [P, CUTS, TILES])
    above = m.sb("above", [P, TILES])
    rise = m.sb("rise", [P, BATCH])
    n_over = m.sb("n_over", [P, BATCH])
    tied = m.sb("tied", [P, TILES])
    rank = m.sb("rank", [P, TILES])
    total = m.sb("total", [P, TILES])
    carry = m.sb("carry", [P, TILES])
    in_row = m.sb("in_row", [P, TILES])
    ps_h = [m.ps(f"ps_h{i}", [P, BLK]) for i in range(2)]
    ps_w = m.ps("ps_w", [P, BLK])
    ps_y = m.ps("ps_y", [P, BLK])
    yT = m.sb("yT", [P, BLK])
    ps_n = m.ps("ps_n", [P, CUTS, BATCH])
    ps_r = m.ps("ps_r", [P, 2, TILES])
    names = ("h_mm", "h_ok", "y_mm", "y_sb", "y_tr", "y_ok", "count_in", "count_mm", "rank_in", "rank_mm")
    S = {n: m.sem(n) for n in names}

    with nc.Block() as block:

        @block.tensor
        def _(pe):
            with pe.Fori(0, NBLK) as k:
                rounds = iter(range(ROUNDS_PER))

                def count():
                    i = next(rounds, None)
                    if i is not None:
                        pe.wait_ge(S["count_in"], k * ROUNDS_PER + i + 1)
                        nc.tensor.matmul(ps_n[:, :, :], ones[:, :], n_here[:, :, :], start=True, stop=True).then_inc(S["count_mm"], 1)

                for a in range(2):
                    for j in range(MT):
                        pe.wait_ge(S["h_ok"], k * (2 * MT) + a * MT + j + 1)
                        nc.tensor.matmul(ps_h[j][:, :], w1[:, a, j * P:(j + 1) * P], xT[:, bass.ts(k, BLK)],
                                         start=True, stop=True).then_inc(S["h_mm"], 1)
                    count()
                    pe.wait_ge(S["h_ok"], k * (2 * MT) + (a + 1) * MT + MT)
                    if a == 0:
                        pe.wait_ge(S["y_sb"], k + 1)
                    for j in range(MT):
                        last = nc.tensor.matmul(ps_w[a * D:(a + 1) * D, :], w2[:, j, :], hT[:, a, j, :],
                                                start=j == 0, stop=j == MT - 1)
                last.then_inc(S["y_mm"], 1)
                pe.wait_ge(S["y_sb"], k + 2)
                pe.wait_ge(S["y_ok"], k + 1)
                for i in range(4):
                    last = nc.tensor.transpose(ps_y[:, i * P:(i + 1) * P], yT[:, i * P:(i + 1) * P], ident[:, :])
                last.then_inc(S["y_tr"], 1)
                assert next(rounds, None) is None
            pe.wait_ge(S["count_in"], ROUNDS + 1)
            nc.tensor.matmul(ps_n[:, 0, :], ones[:, :], n_here[:, 0, :], start=True, stop=True).then_inc(S["count_mm"], 1)
            pe.wait_ge(S["rank_in"], 1)
            nc.tensor.matmul(ps_r[:, 0, :], after[:, :], tied[:, :], start=True, stop=True)
            nc.tensor.matmul(ps_r[:, 1, :], ones[:, :], tied[:, :], start=True, stop=True).then_inc(S["rank_mm"], 1)

        @block.scalar
        def _(act):
            act.preload_act_table(ACT.Gelu_apprx_tanh)
            act.nop().then_inc(S["h_ok"], MT)
            act.nop().then_inc(S["y_sb"], 1)
            act.nop().then_inc(S["y_ok"], 1)
            with act.Fori(0, NBLK) as k:
                for a in range(2):
                    for j in range(MT):
                        act.wait_ge(S["h_mm"], k * (2 * MT) + a * MT + j + 1)
                        nc.scalar.activation(hT[:, a, j, :], ps_h[j][:, :], ACT.Gelu_apprx_tanh, bias=b1[:, j:j + 1]).then_inc(S["h_ok"], 1)
                act.wait_ge(S["y_mm"], k + 1)
                nc.scalar.activation(yT[:, :], ps_w[:, :], ACT.Copy).then_inc(S["y_sb"], 1)
                act.wait_ge(S["y_tr"], k + 1)
                for a in range(2):
                    src = ps_y[:, :].rearrange("p (i a d) -> p i a d", a=2, d=D)[:, :, a, :]
                    last = nc.scalar.activation(y[:, bass.ds(k * 4 + a * HALF, 4), :], src, ACT.Copy)
                last.then_inc(S["y_ok"], 1)

        @block.vector
        def _(dve):
            w_b = w[:, :].rearrange("p (b c) -> p b c", c=CHUNKS)
            least_b = least[:, :].rearrange("p (b c) -> p b c", c=CHUNKS)
            over_b = over[:, :].rearrange("p (b c) -> p b c", c=CHUNKS)

            nc.vector.memset(in_row[:, :], 1.0)
            dve.drain()
            nc.vector.memset(in_row[:, :].rearrange("p (b c) -> p b c", c=CHUNKS)[:, :, 0], 0.0)
            for j in range(CUTS):
                nc.vector.memset(steps[:, j, :], float(j + 1))
            dve.drain()
            w_cuts = w_b.unsqueeze(1).broadcast_to([P, CUTS, BATCH, CHUNKS])
            every = [P, CUTS, BATCH]
            with dve.Fori(0, ROUNDS) as r:
                nc.vector.tensor_tensor(offset[:, :, :], steps[:, :, :], step[:, :].unsqueeze(1).broadcast_to(every), ALU.mult)
                dve.drain()
                nc.vector.tensor_tensor(cut[:, :, :], offset[:, :, :], low[:, :].unsqueeze(1).broadcast_to(every), ALU.add)
                dve.drain()
                nc.vector.tensor_tensor(marks[:, :, :].rearrange("p j (b c) -> p j b c", c=CHUNKS), w_cuts, over_last(cut[:, :, :], CHUNKS), ALU.is_ge)
                dve.drain()
                nc.vector.tensor_reduce(out=n_here[:, :, :], in_=marks[:, :, :].rearrange("p j (b c) -> p j b c", c=CHUNKS), axis=AX.X, op=ALU.add)
                nc.vector.tensor_scalar(step[:, :], step[:, :], 1.0 / (CUTS + 1), None, ALU.mult)
                dve.drain()
                dve.nop().then_inc(S["count_in"], 1)
                dve.wait_ge(S["count_mm"], r + 1)
                nc.vector.scalar_tensor_tensor(risen[:, :, :], ps_n[:, :, :], float(TAKE), offset[:, :, :], ALU.is_ge, ALU.mult)
                dve.drain()
                nc.vector.tensor_reduce(out=rise[:, :], in_=risen[:, :, :].rearrange("p j b -> p b j"), axis=AX.X, op=ALU.max)
                dve.drain()
                nc.vector.tensor_tensor(low[:, :], low[:, :], rise[:, :], ALU.add)
                dve.drain()
            nc.vector.scalar_tensor_tensor(mid[:, :], step[:, :], float(CUTS + 1), low[:, :], ALU.mult, ALU.add)
            nc.vector.tensor_tensor(least_b, w_b, over_last(low[:, :], CHUNKS), ALU.is_ge)
            nc.vector.tensor_tensor(above[:, :].rearrange("p (b c) -> p b c", c=CHUNKS), w_b, over_last(low[:, :], CHUNKS), ALU.is_gt)
            dve.drain()
            nc.vector.tensor_tensor(over_b, w_b, over_last(mid[:, :], CHUNKS), ALU.is_ge)
            dve.drain()
            nc.vector.tensor_tensor(over[:, :], over[:, :], above[:, :], ALU.mult)
            dve.drain()
            nc.vector.tensor_reduce(out=n_here[:, 0, :], in_=over_b, axis=AX.X, op=ALU.add)
            dve.drain()
            dve.nop().then_inc(S["count_in"], 1)
            nc.vector.tensor_tensor(tied[:, :], least[:, :], over[:, :], ALU.subtract)
            dve.drain()
            dve.nop().then_inc(S["rank_in"], 1)
            dve.wait_ge(S["count_mm"], ROUNDS + 1)
            nc.vector.tensor_scalar(n_over[:, :], ps_n[:, 0, :], -1.0, float(TAKE), ALU.mult, ALU.add)
            dve.wait_ge(S["rank_mm"], 1)
            nc.vector.tensor_copy(total[:, :], ps_r[:, 1, :])
            dve.drain()
            nc.vector.tensor_tensor_scan(carry[:, :], in_row[:, :], total[:, :], 0.0, ALU.mult, ALU.add)
            dve.drain()
            nc.vector.tensor_tensor(carry[:, :], carry[:, :], total[:, :], ALU.subtract)
            dve.drain()
            nc.vector.tensor_tensor(rank[:, :], ps_r[:, 0, :], carry[:, :], ALU.add)
            dve.drain()
            nc.vector.tensor_tensor(rank[:, :].rearrange("p (b c) -> p b c", c=CHUNKS), rank[:, :].rearrange("p (b c) -> p b c", c=CHUNKS),
                                    over_last(n_over[:, :], CHUNKS), ALU.is_lt)
            dve.drain()
            nc.vector.tensor_tensor(tied[:, :], tied[:, :], rank[:, :], ALU.mult)
            dve.drain()
            nc.vector.tensor_tensor(tied[:, :], tied[:, :], over[:, :], ALU.add)
            dve.drain()
            nc.vector.tensor_tensor(w[:, :], w[:, :], tied[:, :], ALU.mult)
            dve.wait_ge(S["y_ok"], NBLK + 1)
            nc.vector.tensor_tensor(y[:, :, :], y[:, :, :], b2[:, :].unsqueeze(1).broadcast_to([P, TILES, D]), ALU.add)
            dve.drain()
            nc.vector.tensor_tensor(y[:, :, :], y[:, :, :], over_last(w[:, :], D), ALU.mult)
            dve.drain()
            nc.vector.tensor_tensor(resid[:, :, :], resid[:, :, :], y[:, :, :], ALU.add)


def store_result(nc, m, resid, flip, out):
    PER = 512 // D
    N = TILES // PER
    turned = m.sb("turned", [P, TILES, D])
    ps = [m.ps(f"ps{i}", [P, PER, D]) for i in range(4)]
    flipped, copied, stored = m.sem("flipped"), m.sem("copied"), m.sem("stored")
    out_v = out.rearrange("b (c p) d -> p (b c) d", p=P)
    with nc.Block() as block:

        @block.tensor
        def _(pe):
            for k in range(N):
                if k >= 4:
                    pe.wait_ge(copied, k - 3)
                nc.tensor.matmul(ps[k % 4][:, :, :], flip[:, :], resid[:, k * PER:(k + 1) * PER, :],
                                 start=True, stop=True).then_inc(flipped, 1)

        @block.vector
        def _(dve):
            for k in range(N):
                dve.wait_ge(flipped, k + 1)
                nc.vector.tensor_copy(turned[:, k * PER:(k + 1) * PER, :], ps[k % 4][:, :, :]).then_inc(copied, 1)

        @block.sync
        def _(sp):
            for k in range(N):
                sp.wait_ge(copied, k + 1)
                sp.dma_start(out_v[:, k * PER:(k + 1) * PER, :], turned[:, k * PER:(k + 1) * PER, :]).then_inc(stored, 16)
            sp.wait_ge(stored, 16 * N)


def tower(nc, A, out, phases=5):
    with ExitStack() as whole:
        shared = Memory(nc, whole, "all")
        resid = shared.sb("resid", [P, TILES, D])
        ident, flip = constants(nc, shared)
        with ExitStack() as poles_stack:
            pw = PolePowers(nc, Memory(nc, poles_stack, "poles"))
            with ExitStack() as stack:
                dram_k, programs = pole_parameters(nc, Memory(nc, stack, "pole_work"), A, ident, pw)
                embed_tokens(nc, Memory(nc, stack, "embed_tokens"), A, resid, ident, programs, pw)
            with ExitStack() as stack:
                if phases > 1:
                    state_space_layers(nc, Memory(nc, stack, "state_space_layers"), A, resid, ident, dram_k, pw)
        for phase in (expert_mixture, sigmoid_attention, routed_mlp)[:max(0, phases - 2)]:
            with ExitStack() as stack:
                phase(nc, Memory(nc, stack, phase.__name__), A, resid, ident, flip)
        with ExitStack() as stack:
            store_result(nc, Memory(nc, stack, "end"), resid, flip, out)


def kernel(**inputs):
    import concourse.bacc as bacc
    import numpy as np
    from concourse.bass_utils import run_bass_kernel_spmd

    nc = bacc.Bacc("TRN2", target_bir_lowering=False, num_devices=1)
    arrays, args = {}, {}
    given = {k: np.ascontiguousarray(v) for k, v in inputs.items()}
    tables = ["L0_tok_emb_table", "L0_tok_geo_table", "L0_tok_visit_table"]
    given["rows"] = np.concatenate([given.pop(t) for t in tables], axis=1)
    for name, a in given.items():
        arrays[f"in_{name}"] = a
        args[name] = nc.dram_tensor(f"in_{name}", a.shape, mybir.dt.from_np(a.dtype), kind="ExternalInput").ap()
    out = nc.dram_tensor("out_h", (BATCH, SEQ, D), F32, kind="ExternalOutput").ap()
    tower(nc, args, out)
    r = run_bass_kernel_spmd(nc, [arrays], core_ids=[0])
    return r.results[0]["out_h"]
```
